# Optimizing a Trainium2 kernel written in Bass

```python
import numpy as np
import jax
import jax.numpy as jnp

def _softmax(x, axis=-1):
    return jax.nn.softmax(x, axis=axis)

def _gelu(x):
    return jax.nn.gelu(x, approximate=True)

def _silu(x):
    return jax.nn.silu(x)

def _sigmoid(x):
    return jax.nn.sigmoid(x)

def _layernorm(x, axis=-1, eps=1e-05):
    m = jnp.mean(x, axis=axis, keepdims=True)
    v = jnp.var(x, axis=axis, keepdims=True)
    return (x - m) / jnp.sqrt(v + eps)

def _scatter_add(tgt, idx, src, axis=0):
    return tgt.at[idx].add(src)

def _segment_sum(src, seg, n):
    return jax.ops.segment_sum(src, seg, n)
kernel_name = 'mk_prb_d2_jaxref_r4_764199'

def setup_inputs(seed: int=0):
    np.random.seed(seed)
    _w = jnp.asarray

    def _L0_attn_setup():
        import jax, jax.numpy as jnp
        import numpy as np
        H, P, HID, N, G, K, CS = (32, 64, 256, 128, 1, 4, 64)
        INTER = H * P
        CONV_DIM = INTER + 2 * G * N
        PROJ = INTER + CONV_DIM + H
        EPS = 1e-05

        def segsum(x):
            T = x.shape[-1]
            xx = jnp.broadcast_to(x[..., None], x.shape + (T,))
            xx = jnp.where(jnp.tril(jnp.ones((T, T), bool), -1), xx, 0.0)
            s = jnp.cumsum(xx, axis=-2)
            return jnp.where(jnp.tril(jnp.ones((T, T), bool)), s, -jnp.inf)
        key = jax.random.key(seed)
        ks = jax.random.split(key, 8)
        B_, S = (2, 512)
        x = jax.random.normal(ks[0], (B_, S, HID), jnp.float32)
        W_in = jax.random.normal(ks[1], (PROJ, HID), jnp.float32) / np.sqrt(HID)
        b_in = jnp.zeros((PROJ,), jnp.float32)
        conv_w = jax.random.normal(ks[2], (CONV_DIM, K), jnp.float32) / np.sqrt(K)
        dt = jnp.exp(jax.random.uniform(ks[3], (H,)) * (np.log(0.1) - np.log(0.001)) + np.log(0.001))
        dt = jnp.clip(dt, 0.0001)
        dt_bias = dt + jnp.log(-jnp.expm1(-dt))
        A_log = jnp.log(jax.random.uniform(ks[4], (H,), minval=1.0, maxval=16.0))
        D = jnp.ones((H,), jnp.float32)
        norm_w = jnp.ones((INTER,), jnp.float32)
        W_out = jax.random.normal(ks[5], (HID, INTER), jnp.float32) / np.sqrt(INTER)
        b_out = jnp.zeros((HID,), jnp.float32)
        return {'x': x, 'W_in': W_in, 'b_in': b_in, 'conv_w': conv_w, 'dt_bias': dt_bias, 'A_log': A_log, 'D': D, 'norm_w': norm_w, 'W_out': W_out, 'b_out': b_out}
    _L0_attn_in = _L0_attn_setup()

    def _L0_ffn_setup():
        import jax, jax.numpy as jnp
        import numpy as np
        B, S, H = (2, 256, 256)
        E, F = (16, 128)
        G, TOPK_G, TOPK = (4, 2, 4)
        N_SHARED = 2
        ROUTE_SCALE = 1.0
        FS = N_SHARED * F

        def _gate(x, w_gate):
            T = x.shape[0]
            scores = jax.nn.sigmoid(x @ w_gate.T)
            sv = scores.reshape(T, G, E // G)
            group_scores = jax.lax.top_k(sv, 2)[0].sum(-1)
            top_groups = jax.lax.top_k(group_scores, TOPK_G)[1]
            allowed = jnp.zeros((T, G), dtype=bool).at[jnp.arange(T)[:, None], top_groups].set(True)
            masked = jnp.where(allowed[:, :, None], sv, -jnp.inf).reshape(T, E)
            _, idx = jax.lax.top_k(masked, TOPK)
            w = jnp.take_along_axis(scores, idx, axis=1)
            w = w / (w.sum(-1, keepdims=True) + 1e-06) * ROUTE_SCALE
            return (w, idx)

        def _swiglu(x, w1, w3, w2):
            return jax.nn.silu(x @ w1.T) * (x @ w3.T) @ w2.T
        key = jax.random.key(seed)
        ks = jax.random.split(key, 8)
        scale = 0.02
        return {'hidden_states': jax.random.normal(ks[0], (B, S, H), dtype=jnp.float32), 'w_gate': jax.random.normal(ks[1], (E, H), dtype=jnp.float32) * scale, 'w1_e': jax.random.normal(ks[2], (E, F, H), dtype=jnp.float32) * scale, 'w3_e': jax.random.normal(ks[3], (E, F, H), dtype=jnp.float32) * scale, 'w2_e': jax.random.normal(ks[4], (E, H, F), dtype=jnp.float32) * scale, 'w1_s': jax.random.normal(ks[5], (FS, H), dtype=jnp.float32) * scale, 'w3_s': jax.random.normal(ks[6], (FS, H), dtype=jnp.float32) * scale, 'w2_s': jax.random.normal(ks[7], (H, FS), dtype=jnp.float32) * scale}
    _L0_ffn_in = _L0_ffn_setup()

    def _L1_attn_setup():
        import jax, jax.numpy as jnp
        import numpy as np
        DIM = 256
        NUM_HEADS = 16
        HEAD_DIM = DIM // NUM_HEADS
        TAU = 2.0
        V_TH = 1.0
        BN_EPS = 1e-05

        def _branch(x, W, gamma, beta):
            B, N, D = x.shape
            h = jnp.einsum('bnd,ed->bne', x, W)
            hf = h.reshape(B * N, D)
            mean = jnp.mean(hf, axis=0)
            var = jnp.var(hf, axis=0)
            hn = (hf - mean) * jax.lax.rsqrt(var + BN_EPS) * gamma + beta
            hn = hn.reshape(B, N, D)
            return jax.nn.sigmoid(4.0 * (hn - V_TH))

        def _heads(x):
            B, N, D = x.shape
            return x.reshape(B, N, NUM_HEADS, HEAD_DIM).transpose(0, 2, 1, 3)
        key = jax.random.key(seed)
        ks = jax.random.split(key, 12)
        B, N, D = (8, 1024, DIM)
        s = 0.02
        return {'x': jax.random.normal(ks[0], (B, N, D), dtype=jnp.float32), 'Wq': jax.random.normal(ks[1], (D, D), dtype=jnp.float32) * s, 'gq': jnp.ones((D,), jnp.float32), 'bq': jnp.zeros((D,), jnp.float32), 'Wk': jax.random.normal(ks[2], (D, D), dtype=jnp.float32) * s, 'gk': jnp.ones((D,), jnp.float32), 'bk': jnp.zeros((D,), jnp.float32), 'Wv': jax.random.normal(ks[3], (D, D), dtype=jnp.float32) * s, 'gv': jnp.ones((D,), jnp.float32), 'bv': jnp.zeros((D,), jnp.float32), 'Wp': jax.random.normal(ks[4], (D, D), dtype=jnp.float32) * s, 'bp': jnp.zeros((D,), jnp.float32)}
    _L1_attn_in = _L1_attn_setup()

    def _L1_ffn_setup():
        import jax, jax.numpy as jnp
        import numpy as np
        B, S, D, F, E, K = (2, 512, 256, 512, 8, 2)
        key = jax.random.key(seed)
        ks = jax.random.split(key, 5)
        scale = 0.02
        return {'x': jax.random.normal(ks[0], (B, S, D), dtype=jnp.float32), 'Wg': jax.random.normal(ks[1], (E, D), dtype=jnp.float32) * scale, 'W1': jax.random.normal(ks[2], (E, F, D), dtype=jnp.float32) * scale, 'W2': jax.random.normal(ks[3], (E, F, D), dtype=jnp.float32) * scale, 'W3': jax.random.normal(ks[4], (E, D, F), dtype=jnp.float32) * scale}
    _L1_ffn_in = _L1_ffn_setup()
    _d = {'L0_attn_x': _L0_attn_in['x'], 'L0_attn_W_in': _L0_attn_in['W_in'], 'L0_attn_b_in': _L0_attn_in['b_in'], 'L0_attn_conv_w': _L0_attn_in['conv_w'], 'L0_attn_dt_bias': _L0_attn_in['dt_bias'], 'L0_attn_A_log': _L0_attn_in['A_log'], 'L0_attn_D': _L0_attn_in['D'], 'L0_attn_norm_w': _L0_attn_in['norm_w'], 'L0_attn_W_out': _L0_attn_in['W_out'], 'L0_attn_b_out': _L0_attn_in['b_out'], 'L0_ffn_w_gate': _L0_ffn_in['w_gate'], 'L0_ffn_w1_e': _L0_ffn_in['w1_e'], 'L0_ffn_w3_e': _L0_ffn_in['w3_e'], 'L0_ffn_w2_e': _L0_ffn_in['w2_e'], 'L0_ffn_w1_s': _L0_ffn_in['w1_s'], 'L0_ffn_w3_s': _L0_ffn_in['w3_s'], 'L0_ffn_w2_s': _L0_ffn_in['w2_s'], 'L1_attn_Wq': _L1_attn_in['Wq'], 'L1_attn_gq': _L1_attn_in['gq'], 'L1_attn_bq': _L1_attn_in['bq'], 'L1_attn_Wk': _L1_attn_in['Wk'], 'L1_attn_gk': _L1_attn_in['gk'], 'L1_attn_bk': _L1_attn_in['bk'], 'L1_attn_Wv': _L1_attn_in['Wv'], 'L1_attn_gv': _L1_attn_in['gv'], 'L1_attn_bv': _L1_attn_in['bv'], 'L1_attn_Wp': _L1_attn_in['Wp'], 'L1_attn_bp': _L1_attn_in['bp'], 'L1_ffn_Wg': _L1_ffn_in['Wg'], 'L1_ffn_W1': _L1_ffn_in['W1'], 'L1_ffn_W2': _L1_ffn_in['W2'], 'L1_ffn_W3': _L1_ffn_in['W3']}
    _x0 = _d['L0_attn_x']
    _d['L0_attn_x'] = jax.random.normal(jax.random.fold_in(jax.random.key(seed), 1), (1, 4096, 256), dtype=_x0.dtype)
    del _x0
    return _d

def reference(L0_attn_x, L0_attn_W_in, L0_attn_b_in, L0_attn_conv_w, L0_attn_dt_bias, L0_attn_A_log, L0_attn_D, L0_attn_norm_w, L0_attn_W_out, L0_attn_b_out, L0_ffn_w_gate, L0_ffn_w1_e, L0_ffn_w3_e, L0_ffn_w2_e, L0_ffn_w1_s, L0_ffn_w3_s, L0_ffn_w2_s, L1_attn_Wq, L1_attn_gq, L1_attn_bq, L1_attn_Wk, L1_attn_gk, L1_attn_bk, L1_attn_Wv, L1_attn_gv, L1_attn_bv, L1_attn_Wp, L1_attn_bp, L1_ffn_Wg, L1_ffn_W1, L1_ffn_W2, L1_ffn_W3):

    def _L0_attn_ref(x, W_in, b_in, conv_w, dt_bias, A_log, D, norm_w, W_out, b_out):
        import jax, jax.numpy as jnp
        import numpy as np
        H, P, HID, N, G, K, CS = (32, 64, 256, 128, 1, 4, 64)
        INTER = H * P
        CONV_DIM = INTER + 2 * G * N
        PROJ = INTER + CONV_DIM + H
        EPS = 1e-05

        def segsum(x):
            T = x.shape[-1]
            xx = jnp.broadcast_to(x[..., None], x.shape + (T,))
            xx = jnp.where(jnp.tril(jnp.ones((T, T), bool), -1), xx, 0.0)
            s = jnp.cumsum(xx, axis=-2)
            return jnp.where(jnp.tril(jnp.ones((T, T), bool)), s, -jnp.inf)
        B_, S, _ = x.shape
        proj = x @ W_in.T + b_in
        gate = proj[..., :INTER]
        hBC = proj[..., INTER:INTER + CONV_DIM]
        dt = proj[..., INTER + CONV_DIM:]
        xp = jnp.pad(hBC, ((0, 0), (K - 1, 0), (0, 0)))
        conv = sum((xp[:, i:i + S, :] * conv_w[:, i] for i in range(K)))
        hBC = jax.nn.silu(conv)
        h = hBC[..., :INTER]
        Bm = hBC[..., INTER:INTER + G * N]
        Cm = hBC[..., INTER + G * N:]
        A = -jnp.exp(A_log.astype(jnp.float32))
        dt = jax.nn.softplus(dt + dt_bias)
        h = h.reshape(B_, S, H, P).astype(jnp.float32)
        Bm = jnp.tile(Bm.reshape(B_, S, G, N).astype(jnp.float32), (1, 1, H // G, 1))
        Cm = jnp.tile(Cm.reshape(B_, S, G, N).astype(jnp.float32), (1, 1, H // G, 1))
        pad = -S % CS
        D_res = D[..., None] * jnp.pad(h, ((0, 0), (0, pad), (0, 0), (0, 0)))
        h = h * dt[..., None]
        Adt = A * dt

        def chunk(t):
            t = jnp.pad(t, [(0, 0), (0, pad)] + [(0, 0)] * (t.ndim - 2))
            return t.reshape(B_, -1, CS, *t.shape[2:])
        h_c, B_c, C_c = (chunk(h), chunk(Bm), chunk(Cm))
        A_c = chunk(Adt).transpose(0, 3, 1, 2)
        A_cum = jnp.cumsum(A_c, axis=-1)
        Lmat = jnp.exp(segsum(A_c))
        Gm = jnp.einsum('bclhn,bcshn->bclsh', C_c, B_c)
        M = Gm * Lmat.transpose(0, 2, 3, 4, 1)
        Y_diag = jnp.einsum('bclsh,bcshp->bclhp', M, h_c)
        decay = jnp.exp(A_cum[..., -1:] - A_cum)
        B_decay = B_c * decay.transpose(0, 2, 3, 1)[..., None]
        states = jnp.einsum('bclhn,bclhp->bchpn', B_decay, h_c)
        states = jnp.concatenate([jnp.zeros_like(states[:, :1]), states], axis=1)
        dc = jnp.exp(segsum(jnp.pad(A_cum[..., -1], ((0, 0), (0, 0), (1, 0)))))
        states = jnp.einsum('bhij,bjhpn->bihpn', dc, states)[:, :-1]
        sdo = jnp.exp(A_cum).transpose(0, 2, 3, 1)
        Y_off = jnp.einsum('bclhn,bchpn->bclhp', C_c, states) * sdo[..., None]
        y = (Y_diag + Y_off).reshape(B_, -1, H, P) + D_res
        y = y[:, :S].reshape(B_, S, INTER)
        g = y * jax.nn.silu(gate.astype(jnp.float32))
        g = g * jax.lax.rsqrt(jnp.mean(g * g, axis=-1, keepdims=True) + EPS) * norm_w
        return g.astype(x.dtype) @ W_out.T + b_out

    def _L0_ffn_ref(hidden_states, w_gate, w1_e, w3_e, w2_e, w1_s, w3_s, w2_s):
        import jax, jax.numpy as jnp
        import numpy as np
        B, S, H = (2, 256, 256)
        E, F = (16, 128)
        G, TOPK_G, TOPK = (4, 2, 4)
        N_SHARED = 2
        ROUTE_SCALE = 1.0
        FS = N_SHARED * F

        def _gate(x, w_gate):
            T = x.shape[0]
            scores = jax.nn.sigmoid(x @ w_gate.T)
            sv = scores.reshape(T, G, E // G)
            group_scores = jax.lax.top_k(sv, 2)[0].sum(-1)
            top_groups = jax.lax.top_k(group_scores, TOPK_G)[1]
            allowed = jnp.zeros((T, G), dtype=bool).at[jnp.arange(T)[:, None], top_groups].set(True)
            masked = jnp.where(allowed[:, :, None], sv, -jnp.inf).reshape(T, E)
            _, idx = jax.lax.top_k(masked, TOPK)
            w = jnp.take_along_axis(scores, idx, axis=1)
            w = w / (w.sum(-1, keepdims=True) + 1e-06) * ROUTE_SCALE
            return (w, idx)

        def _swiglu(x, w1, w3, w2):
            return jax.nn.silu(x @ w1.T) * (x @ w3.T) @ w2.T
        shape = hidden_states.shape
        x = hidden_states.reshape(-1, H)
        weights, idx = _gate(x, w_gate)
        combine = (jax.nn.one_hot(idx, E, dtype=x.dtype) * weights[..., None]).sum(1)
        g = jax.nn.silu(jnp.einsum('th,efh->tef', x, w1_e))
        u = jnp.einsum('th,efh->tef', x, w3_e)
        routed = jnp.einsum('tef,ehf,te->th', g * u, w2_e, combine)
        shared = _swiglu(x, w1_s, w3_s, w2_s)
        return (routed + shared).reshape(shape)

    def _L1_attn_ref(x, Wq, gq, bq, Wk, gk, bk, Wv, gv, bv, Wp, bp):
        import jax, jax.numpy as jnp
        import numpy as np
        DIM = 256
        NUM_HEADS = 16
        HEAD_DIM = DIM // NUM_HEADS
        TAU = 2.0
        V_TH = 1.0
        BN_EPS = 1e-05

        def _branch(x, W, gamma, beta):
            B, N, D = x.shape
            h = jnp.einsum('bnd,ed->bne', x, W)
            hf = h.reshape(B * N, D)
            mean = jnp.mean(hf, axis=0)
            var = jnp.var(hf, axis=0)
            hn = (hf - mean) * jax.lax.rsqrt(var + BN_EPS) * gamma + beta
            hn = hn.reshape(B, N, D)
            return jax.nn.sigmoid(4.0 * (hn - V_TH))

        def _heads(x):
            B, N, D = x.shape
            return x.reshape(B, N, NUM_HEADS, HEAD_DIM).transpose(0, 2, 1, 3)
        B, N, D = x.shape
        scale = HEAD_DIM ** (-0.5)
        q = _branch(x, Wq, gq, bq)
        k = _branch(x, Wk, gk, bk)
        v = _branch(x, Wv, gv, bv)
        qk = _heads(q * k) * scale
        v_h = _heads(v)
        vv = jnp.einsum('bhnd,bhne->bhde', v_h, v_h)
        out = jnp.einsum('bhnd,bhde->bhne', qk, vv)
        out = out.transpose(0, 2, 1, 3).reshape(B, N, D)
        return jnp.einsum('bnd,ed->bne', out, Wp) + bp

    def _L1_ffn_ref(x, Wg, W1, W2, W3):
        import jax, jax.numpy as jnp
        import numpy as np
        B, S, D, F, E, K = (2, 512, 256, 512, 8, 2)
        k = K
        scores = jnp.einsum('bsd,ed->bse', x, Wg)
        topk_scores, topk_idx = jax.lax.top_k(scores, k)
        topk_probs = jax.nn.softmax(topk_scores, axis=-1)
        h1 = jnp.einsum('bsd,efd->bsef', x, W1)
        h2 = jnp.einsum('bsd,efd->bsef', x, W2)
        hidden = jax.nn.silu(h1) * h2
        expert_out = jnp.einsum('bsef,edf->bsed', hidden, W3)
        onehot = jax.nn.one_hot(topk_idx, scores.shape[-1], dtype=x.dtype)
        gating = jnp.einsum('bsk,bske->bse', topk_probs, onehot)
        return jnp.einsum('bse,bsed->bsd', gating, expert_out)
    x = L0_attn_x
    xn = _layernorm(x, axis=-1)
    x = x + _L0_attn_ref(xn, L0_attn_W_in, L0_attn_b_in, L0_attn_conv_w, L0_attn_dt_bias, L0_attn_A_log, L0_attn_D, L0_attn_norm_w, L0_attn_W_out, L0_attn_b_out) + _L0_ffn_ref(xn, L0_ffn_w_gate, L0_ffn_w1_e, L0_ffn_w3_e, L0_ffn_w2_e, L0_ffn_w1_s, L0_ffn_w3_s, L0_ffn_w2_s)
    xn = _layernorm(x, axis=-1)
    x = x + _L1_attn_ref(xn, L1_attn_Wq, L1_attn_gq, L1_attn_bq, L1_attn_Wk, L1_attn_gk, L1_attn_bk, L1_attn_Wv, L1_attn_gv, L1_attn_bv, L1_attn_Wp, L1_attn_bp) + _L1_ffn_ref(xn, L1_ffn_Wg, L1_ffn_W1, L1_ffn_W2, L1_ffn_W3)
    return x

_drawn_inputs = setup_inputs


def setup_inputs(seed=0):
    import zlib

    import numpy as np

    out = dict(_drawn_inputs(seed))
    spreads = {'L0_attn_b_in': (0.0, 0.1),
     'L0_attn_D': (1.0, 0.2),
     'L0_attn_norm_w': (1.0, 0.2),
     'L0_attn_b_out': (0.0, 0.629),
     'L1_attn_gq': (1.0, 0.2),
     'L1_attn_bq': (0.0, 0.1),
     'L1_attn_gk': (1.0, 0.2),
     'L1_attn_bk': (0.0, 0.1),
     'L1_attn_gv': (1.0, 0.2),
     'L1_attn_bv': (0.0, 0.1),
     'L1_attn_bp': (0.0, 0.8)}
    factors = {'L0_ffn_w_gate': 8.0,
     'L0_ffn_w1_e': 8.0,
     'L0_ffn_w3_e': 8.0,
     'L0_ffn_w2_e': 8.0,
     'L0_ffn_w1_s': 3.948,
     'L0_ffn_w3_s': 3.939,
     'L0_ffn_w2_s': 3.958,
     'L1_ffn_Wg': 8.0,
     'L1_ffn_W1': 8.0,
     'L1_ffn_W2': 8.0,
     'L1_ffn_W3': 8.0}
    for name, (base, spread) in spreads.items():
        noise = np.random.default_rng([zlib.crc32(name.encode()), seed]).standard_normal(out[name].shape)
        drawn = base * np.exp(spread * noise) if base else spread * noise
        out[name] = jnp.asarray(drawn.astype(out[name].dtype))
    for name, factor in factors.items():
        out[name] = (out[name] * factor).astype(out[name].dtype)
    return out
```

```python
import numpy as np
import concourse.bass as bass
from concourse import mybir
from contextlib import ExitStack

F32 = mybir.dt.float32
I32 = mybir.dt.int32
ALU = mybir.AluOpType
ACT = mybir.ActivationFunctionType
AX = mybir.AxisListType
ds = bass.ds

P = 128
S, D = 4096, 256
T = S // P
KD = D // P
LN_EPS = 1e-5
BIG = 4
GT = BIG * P
NG = T // BIG

H, HP, N = 32, 64, 128
INTER = H * HP
CH = INTER // P
CC = CH + 2
TAPS = 4
TB = 2
BLK = TB * P
NB = S // BLK
NQ = 4
HQ = H // NQ
CQ = CH // NQ
GW = HQ * HP
STEPS = TB * NQ
SSD_EPS = 1e-5

E0, K0, F0, GR0, TG0 = 16, 4, 128, 4, 2
E1, K1, F1 = 8, 2, 512
NT0 = S * K0 // P + E0
NT1 = S * K1 // P + E1
FS = 256
SM0 = E0 + H

HD = 16
BN_EPS = 1e-5
V_TH, SHARP = 1.0, 4.0


class Step:

    def __init__(self, i, k, unroll):
        self.i, self.k, self.unroll = i, k, unroll
        self.n = i * unroll + k

    def back(self, lag):
        return Step(self.i, self.k - lag, self.unroll)

    def inside(self, total):
        return not isinstance(self.n, int) or 0 <= self.n < total

    def slot(self, ring):
        return self.k % ring

    def rounds(self, ring):
        return self.i * (self.unroll // ring) + self.k // ring


def pipeline(eng, total, unroll, warm, drain, body):
    for s in range(warm):
        body(Step(s // unroll, s % unroll, unroll))
    with eng.Fori(warm // unroll, total // unroll) as i:
        for k in range(unroll):
            body(Step(i, k, unroll))
    for s in range(total, total + drain):
        body(Step(s // unroll, s % unroll, unroll))


def reached(eng, sem, step, ring=0, per=1):
    at = step.back(ring)
    if not isinstance(at.n, int) or at.n >= 0:
        eng.wait_ge(sem, at.n * per + per)


def landed(eng, sems, step, ring=0):
    at = step.back(ring)
    if not isinstance(at.n, int) or at.n >= 0:
        eng.wait_ge(sems[at.slot(len(sems))], at.rounds(len(sems)) * 16 + 16)


class Chain:

    def __init__(self, eng, sem):
        self.eng, self.sem, self.count = eng, sem, 0

    def __call__(self, ins):
        self.count += 1
        ins.then_inc(self.sem, 1)
        self.eng.wait_ge(self.sem, self.count)


def bcast(ap, n):
    return ap.unsqueeze(2).to_broadcast([ap.shape[0], ap.shape[1], n])


def middle(ap, n):
    return ap.unsqueeze(1).to_broadcast([ap.shape[0], n, ap.shape[1]])


def tokens(dram, t, n=1):
    return dram.rearrange("(t p) d -> p t d", p=P)[:, ds(t, n), :]


class Semaphores:

    def __init__(self, nc, lasting):
        self.nc, self.lasting, self.ctx, self.numbers = nc, lasting, ExitStack(), []

    def __call__(self, name):
        handle = self.ctx.enter_context(self.nc.semaphore(name))
        self.numbers.append(handle.num)
        return handle

    def __enter__(self):
        return self

    def __exit__(self, *_):
        with self.nc.Block() as block:
            @block.sync
            def _(sp):
                at = sorted(self.numbers)
                while at:
                    n = 1
                    while n < len(at) and at[n] == at[0] + n:
                        n += 1
                    sp.sem_clear(range(at[0], at[0] + n))
                    at = at[n:]
        self.ctx.close()


def constants(nc, top, sem):
    sb = lambda n, s, d=F32: top.enter_context(nc.sbuf_tensor(n, s, d))
    k = {
        "ident": sb("ident", [P, P]),
        "upto": sb("upto", [P, P]),
        "before": sb("before", [P, P]),
        "ones": sb("ones", [P, P]),
    }
    zeroed, built = sem("const_zeroed"), sem("const_built")
    with nc.Block() as block:
        @block.gpsimd
        def _(pool):
            nc.gpsimd.memset(k["ident"][:], 0.0).then_inc(zeroed, 1)
            nc.gpsimd.memset(k["upto"][:], 1.0).then_inc(zeroed, 1)
            nc.gpsimd.memset(k["before"][:], 1.0).then_inc(zeroed, 1)
            nc.gpsimd.memset(k["ones"][:], 1.0).then_inc(zeroed, 1)
            pool.wait_ge(zeroed, 4)
            for name, op, fill in (("ident", ALU.not_equal, 1.0), ("upto", ALU.is_ge, 0.0),
                                   ("before", ALU.is_gt, 0.0)):
                nc.gpsimd.affine_select(out=k[name][:], in_=k[name][:], compare_op=op, fill=fill, base=0,
                                        pattern=[[1, P]], channel_multiplier=-1).then_inc(built, 1)
            pool.wait_ge(built, 3)
    return k


def norm_phase(nc, sem, tag, k, xs, x_dram, xnT, rows, w_small, small, ns, loads):
    ctx = ExitStack()
    sb = lambda n, s, d=F32: ctx.enter_context(nc.sbuf_tensor(tag + n, s, d))
    ps = lambda n: ctx.enter_context(nc.psum_tensor(tag + n, [P, GT], F32))
    with ctx:
        stats = sb("stats", [P, T, 6])
        mean, var, rstd, tmp = (sb(n, [P, T]) for n in ("mean", "var", "rstd", "tmp"))
        xn = sb("xn", [P, 2, BIG, D])
        proj = sb("proj", [P, 2, GT])
        t_ps = [[ps(f"t{r}{c}") for c in range(KD)] for r in range(2)]
        p_ps, q_ps = ps("p"), ps("q")
        s_x = [sem(f"{tag}x_loaded{n}") for n in range(4)]
        s_stats, s_small, s_std, s_rstd = (sem(tag + n) for n in ("stats_done", "moments_done", "std_done", "rstd_done"))
        s_xn, s_row = sem(tag + "xn_done"), [sem(f"{tag}rows_stored{n}") for n in range(2)]
        s_t, s_tc, s_p, s_pc, s_q, s_qc = (sem(tag + n) for n in (
            "transposed", "xnT_kept", "projected", "proj_kept", "proj_turned", "small_kept"))
        with nc.Block() as block:
            @block.sync
            def _(sp):
                if x_dram is not None:
                    for n in range(4):
                        sp.dma_start(xs[:, n * 8:n * 8 + 8, :], tokens(x_dram, n * 8, 8)).then_inc(s_x[n], 16)
                for load in loads:
                    load(sp)

                def step(s):
                    g = s.back(1)
                    if g.inside(NG):
                        reached(sp, s_xn, g)
                        sp.sem_inc(s_settled, 1)
                        sp.dma_start(tokens(rows, g.n * BIG, BIG), xn[:, g.slot(2)]).then_inc(s_row[g.slot(2)], 16)
                s_settled = sem(tag + "sp_settled")
                pipeline(sp, NG, 2, 4, 1, step)
                for r in range(2):
                    sp.wait_ge(s_row[r], NG // 2 * 16)

            @block.vector
            def _(dve):
                if x_dram is not None:
                    for n in range(4):
                        dve.wait_ge(s_x[n], 16)
                with dve.Fori(0, T // 4) as i:
                    for u in range(4):
                        nc.vector.bn_stats(stats[:, ds(i * 4 + u, 1), :].rearrange("p a s -> p (a s)"),
                                           xs[:, ds(i * 4 + u, 1), :].rearrange("p a d -> p (a d)")).then_inc(s_stats, 1)
                dve.wait_ge(s_stats, T)
                link = Chain(dve, s_small)
                link(nc.vector.tensor_tensor(mean[:], stats[:, :, 1], stats[:, :, 4], ALU.add))
                link(nc.vector.tensor_scalar(mean[:], mean[:], 0.5, None, ALU.mult))
                link(nc.vector.tensor_tensor(tmp[:], stats[:, :, 1], stats[:, :, 4], ALU.subtract))
                link(nc.vector.scalar_tensor_tensor(tmp[:], tmp[:], 0.25, tmp[:], ALU.mult, ALU.mult))
                link(nc.vector.tensor_tensor(var[:], stats[:, :, 2], stats[:, :, 5], ALU.add))
                link(nc.vector.scalar_tensor_tensor(var[:], var[:], 1.0 / D, tmp[:], ALU.mult, ALU.add))
                link(nc.vector.tensor_scalar(var[:], var[:], LN_EPS, None, ALU.add))
                dve.wait_ge(s_std, 1)
                nc.vector.reciprocal(rstd[:], tmp[:]).then_inc(s_rstd, 1)
                dve.wait_ge(s_rstd, 1)

                def step(s):
                    if s.inside(NG):
                        reached(dve, s_t, s, 2)
                        landed(dve, s_row, s, 2)
                        for u in range(BIG):
                            t = s.n * BIG + u
                            one = lambda a: a[:, ds(t, 1)]
                            ins = nc.vector.tensor_scalar(xn[:, s.slot(2), u, :],
                                                          xs[:, ds(t, 1), :].rearrange("p a d -> p (a d)"),
                                                          one(mean), one(rstd), ALU.subtract, ALU.mult)
                        ins.then_inc(s_xn, 1)
                    q = s.back(3)
                    if q.inside(NG):
                        reached(dve, s_q, q)
                        dve.sem_inc(s_settled, 1)
                        nc.vector.tensor_copy(small[:, ds(q.n * BIG, BIG), :],
                                              q_ps[:].rearrange("p (t c) -> p t c", t=BIG)[:, :, 0:ns]).then_inc(s_qc, 1)
                s_settled = sem(tag + "dve_settled")
                pipeline(dve, NG, 2, 4, 3, step)

            @block.scalar
            def _(act):
                act.wait_ge(s_small, 7)
                nc.scalar.activation(tmp[:], var[:], ACT.Sqrt).then_inc(s_std, 1)

                def step(s):
                    g = s.back(1)
                    if g.inside(NG):
                        reached(act, s_t, g)
                        act.sem_inc(s_settled, 1)
                        for c in range(KD):
                            ins = nc.scalar.activation(xnT[:, c, ds(g.n * GT, GT)], t_ps[g.slot(2)][c][:], ACT.Copy)
                        ins.then_inc(s_tc, 1)
                    p = s.back(2)
                    if p.inside(NG):
                        reached(act, s_q, p, 2)
                        reached(act, s_p, p)
                        nc.scalar.activation(proj[:, p.slot(2), :], p_ps[:], ACT.Copy).then_inc(s_pc, 1)
                s_settled = sem(tag + "act_settled")
                pipeline(act, NG, 2, 4, 3, step)

            @block.tensor
            def _(pe):
                def step(s):
                    if s.inside(NG):
                        reached(pe, s_tc, s, 2)
                        reached(pe, s_xn, s)
                        for u in range(BIG):
                            for c in range(KD):
                                ins = nc.tensor.transpose(t_ps[s.slot(2)][c][:, u * P:(u + 1) * P],
                                                          xn[:, s.slot(2), u, c * P:(c + 1) * P], k["ident"][:])
                        ins.then_inc(s_t, 1)
                    p = s.back(2)
                    if p.inside(NG):
                        reached(pe, s_pc, p, 1)
                        reached(pe, s_tc, p)
                        for c in range(KD):
                            ins = nc.tensor.matmul(p_ps[:], w_small[:, c, :], xnT[:, c, ds(p.n * GT, GT)],
                                                   start=c == 0, stop=c == KD - 1)
                        ins.then_inc(s_p, 1)
                    q = s.back(3)
                    if q.inside(NG):
                        reached(pe, s_qc, q, 1)
                        reached(pe, s_pc, q)
                        for u in range(BIG):
                            ins = nc.tensor.transpose(q_ps[:, u * P:(u + 1) * P],
                                                      proj[:, q.slot(2), u * P:(u + 1) * P], k["ident"][:])
                        ins.then_inc(s_q, 1)
                pipeline(pe, NG, 2, 4, 3, step)


def route_phase(nc, sem, tag, k, small, e_n, k_n, nt, groups, posi, pay, etab, table, extra=None):
    ctx = ExitStack()
    sb = lambda n, s, d=F32: ctx.enter_context(nc.sbuf_tensor(tag + n, s, d))
    ps = lambda n: ctx.enter_context(nc.psum_tensor(tag + n, [P, GT], F32))
    with ctx:
        sc, masked, sel, wgt, rank, pos, tmp = (sb(n, [P, T, e_n]) for n in (
            "sc", "masked", "sel", "wgt", "rank", "pos", "rtmp"))
        cmp = sb("cmp", [P, T, e_n, e_n])
        gs, grank, pair, gcmp = (sb(n, [P, T, GR0]) for n in ("gs", "grank", "pair", "gsel")) if groups else (None,) * 4
        gpc = sb("gcmp", [P, T, GR0, GR0]) if groups else None
        row = sb("row", [P, T])
        onesT = k["ones"][:, 0:T]
        incl = sb("incl", [P, T, e_n])
        cnt, ntf, endt, base = (sb(n, [P, e_n]) for n in ("cnt", "ntf", "endt", "base"))
        nti = sb("nti", [P, e_n], I32)
        posf = sb("posf", [P, T, k_n])
        gates = sb("gates", [P, T, k_n])
        tokid = sb("tokid", [P, T], I32)
        ji, jf = sb("ji", [1, nt], I32), sb("jf", [1, nt])
        ecmp = sb("ecmp", [1, nt, e_n])
        ef = sb("ef", [1, nt])
        zero = sb("zero", [P, nt * 2], I32)
        within, totals = ps("within"), ps("totals")
        s_sc, s_ch, s_sel, s_pre, s_e, s_ex = (sem(tag + n) for n in (
            "scores", "route_chain", "selected", "counted", "exp_in", "exp_out"))
        s_iota, s_zero, s_zeroed = (sem(tag + n) for n in ("iotas", "zeros", "table_zeroed"))
        W = T * e_n
        with nc.Block() as block:
            @block.scalar
            def _(act):
                if groups:
                    nc.scalar.activation(sc[:], small[:, :, 0:e_n], ACT.Sigmoid).then_inc(s_sc, 1)
                else:
                    nc.scalar.activation(sc[:], small[:, :, 0:e_n], ACT.Copy).then_inc(s_sc, 1)
                    act.wait_ge(s_e, 1)
                    nc.scalar.activation(wgt[:], tmp[:], ACT.Exp).then_inc(s_ex, 1)
                if extra:
                    extra["scalar"](act)

            @block.tensor
            def _(pe):
                pe.wait_ge(s_sel, 1)
                nc.tensor.matmul(within[:, 0:W], k["before"][:], sel[:].rearrange("p t e -> p (t e)"),
                                 start=True, stop=True)
                nc.tensor.matmul(totals[:, 0:W], k["ones"][:], sel[:].rearrange("p t e -> p (t e)"),
                                 start=True, stop=True).then_inc(s_pre, 1)
                if extra:
                    extra["tensor"](pe)

            @block.gpsimd
            def _(pool):
                nc.gpsimd.iota(tokid[:], pattern=[[P, T]], base=0, channel_multiplier=1).then_inc(s_iota, 1)
                nc.gpsimd.iota(ji[:], pattern=[[1, nt]], base=0, channel_multiplier=0).then_inc(s_iota, 1)
                nc.gpsimd.memset(zero[:], 0).then_inc(s_zero, 1)

            @block.sync
            def _(sp):
                sp.wait_ge(s_zero, 1)
                sp.dma_start(table.rearrange("(p a) b -> p (a b)", p=P), zero[:]).then_inc(s_zeroed, 16)
                sp.wait_ge(s_zeroed, 16)
                if extra:
                    extra["sync"](sp)

            @block.vector
            def _(dve):
                link = Chain(dve, s_ch)
                v = nc.vector

                def ranks(dst, src, n, buf):
                    link(v.memset(buf[:], 0.0))
                    for e in range(n):
                        one = src[:, :, e:e + 1]
                        if e + 1 < n:
                            ins = v.tensor_tensor(buf[:, :, e + 1:, e], one.to_broadcast([P, T, n - 1 - e]), src[:, :, e + 1:], ALU.is_ge)
                        if e:
                            ins = v.tensor_tensor(buf[:, :, :e, e], one.to_broadcast([P, T, e]), src[:, :, :e], ALU.is_gt)
                    link(ins)
                    link(v.tensor_reduce(dst[:], buf[:], AX.X, ALU.add))

                dve.wait_ge(s_sc, 1)
                if groups:
                    s4 = sc[:].rearrange("p t (g m) -> p t g m", m=E0 // GR0)
                    link(v.tensor_tensor(gs[:], s4[:, :, :, 0], s4[:, :, :, 1], ALU.add))
                    for a, b in ((0, 2), (0, 3), (1, 2), (1, 3), (2, 3)):
                        link(v.tensor_tensor(pair[:], s4[:, :, :, a], s4[:, :, :, b], ALU.add))
                        link(v.tensor_tensor(gs[:], gs[:], pair[:], ALU.max))
                    ranks(grank, gs, GR0, gpc)
                    link(v.tensor_scalar(gcmp[:], grank[:], float(TG0), None, ALU.is_lt))
                    m4 = masked[:].rearrange("p t (g m) -> p (t g) m", m=E0 // GR0)
                    allow = gcmp[:].rearrange("p t g -> p (t g)")
                    link(v.tensor_tensor(m4, sc[:].rearrange("p t (g m) -> p (t g) m", m=E0 // GR0),
                                         bcast(allow, E0 // GR0), ALU.mult))
                    link(v.tensor_scalar(gcmp[:], gcmp[:], 1.0, None, ALU.subtract))
                    link(v.tensor_tensor(m4, m4, bcast(allow, E0 // GR0), ALU.add))
                    ranks(rank, masked, e_n, cmp)
                else:
                    ranks(rank, sc, e_n, cmp)
                link(v.tensor_scalar(sel[:], rank[:], float(k_n), None, ALU.is_lt))
                dve.sem_inc(s_sel, 1)
                if groups:
                    link(v.tensor_tensor(wgt[:], sc[:], sel[:], ALU.mult))
                    link(v.tensor_reduce(row[:], wgt[:], AX.X, ALU.add))
                    link(v.tensor_scalar(row[:], row[:], 1e-6, None, ALU.add))
                else:
                    link(v.tensor_reduce(row[:], sc[:], AX.X, ALU.max))
                    link(v.tensor_tensor(tmp[:], sc[:], bcast(row[:], e_n), ALU.subtract))
                    dve.sem_inc(s_e, 1)
                    dve.wait_ge(s_ex, 1)
                    link(v.tensor_tensor(wgt[:], wgt[:], sel[:], ALU.mult))
                    link(v.tensor_reduce(row[:], wgt[:], AX.X, ALU.add))
                link(v.reciprocal(row[:], row[:]))
                link(v.tensor_tensor(wgt[:], wgt[:], bcast(row[:], e_n), ALU.mult))
                dve.wait_ge(s_pre, 1)
                tot = totals[:, 0:W].rearrange("p (t e) -> p t e", e=e_n)
                for e in range(e_n):
                    ins = v.tensor_tensor_scan(incl[:, :, e], onesT, tot[:, :, e], 0.0, ALU.mult, ALU.add)
                link(ins)
                link(v.tensor_scalar(nti[:], incl[:, T - 1, :], 1.0 / P, (P - 1 - 63.5) / P, ALU.mult, ALU.add))
                link(v.tensor_copy(ntf[:], nti[:]))
                link(v.tensor_tensor_scan(endt[:], k["ones"][:, 0:e_n], ntf[:], 0.0, ALU.mult, ALU.add))
                link(v.tensor_tensor(base[:], endt[:], ntf[:], ALU.subtract))
                link(v.tensor_tensor(pos[:], incl[:], tot, ALU.subtract))
                link(v.tensor_tensor(pos[:], pos[:], within[:, 0:W].rearrange("p (t e) -> p t e", e=e_n), ALU.add))
                link(v.scalar_tensor_tensor(pos[:], middle(base[:], T), float(P), pos[:], ALU.mult, ALU.add))
                for q in range(k_n):
                    link(v.scalar_tensor_tensor(tmp[:], rank[:], float(q), pos[:], ALU.is_equal, ALU.mult))
                    link(v.tensor_reduce(posf[:, :, q], tmp[:], AX.X, ALU.add))
                    link(v.scalar_tensor_tensor(tmp[:], rank[:], float(q), wgt[:], ALU.is_equal, ALU.mult))
                    link(v.tensor_reduce(gates[:, :, q], tmp[:], AX.X, ALU.add))
                link(v.tensor_copy(posi[:], posf[:]))
                dve.wait_ge(s_iota, 2)
                link(v.tensor_copy(pay[:, :, :, 0], bcast(tokid[:], k_n)))
                link(v.tensor_copy(pay[:, :, :, 1].bitcast(F32), gates[:]))
                link(v.tensor_copy(jf[:], ji[:]))
                link(v.tensor_tensor(ecmp[:], middle(endt[0:1, :], nt), bcast(jf[:], e_n), ALU.is_le))
                link(v.tensor_reduce(ef[:], ecmp[:], AX.X, ALU.add))
                link(v.tensor_scalar(etab[:], ef[:], float(e_n - 1), None, ALU.min))
                if extra:
                    extra["vector"](dve)


def scatter_slots(nc, pool, posi, pay, table, k_n, idx_ring, pay_ring, s_copy, s_scat, s_settled):
    def step(s):
        r, at = s.slot(2), s.back(2)
        if not isinstance(at.n, int) or at.n >= 0:
            pool.wait_ge(s_scat[r], at.rounds(2) * 16 * k_n + 16 * k_n)
            pool.sem_inc(s_settled, 1)
        nc.gpsimd.tensor_copy(idx_ring[:, r:r + 1, :], posi[:, ds(s.n, 1), :])
        nc.gpsimd.tensor_copy(pay_ring[:, r:r + 1, :, :], pay[:, ds(s.n, 1), :, :]).then_inc(s_copy, 1)
        reached(pool, s_copy, s)
        pool.sem_inc(s_settled, 1)
        for q in range(k_n):
            pool.indirect_dma_start(table, bass.IndirectOffsetOnAxis(idx_ring[:, r, q:q + 1], 0),
                                    pay_ring[:, r, q, :], None).then_inc(s_scat[r], 16)
    pipeline(pool, T, 2, 2, 0, step)
    for r in range(2):
        pool.wait_ge(s_scat[r], T // 2 * k_n * 16)


def decay_work(nc, ctx, sem, k, small, bias_dt, a_log, dt, tabs, acum_dram, w_out, norm_col, s_weights):
    sb = lambda n, s, d=F32: ctx.enter_context(nc.sbuf_tensor(n, s, d))
    ps = lambda n: ctx.enter_context(nc.psum_tensor(n, [P, GT], F32))
    u, e, z, z2, acc = (sb(n, [P, T, H]) for n in ("dt_u", "dt_e", "dt_z", "dt_z2", "dt_acc"))
    ea = sb("exp_a", [P, H])
    rowsT = sb("acum_rows", [P, T // BIG, P])
    sum_ps = [ps(f"sum{n}") for n in range(2)]
    tot_ps = [ps(f"tot{n}") for n in range(2)]
    row_ps = [ps(f"row{n}") for n in range(2)]
    s_u, s_e, s_ch, s_adt, s_sum, s_rows, s_rowc, s_k, s_exp, s_st = (sem("dt_" + n) for n in (
        "u", "exp", "chain", "adt", "sums", "rows", "rows_kept", "diff", "exps", "stored"))
    cols = T * H // 2
    half = lambda ap, n: ap[:, n * T // 2:(n + 1) * T // 2, :]

    def vector(dve):
        v = nc.vector
        link = Chain(dve, s_ch)
        dve.wait_ge(s_weights, 16 * N_LOADS)
        for c in range(CH):
            v.tensor_scalar(w_out[:, c, :], w_out[:, c, :], norm_col[:, c:c + 1], None, ALU.mult)
        link(v.tensor_tensor(bias_dt[:, 0, :], bias_dt[:, 0, :], bias_dt[:, 1, :], ALU.add))
        link(v.tensor_tensor(u[:], small[:, :, E0:SM0], middle(bias_dt[:, 0, :], T), ALU.add))
        link(v.tensor_scalar(z[:], u[:], -1.0, None, ALU.mult))
        link(v.tensor_tensor(z[:], u[:], z[:], ALU.min))
        dve.sem_inc(s_u, 1)
        dve.wait_ge(s_e, 2)
        link(v.tensor_scalar(z[:], e[:], 2.0, None, ALU.add))
        link(v.reciprocal(z[:], z[:]))
        link(v.tensor_tensor(z[:], z[:], e[:], ALU.mult))
        link(v.tensor_tensor(z2[:], z[:], z[:], ALU.mult))
        top = 17
        link(v.tensor_scalar(acc[:], z2[:], 1.0 / top, None, ALU.mult))
        for n in range(top - 2, 1, -2):
            link(v.scalar_tensor_tensor(acc[:], acc[:], 1.0 / n, z2[:], ALU.add, ALU.mult))
        link(v.scalar_tensor_tensor(acc[:], acc[:], 1.0, z[:], ALU.add, ALU.mult))
        link(v.tensor_scalar(u[:], u[:], 0.0, None, ALU.max))
        link(v.scalar_tensor_tensor(dt[:], acc[:], 2.0, u[:], ALU.mult, ALU.add))
        link(v.tensor_tensor(u[:], dt[:], middle(ea[:], T), ALU.mult))
        link(v.tensor_scalar(u[:], u[:], -1.0, None, ALU.mult))
        dve.sem_inc(s_adt, 1)
        dve.wait_ge(s_sum, 1)
        for n in range(2):
            s3 = sum_ps[n][:].rearrange("p (t h) -> p t h", h=H)
            t3 = tot_ps[n][:].rearrange("p (t h) -> p t h", h=H)
            link(v.tensor_copy(half(tabs[:, :, 0, :], n), s3))
            link(v.tensor_tensor(half(tabs[:, :, 2, :], n), t3, half(tabs[:, :, 0, :], n), ALU.subtract))
            link(v.tensor_copy(half(tabs[:, :, 3, :], n), t3))
        dve.sem_inc(s_k, 1)

    def scalar(act):
        act.wait_ge(s_weights, 16 * N_LOADS)
        act.wait_ge(s_u, 1)
        nc.scalar.activation(e[:], z[:], ACT.Exp).then_inc(s_e, 1)
        nc.scalar.activation(ea[:], a_log[:], ACT.Exp).then_inc(s_e, 1)
        for g in range(T // BIG):
            act.wait_ge(s_rows, g + 1)
            nc.scalar.activation(rowsT[:, g, :], row_ps[g % 2][:, 0:P], ACT.Copy).then_inc(s_rowc, 1)
        act.wait_ge(s_k, 1)
        nc.scalar.activation(tabs[:, :, 1, :], tabs[:, :, 0, :], ACT.Exp).then_inc(s_exp, 1)
        nc.scalar.activation(tabs[:, :, 2:4, :].rearrange("p t a h -> p t (a h)"),
                             tabs[:, :, 2:4, :].rearrange("p t a h -> p t (a h)"), ACT.Exp).then_inc(s_exp, 1)

    def tensor(pe):
        pe.wait_ge(s_adt, 1)
        flat = u[:].rearrange("p t h -> p (t h)")
        for n in range(2):
            nc.tensor.matmul(sum_ps[n][:], k["upto"][:], flat[:, n * cols:(n + 1) * cols], start=True, stop=True)
            ins = nc.tensor.matmul(tot_ps[n][:], k["ones"][:], flat[:, n * cols:(n + 1) * cols], start=True, stop=True)
        ins.then_inc(s_sum, 1)
        for g in range(T // BIG):
            if g >= 2:
                pe.wait_ge(s_rowc, g - 1)
            nc.tensor.matmul(row_ps[g % 2][:, 0:P], flat[:, g * P:(g + 1) * P], k["upto"][:],
                             start=True, stop=True).then_inc(s_rows, 1)

    def sync(sp):
        sp.wait_ge(s_rowc, T // BIG)
        sp.dma_start(acum_dram.rearrange("(g a) h l -> (a h) g l", a=BIG), rowsT[:]).then_inc(s_st, 16)
        sp.wait_ge(s_st, 16)

    return {"vector": vector, "scalar": scalar, "tensor": tensor, "sync": sync}


BEATS = 32


class Events:

    def __init__(self, sem, per):
        self.sem, self.per = sem, per

    def wait(self, eng, i, n):
        value = i * self.per + n
        if not isinstance(value, int) or value > 0:
            eng.wait_ge(self.sem, value)


def beats(eng, tail, body):
    def run(i, b):
        def at(lag):
            j, c = (i, b - lag) if b >= lag else (i - 1, b - lag + BEATS)
            return None if isinstance(j, int) and not 0 <= j < NB else (j, c)
        body(at)

    for b in range(BEATS):
        run(0, b)
    with eng.Fori(1, NB) as i:
        for b in range(BEATS):
            run(i, b)
    for b in range(tail):
        run(NB, b)


def ssd_phase(nc, sem, k, xnT, w_proj, w_out, bias, conv, d_col, dt, tabs, acum_dram, ss, mo_dram,
              posi, pay, table):
    ctx = ExitStack()
    sb = lambda n, s, d=F32: ctx.enter_context(nc.sbuf_tensor("m_" + n, s, d))
    with ctx:
        raw = sb("raw", [P, 2, TAPS - 1 + BLK])
        halo = sb("halo", [P, CC, TAPS - 1])
        cv = sb("cv", [P, 2, BLK])
        hT = sb("hT", [P, CC, BLK])
        cT = sb("cT", [P, BLK])
        gT = sb("gT", [P, CH, BLK])
        hdt = sb("hdt", [P, TB, INTER])
        btok = sb("btok", [P, TB, N])
        ta = sb("ta", [P, TB, H])
        tb = sb("tb", [P, TB, 3, H])
        gm = sb("gm", [P, TB, P])
        ar = sb("ar", [P, 4, HQ, P])
        y1 = sb("y1", [P, 2, GW])
        hdd = sb("hdd", [P, 2, GW])
        state = sb("state", [P, INTER])
        sq = sb("sq", [P, 2, CQ, P])
        sqs = sb("sqs", [P, TB, P])
        bias3 = sb("bias3", [P, CC])
        mo = sb("mo", [P, TB, D])
        idx_ring = sb("idx_ring", [P, TB, K0], I32)
        pay_ring = sb("pay_ring", [P, TB, K0, 2], I32)
        pj = [ctx.enter_context(nc.psum_tensor(f"m_pj{n}", [P, GT], F32)) for n in range(2)]
        x_ps = [ctx.enter_context(nc.psum_tensor(f"m_x{n}", [P, GT], F32)) for n in range(2)]
        yt = [ctx.enter_context(nc.psum_tensor(f"m_yt{n}", [P, GT], F32)) for n in range(2)]
        tr, out_ps = (ctx.enter_context(nc.psum_tensor("m_" + n, [P, GT], F32)) for n in ("tr", "out"))
        ev = lambda name, per: Events(sem("m_" + name), per)

        items = [([("h", b // 2)] if b % 2 == 0 else [("h", CH + b // 2)] * (b in (1, 3)) + [("g", b // 2)])
                 for b in range(BEATS)]
        flat = [x for beat in items for x in beat]
        convs = [x for x in flat if x[0] == "h"]
        convs_at = lambda b: [(convs.index(x), x[1]) for x in items[b] if x[0] == "h"]
        TURN_G, TURN_B = 6, 10
        turns = sorted([(2 * c + 3, c) for c in range(CH)] + [(TURN_G, "G"), (TURN_B, "B")], key=lambda x: x[0])
        turn_no = {what: n for n, (_, what) in enumerate(turns)}

        def turned_at(b, late):
            return [(n, what) for n, (beat, what) in enumerate(turns) if beat == b - late]

        NTURN = len(turns)
        OLD = TAPS - 1
        projected, kept = ev("projected", len(flat)), ev("kept", len(flat))
        haloed, saved = ev("haloed", CC), ev("saved", CC)
        tapped, silued = ev("tapped", CC * OLD), ev("silued", CC)
        turned, turn_kept = ev("turned", NTURN), ev("turn_kept", NTURN)
        ta_done, tb_done, c_copied = ev("sums_copied", 1), ev("decays_copied", 1), ev("c_copied", 1)
        clipped, exped, mixed = ev("clipped", STEPS), ev("exped", STEPS), ev("mixed", STEPS)
        off, upd, diag = ev("off_done", STEPS), ev("update_done", STEPS), ev("diag_done", STEPS)
        y1d, grown = ev("y1_done", STEPS), ev("state_grown", STEPS)
        hddd, aged = ev("hdd_done", STEPS), ev("state_aged", STEPS)
        ytd, y3d, gated = ev("y_turned", STEPS), ev("y3_done", STEPS * CQ), ev("gated", STEPS)
        squared, summed, outd, mok = ev("squared", STEPS), ev("squares_summed", STEPS), ev("out_done", STEPS), ev("mo_kept", 1)
        ss_done, ss_kept, parted = ev("ss_done", 1), ev("ss_kept", 1), ev("part_summed", STEPS * 2 - TB)
        s_ar = [sem(f"m_rows_loaded{n}") for n in range(4)]
        s_mo, s_ring = sem("m_mo_stored"), sem("m_ring_copied")
        s_scat = sem.lasting("m_scattered")
        s_bias, s_init, s_sp, s_act, s_dve, s_pool = (sem("m_" + n) for n in (
            "tap_bias", "init", "sp_settled", "act_settled", "dve_settled", "pool_settled"))
        acum_rows = acum_dram.rearrange("t h l -> t (h l)")

        LAG_ROWS, LAG_CLIP, LAG_EXP, LAG_MIX = 2, 6, 7, 9
        LAG_OFF, LAG_DIAG, LAG_TURN, LAG_GATE, LAG_SQ, LAG_SUM, LAG_SS, LAG_OUT = 12, 13, 14, 15, 16, 17, 18, 19
        LAG_MO = (STEPS - 1) * 4 + 20
        LAG_TILE = LAG_MO - (STEPS - 1) * 4
        TAIL = LAG_MO - BEATS + 1

        def step_at(at, lag):
            x = at(lag)
            if x is None or x[1] % 4:
                return None
            s = x[1] // 4
            return x[0], s, s // TB, s % TB

        with nc.Block() as block:
            @block.sync
            def _(sp):
                def body(at):
                    st = step_at(at, LAG_ROWS)
                    if st:
                        i, s, q, t = st
                        diag.wait(sp, i, s - 3)
                        sp.sem_inc(s_sp, 1)
                        src = acum_rows[ds(i * TB + t, 1), q * HQ * P:(q + 1) * HQ * P]
                        sp.dma_start(ar[:, s % 4].rearrange("p h l -> p (h l)"),
                                     src.rearrange("a n -> (a n)").partition_broadcast(P)).then_inc(s_ar[s % 4], 16)
                sp.sem_inc(s_mo, 16)
                beats(sp, TAIL, body)
                sp.wait_ge(s_mo, NB * 16 + 16)

            @block.gpsimd
            def _(pool):
                g = nc.gpsimd
                g.memset(halo[:], 0.0).then_inc(s_init, 1)
                g.memset(state[:], 0.0).then_inc(s_init, 1)
                pool.wait_ge(s_init, 2)

                def body(at):
                    st = step_at(at, LAG_MIX)
                    if st:
                        i, s, q, t = st
                        exped.wait(pool, i, s + 1)
                        turn_kept.wait(pool, i, turn_no["G"] + 1)
                        g.tensor_tensor(ar[:, s % 4], ar[:, s % 4], middle(gm[:, t, :], HQ), ALU.mult).then_inc(mixed.sem, 1)
                    st = step_at(at, LAG_OFF)
                    if st:
                        i, s, q, t = st
                        cols = slice(q * GW, (q + 1) * GW)
                        tb_done.wait(pool, i, 1)
                        turn_kept.wait(pool, i, turn_no[q * CQ + CQ - 1] + 1)
                        upd.wait(pool, i, s - 1)
                        g.tensor_tensor(hdd[:, s % 2].rearrange("p (h c) -> p h c", c=HP),
                                        hdt[:, t, cols].rearrange("p (h c) -> p h c", c=HP),
                                        bcast(tb[:, t, 1, q * HQ:(q + 1) * HQ], HP), ALU.mult).then_inc(hddd.sem, 1)
                        off.wait(pool, i, s + 1)
                        grown.wait(pool, i, s)
                        sv = state[:, cols].rearrange("p (h c) -> p h c", c=HP)
                        g.tensor_tensor(sv, sv, bcast(tb[:, t, 2, q * HQ:(q + 1) * HQ], HP), ALU.mult).then_inc(aged.sem, 1)
                    st = step_at(at, LAG_SUM)
                    if st:
                        i, s, q, t = st
                        squared.wait(pool, i, s + 1)
                        pair = sq[:, s % 2, 0:CQ // 2]
                        g.tensor_tensor(pair, pair, sq[:, s % 2, CQ // 2:], ALU.add).then_inc(parted.sem, 1)
                        parted.wait(pool, i, s + 1 + max(0, s - TB))
                        if q == 0:
                            if s == 0:
                                ss_done.wait(pool, i, 0)
                            g.tensor_tensor(sqs[:, t, :], pair[:, 0], pair[:, 1], ALU.add).then_inc(summed.sem, 1)
                        else:
                            g.tensor_tensor(pair[:, 0], pair[:, 0], pair[:, 1], ALU.add).then_inc(parted.sem, 1)
                            parted.wait(pool, i, s + 2 + s - TB)
                            summed.wait(pool, i, s - 1)
                            g.tensor_tensor(sqs[:, t, :], sqs[:, t, :], pair[:, 0], ALU.add).then_inc(summed.sem, 1)
                    x = at(0)
                    if x and x[1] == 0:
                        i = x[0]
                        if not isinstance(i, int) or i:
                            pool.wait_ge(s_scat, i * (TB * K0 * 16))
                            pool.sem_inc(s_pool, 1)
                        g.tensor_copy(idx_ring[:], posi[:, ds(i * TB, TB), :]).then_inc(s_ring, 1)
                        g.tensor_copy(pay_ring[:], pay[:, ds(i * TB, TB), :, :]).then_inc(s_ring, 1)
                    if x and x[1] % 4 == 3:
                        t, q = divmod(x[1] // 4, K0)
                        if x[1] == 3:
                            pool.wait_ge(s_ring, x[0] * 2 + 2)
                            pool.sem_inc(s_pool, 1)
                        pool.indirect_dma_start(table, bass.IndirectOffsetOnAxis(idx_ring[:, t, q:q + 1], 0),
                                                pay_ring[:, t, q, :], None).then_inc(s_scat, 16)
                    x = at(1)
                    if x:
                        for n, c in convs_at(x[1]):
                            kept.wait(pool, x[0], flat.index(("h", c)) + 1)
                            haloed.wait(pool, x[0], n + 1)
                            pool.sem_inc(s_pool, 1)
                            g.tensor_copy(halo[:, c, :], raw[:, n % 2, BLK:]).then_inc(saved.sem, 1)
                    x = at(0)
                    if x:
                        for n, c in convs_at(x[1]):
                            tapped.wait(pool, x[0], (n - 1) * OLD)
                            saved.wait(pool, x[0], n + 1 - CC)
                            pool.sem_inc(s_pool, 1)
                            g.tensor_copy(raw[:, n % 2, 0:TAPS - 1], halo[:, c, :]).then_inc(haloed.sem, 1)
                beats(pool, TAIL, body)
                pool.wait_ge(s_scat, NB * TB * K0 * 16)

            @block.scalar
            def _(act):
                act.wait_ge(s_bias, 1)
                def body(at):
                    st = step_at(at, LAG_EXP)
                    if st:
                        i, s, q, t = st
                        clipped.wait(act, i, s + 1)
                        a = ar[:, s % 4].rearrange("p h l -> p (h l)")
                        nc.scalar.activation(a, a, ACT.Exp).then_inc(exped.sem, 1)
                    st = step_at(at, LAG_SQ)
                    if st:
                        i, s, q, t = st
                        gated.wait(act, i, s + 1)
                        summed.wait(act, i, s - 1)
                        nc.scalar.activation(sq[:, s % 2], gT[:, q * CQ:(q + 1) * CQ, t * P:(t + 1) * P],
                                             ACT.Square).then_inc(squared.sem, 1)
                    st = step_at(at, LAG_SS)
                    if st and st[1] == STEPS - 1:
                        i = st[0]
                        ss_done.wait(act, i, 1)
                        act.sem_inc(s_act, 1)
                        nc.scalar.activation(ss[:, ds(i * TB, TB)], tr[:, 0:TB], ACT.Copy).then_inc(ss_kept.sem, 1)
                    st = step_at(at, LAG_TILE)
                    if st and st[1] == STEPS - 1:
                        i = st[0]
                        outd.wait(act, i, STEPS)
                        act.wait_ge(s_mo, i * 16 + 16)
                        act.sem_inc(s_act, 1)
                        nc.scalar.activation(mo[:].rearrange("p t d -> p (t d)"), out_ps[:], ACT.Copy).then_inc(mok.sem, 1)
                        mok.wait(act, i, 1)
                        act.sem_inc(s_act, 1)
                        act.dma_start(tokens(mo_dram, i * TB, TB), mo[:]).then_inc(s_mo, 16)
                    x = at(2)
                    if x:
                        i = x[0]
                        for n, c in convs_at(x[1]):
                            if c < CH:
                                y3d.wait(act, i - 1, (c // CQ + 1) * TB * CQ)
                            else:
                                turned.wait(act, i - 1, turn_no["B"] + 1)
                                c_copied.wait(act, i, 0)
                            tapped.wait(act, i, (n + 1) * OLD)
                            nc.scalar.activation(hT[:, c, :], cv[:, n % 2, :], ACT.Silu).then_inc(silued.sem, 1)
                    x = at(0)
                    if x:
                        i = x[0]
                        for kind, c in items[x[1]]:
                            m = flat.index((kind, c))
                            if kind == "h":
                                n = convs.index((kind, c))
                                tapped.wait(act, i, (n - 1) * OLD)
                                saved.wait(act, i, n - 1)
                                projected.wait(act, i, m + 1)
                                nc.scalar.activation(raw[:, n % 2, TAPS - 1:], pj[m % 2][:, 0:BLK], ACT.Identity,
                                                     bias=bias[:, CH + c:CH + c + 1])
                                silued.wait(act, i, n - 1)
                                nc.scalar.activation(cv[:, n % 2, :], pj[m % 2][:, 0:BLK], ACT.Identity,
                                                     bias=bias3[:, c:c + 1],
                                                     scale=conv[:, c, OLD:TAPS]).then_inc(kept.sem, 1)
                            else:
                                outd.wait(act, i - 1, (c // CQ + 1) * TB)
                                projected.wait(act, i, m + 1)
                                nc.scalar.activation(gT[:, c, :], pj[m % 2][:, 0:BLK], ACT.Silu,
                                                     bias=bias[:, c:c + 1]).then_inc(kept.sem, 1)
                beats(act, TAIL, body)

            @block.vector
            def _(dve):
                v = nc.vector
                v.tensor_tensor(bias3[:], bias[:, CH:CH + CC], conv[:, :, OLD], ALU.mult).then_inc(s_bias, 1)

                def body(at):
                    x = at(0)
                    if x and x[1] == 4:
                        clipped.wait(dve, x[0], 0)
                        dve.sem_inc(s_dve, 1)
                        v.tensor_copy(ta[:], tabs[:, ds(x[0] * TB, TB), 0, :]).then_inc(ta_done.sem, 1)
                    if x and x[1] == 11:
                        hddd.wait(dve, x[0], 0)
                        aged.wait(dve, x[0], 0)
                        y1d.wait(dve, x[0], 0)
                        dve.sem_inc(s_dve, 1)
                        v.tensor_copy(tb[:], tabs[:, ds(x[0] * TB, TB), 1:4, :]).then_inc(tb_done.sem, 1)
                    if x and x[1] == 10:
                        silued.wait(dve, x[0], convs.index(("h", CH + 1)) + 1)
                        off.wait(dve, x[0], 0)
                        v.tensor_copy(cT[:], hT[:, CH + 1, :]).then_inc(c_copied.sem, 1)

                    st = step_at(at, LAG_CLIP)
                    if st:
                        i, s, q, t = st
                        dve.wait_ge(s_ar[s % 4], (i * 2 + s // 4) * 16 + 16)
                        if s == 0:
                            ta_done.wait(dve, i, 1)
                        for h in range(HQ):
                            a = ar[:, s % 4, h, :]
                            ins = v.tensor_scalar(a, a, ta[:, t, q * HQ + h:q * HQ + h + 1], 0.0, ALU.subtract, ALU.min)
                        ins.then_inc(clipped.sem, 1)
                    st = step_at(at, LAG_OFF)
                    if st:
                        i, s, q, t = st
                        off.wait(dve, i, s + 1)
                        tb_done.wait(dve, i, 1)
                        ytd.wait(dve, i, s - 1)
                        v.tensor_tensor(y1[:, s % 2].rearrange("p (h c) -> p h c", c=HP),
                                        x_ps[0][:].rearrange("p (h c) -> p h c", c=HP),
                                        bcast(tb[:, t, 0, q * HQ:(q + 1) * HQ], HP), ALU.mult).then_inc(y1d.sem, 1)
                        upd.wait(dve, i, s + 1)
                        aged.wait(dve, i, s + 1)
                        cols = slice(q * GW, (q + 1) * GW)
                        v.tensor_tensor(state[:, cols], state[:, cols], x_ps[1][:], ALU.add).then_inc(grown.sem, 1)
                    st = step_at(at, LAG_GATE)
                    if st:
                        i, s, q, t = st
                        ytd.wait(dve, i, s + 1)
                        for c in range(CQ):
                            cc = q * CQ + c
                            v.scalar_tensor_tensor(yt[s % 2][:, c * P:(c + 1) * P], hT[:, cc, t * P:(t + 1) * P],
                                                   d_col[:, cc:cc + 1], yt[s % 2][:, c * P:(c + 1) * P],
                                                   ALU.mult, ALU.add).then_inc(y3d.sem, 1)
                        y3d.wait(dve, i, s * CQ + CQ)
                        kept.wait(dve, i, flat.index(("g", q * CQ + CQ - 1)) + 1)
                        gg = gT[:, q * CQ:(q + 1) * CQ, t * P:(t + 1) * P]
                        v.tensor_tensor(gg, gg, yt[s % 2][:].rearrange("p (c l) -> p c l", l=P), ALU.mult).then_inc(gated.sem, 1)

                    for lag_block in (0, BEATS):
                        x = at(0) if not lag_block else at(BEATS)
                        if x:
                            for n, what in turned_at(x[1] + lag_block, 1):
                                i = x[0]
                                src = tr[:, 0:BLK].rearrange("p (t c) -> p t c", t=TB)
                                turned.wait(dve, i, n + 1)
                                if what == "G":
                                    mixed.wait(dve, i, 0)
                                    v.tensor_tensor(gm[:], src, middle(k["upto"][:], TB), ALU.mult).then_inc(turn_kept.sem, 1)
                                elif what == "B":
                                    upd.wait(dve, i, 0)
                                    v.tensor_copy(btok[:], src).then_inc(turn_kept.sem, 1)
                                else:
                                    diag.wait(dve, i - 1, (what // CQ + 1) * TB)
                                    hddd.wait(dve, i - 1, (what // CQ + 1) * TB)
                                    v.tensor_tensor(hdt[:, :, what * P:(what + 1) * P].rearrange("p t (h d) -> p t h d", d=HP),
                                                    src.rearrange("p t (h d) -> p t h d", d=HP),
                                                    dt[:, ds(i * TB, TB), 2 * what:2 * what + 2].unsqueeze(3)
                                                    .to_broadcast([P, TB, 2, HP]), ALU.mult).then_inc(turn_kept.sem, 1)
                    x = at(1)
                    if x:
                        i = x[0]
                        for n, c in convs_at(x[1]):
                            haloed.wait(dve, i, n + 1)
                            kept.wait(dve, i, flat.index(("h", c)) + 1)
                            r, o = raw[:, n % 2], cv[:, n % 2, :]
                            for j in range(OLD):
                                if j:
                                    tapped.wait(dve, i, n * OLD + j)
                                v.scalar_tensor_tensor(o, r[:, j:j + BLK], conv[:, c, j:j + 1], o,
                                                       ALU.mult, ALU.add).then_inc(tapped.sem, 1)
                beats(dve, TAIL, body)

            @block.tensor
            def _(pe):
                mm = nc.tensor.matmul

                def body(at):
                    st = step_at(at, LAG_OFF)
                    if st:
                        i, s, q, t = st
                        cols = slice(q * GW, (q + 1) * GW)
                        grown.wait(pe, i, s)
                        y1d.wait(pe, i, s)
                        c_copied.wait(pe, i, 1)
                        mm(x_ps[0][:], cT[:, t * P:(t + 1) * P], state[:, cols], start=True, stop=True).then_inc(off.sem, 1)
                        hddd.wait(pe, i, s + 1)
                        turn_kept.wait(pe, i, turn_no["B"] + 1)
                        mm(x_ps[1][:], btok[:, t, :], hdd[:, s % 2], start=True, stop=True).then_inc(upd.sem, 1)
                    st = step_at(at, LAG_DIAG)
                    if st:
                        i, s, q, t = st
                        gated.wait(pe, i, s - 1)
                        mixed.wait(pe, i, s + 1)
                        for h in range(HQ):
                            hc, c = (q * HQ + h) * HP, h // 2
                            half = slice(h % 2 * HP, (h % 2 + 1) * HP)
                            ins = mm(yt[s % 2][half, c * P:(c + 1) * P], hdt[:, t, hc:hc + HP], ar[:, s % 4, h, :],
                                     start=c == 0, stop=False, skip_group_check=True)
                        ins.then_inc(diag.sem, 1)
                    st = step_at(at, LAG_TURN)
                    if st:
                        i, s, q, t = st
                        y1d.wait(pe, i, s + 1)
                        for c in range(CQ):
                            ins = mm(yt[s % 2][:, c * P:(c + 1) * P], y1[:, s % 2, c * P:(c + 1) * P], k["ident"][:],
                                     start=False, stop=True, skip_group_check=True)
                        ins.then_inc(ytd.sem, 1)
                    st = step_at(at, LAG_OUT)
                    if st:
                        i, s, q, t = st
                        gated.wait(pe, i, s + 1)
                        if s == 0:
                            mok.wait(pe, i, 0)
                        for c in range(CQ):
                            cc = q * CQ + c
                            ins = mm(out_ps[:, t * D:(t + 1) * D], gT[:, cc, t * P:(t + 1) * P], w_out[:, cc, :],
                                     start=s == 0 and c == 0, stop=cc == CH - 1, skip_group_check=True)
                        ins.then_inc(outd.sem, 1)
                    st = step_at(at, LAG_SS)
                    if st and st[1] == STEPS - 1:
                        i = st[0]
                        if isinstance(i, int) and i == NB - 1:
                            turn_kept.wait(pe, i, NTURN)
                        else:
                            turn_kept.wait(pe, i + 1, len([b for b, _ in turns if b < (STEPS - 1) * 4 + LAG_SS - BEATS]))
                        summed.wait(pe, i, STEPS)
                        for t in range(TB):
                            ins = mm(tr[:, t:t + 1], sqs[:, t, :], k["ones"][:, 0:1], start=True, stop=True)
                        ins.then_inc(ss_done.sem, 1)

                    for lag_block in (0, BEATS):
                        x = at(0) if not lag_block else at(BEATS)
                        if x:
                            for n, what in turned_at(x[1] + lag_block, 0):
                                i = x[0]
                                turn_kept.wait(pe, i, n)
                                if turns[n][0] > (STEPS - 1) * 4 + LAG_SS - BEATS:
                                    ss_kept.wait(pe, i, 0)
                                chunk = {"G": CH + 1, "B": CH}.get(what, what)
                                silued.wait(pe, i, convs.index(("h", chunk)) + 1)
                                for t in range(TB):
                                    rows = slice(t * P, (t + 1) * P)
                                    if what == "G":
                                        ins = mm(tr[:, rows], hT[:, CH, rows], hT[:, CH + 1, rows], start=True, stop=True)
                                    else:
                                        ins = nc.tensor.transpose(tr[:, rows], hT[:, chunk, rows], k["ident"][:])
                                ins.then_inc(turned.sem, 1)
                    x = at(0)
                    if x:
                        i = x[0]
                        for kind, c in items[x[1]]:
                            m = flat.index((kind, c))
                            kept.wait(pe, i, m - 1)
                            col = ((CH if kind == "h" else 0) + c) * P
                            for kd in range(KD):
                                ins = mm(pj[m % 2][:, 0:BLK], w_proj[:, kd, col:col + P], xnT[:, kd, ds(i * BLK, BLK)],
                                         start=kd == 0, stop=kd == KD - 1)
                            ins.then_inc(projected.sem, 1)
                beats(pe, TAIL, body)


def expert_phase(nc, sem, tag, k, rows, table, etab, wup, wdown, e_n, f, nt, y_dram, loads):
    ctx = ExitStack()
    sb = lambda n, s, d=F32: ctx.enter_context(nc.sbuf_tensor(tag + n, s, d))
    ps = lambda n, w=GT: ctx.enter_context(nc.psum_tensor(tag + n, [P, w], F32))
    FC = f // P
    UB = max(1, 2 * f // GT)
    with ctx:
        tab = sb("tab", [P, 4, 2], I32)
        xg = sb("xg", [P, 4, D])
        xgT = sb("xgT", [P, 2, KD, P])
        sil = sb("sil", [P, 2, f])
        hid = sb("hid", [P, 2, f])
        hidT = sb("hidT", [P, 2, f])
        y = sb("y", [P, 2, D])
        x_ps = ps("x_ps")
        u_ps = [[ps(f"u{r}{b}") for b in range(UB)] for r in range(2)]
        h_ps = ps("h_ps")
        d_ps = [ps("d0"), ps("d1")] if UB == 1 else [ps("d0")] * 2
        RD = 2 if UB == 1 else 1
        s_w = [sem(f"{tag}weights{n}") for n in range(len(loads))]
        s_tab = [sem(f"{tag}table_loaded{n}") for n in range(4)]
        s_xg = [sem.lasting(f"{tag}gathered{n}") for n in range(4)]
        s_y = [sem(f"{tag}y_stored{n}") for n in range(2)]
        s_xt, s_xk, s_up, s_sil, s_hid, s_ht, s_hk, s_dn, s_yk, s_set = (sem(tag + n) for n in (
            "x_turned", "x_kept", "up_done", "silu_done", "hidden", "hidden_turned", "hidden_kept",
            "down_done", "y_kept", "settled"))
        with nc.Block() as block:
            @block.sync
            def _(sp):
                def step(s):
                    if s.inside(nt):
                        reached(sp, s_hid, s, 4)
                        landed(sp, s_xg, s, 4)
                        sp.sem_inc(s_set, 1)
                        sp.dma_start(tab[:, s.slot(4):s.slot(4) + 1, :], tokens(table, s.n)).then_inc(s_tab[s.slot(4)], 16)
                    o = s.back(7)
                    if o.inside(nt):
                        reached(sp, s_yk, o)
                        sp.sem_inc(s_set, 1)
                        sp.dma_start(tokens(y_dram, o.n), y[:, o.slot(2):o.slot(2) + 1, :]).then_inc(s_y[o.slot(2)], 16)
                pipeline(sp, nt, 4, 12, 7, step)
                for r in range(2):
                    sp.wait_ge(s_y[r], nt // 2 * 16)

            @block.gpsimd
            def _(pool):
                def step(s):
                    if s.inside(nt):
                        reached(pool, s_xt, s, 4)
                        landed(pool, s_tab, s)
                        pool.sem_inc(s_set, 1)
                        r = s.slot(4)
                        pool.indirect_dma_start(xg[:, r, :], None, rows,
                                                bass.IndirectOffsetOnAxis(tab[:, r, 0:1], 0)).then_inc(s_xg[r], 16)
                pipeline(pool, nt, 4, 4, 0, step)

            @block.scalar
            def _(act):
                for load, s in zip(loads, s_w):
                    load(act).then_inc(s, 16)

                def step(s):
                    a = s.back(1)
                    if a.inside(nt):
                        reached(act, s_up, a)
                        reached(act, s_hid, a, 2)
                        nc.scalar.activation(sil[:, a.slot(2), :], u_ps[a.slot(2)][0][:, 0:f], ACT.Silu).then_inc(s_sil, 1)
                    b = s.back(2)
                    if b.inside(nt):
                        reached(act, s_ht, b)
                        reached(act, s_dn, b, 2)
                        nc.scalar.activation(hidT[:, b.slot(2), :], h_ps[:, 0:f], ACT.Copy).then_inc(s_hk, 1)
                pipeline(act, nt, 4, 8, 3, step)

            @block.vector
            def _(dve):
                v = nc.vector

                def step(s):
                    if s.inside(nt):
                        reached(dve, s_xt, s)
                        reached(dve, s_up, s, 2)
                        v.tensor_copy(xgT[:, s.slot(2)].rearrange("p c t -> p (c t)"), x_ps[:, 0:D]).then_inc(s_xk, 1)
                    a = s.back(1)
                    if a.inside(nt):
                        reached(dve, s_sil, a)
                        reached(dve, s_ht, a, 2)
                        second = u_ps[a.slot(2)][UB - 1][:, f * (2 - UB):f * (3 - UB)] if UB == 1 else u_ps[a.slot(2)][1][:, 0:f]
                        v.scalar_tensor_tensor(hid[:, a.slot(2), :], sil[:, a.slot(2), :],
                                               tab[:, a.slot(4), 1:2].bitcast(F32), second,
                                               ALU.mult, ALU.mult).then_inc(s_hid, 1)
                    c = s.back(3)
                    if c.inside(nt):
                        reached(dve, s_dn, c)
                        landed(dve, s_y, c, 2)
                        v.tensor_copy(y[:, c.slot(2), :], d_ps[c.slot(2)][:, 0:D]).then_inc(s_yk, 1)
                pipeline(dve, nt, 4, 8, 3, step)

            @block.tensor
            def _(pe):
                for s in s_w:
                    pe.wait_ge(s, 16)

                def step(s):
                    if s.inside(nt):
                        reached(pe, s_xk, s, 1)
                        landed(pe, s_xg, s)
                        for c in range(KD):
                            ins = nc.tensor.transpose(x_ps[:, c * P:(c + 1) * P], xg[:, s.slot(4), c * P:(c + 1) * P], k["ident"][:])
                        ins.then_inc(s_xt, 1)
                    a = s.back(1)
                    if a.inside(nt):
                        e = pe.value_load(etab[0:1, ds(a.n, 1)], min_val=0, max_val=e_n - 1)
                        reached(pe, s_xk, a)
                        reached(pe, s_hid, a, 2)
                        for b in range(UB):
                            width = 2 * f // UB
                            for c in range(KD):
                                ins = nc.tensor.matmul(u_ps[a.slot(2)][b][:, 0:width], xgT[:, a.slot(2), c, :],
                                                       wup[:, c, ds(e * (2 * f) + b * width, width)],
                                                       start=c == 0, stop=c == KD - 1)
                        ins.then_inc(s_up, 1)
                    b = s.back(2)
                    if b.inside(nt):
                        reached(pe, s_hk, b, 1)
                        reached(pe, s_hid, b)
                        for c in range(FC):
                            ins = nc.tensor.transpose(h_ps[:, c * P:(c + 1) * P], hid[:, b.slot(2), c * P:(c + 1) * P], k["ident"][:])
                        ins.then_inc(s_ht, 1)
                    d = s.back(3)
                    if d.inside(nt):
                        e = pe.value_load(etab[0:1, ds(d.n, 1)], min_val=0, max_val=e_n - 1)
                        reached(pe, s_hk, d)
                        reached(pe, s_yk, d, RD)
                        for c in range(FC):
                            ins = nc.tensor.matmul(d_ps[d.slot(2)][:, 0:D], hidT[:, d.slot(2), c * P:(c + 1) * P],
                                                   wdown[:, ds(e * (FC * D) + c * D, D)], start=c == 0, stop=c == FC - 1)
                        ins.then_inc(s_dn, 1)
                pipeline(pe, nt, 4, 8, 3, step)


def join_phase(nc, sem, xs, x_dram, mo_dram, ss, b_out, xnT, w13s, w2s, posi, y_dram):
    ctx = ExitStack()
    sb = lambda n, s, d=F32: ctx.enter_context(nc.sbuf_tensor("j_" + n, s, d))
    ps = lambda n: ctx.enter_context(nc.psum_tensor("j_" + n, [P, GT], F32))
    FSC = FS // P
    with ctx:
        rs = sb("rs", [P, T])
        xr, mr, acc, part = sb("xr", [P, 2, D]), sb("mr", [P, 2, D]), sb("acc", [P, 2, D]), sb("part", [P, 2, D])
        yg = sb("yg", [P, 2, K0, D])
        idx = sb("idx", [P, 2, K0], I32)
        sil, hs = sb("sil", [P, FSC, GT]), sb("hs", [P, 2, FSC, GT])
        h1, h3 = [ps(f"h1{c}") for c in range(FSC)], [ps(f"h3{c}") for c in range(FSC)]
        d_ps = [ps("d0"), ps("d1")]
        s_v, s_std, s_rs = sem("j_moment"), sem("j_std"), sem("j_rstd")
        s_up, s_sil, s_hs, s_dn, s_dk, s_set, s_idx, s_ys, s_ch = (sem("j_" + n) for n in (
            "up", "silu", "hidden", "down", "joined", "settled", "idx", "y_summed", "chain"))
        s_in = [sem(f"j_rows{n}") for n in range(2)]
        s_yg = [sem.lasting(f"j_gathered{n}") for n in range(2)]
        with nc.Block() as block:
            @block.sync
            def _(sp):
                def step(s):
                    if s.inside(T):
                        r = s.slot(2)
                        sp.wait_ge(s_dk, s.n + 1)
                        sp.sem_inc(s_set, 1)
                        sp.dma_start(xr[:, r:r + 1, :], tokens(x_dram, s.n)).then_inc(s_in[r], 16)
                        sp.dma_start(mr[:, r:r + 1, :], tokens(mo_dram, s.n)).then_inc(s_in[r], 16)
                pipeline(sp, T, 4, 4, 0, step)

            @block.gpsimd
            def _(pool):
                def step(s):
                    if s.inside(T):
                        r = s.slot(2)
                        at = s.back(2)
                        if not isinstance(at.n, int) or at.n >= 0:
                            pool.wait_ge(s_yg[r], at.rounds(2) * 16 * K0 + 16 * K0)
                            reached(pool, s_ys, s, 2)
                            pool.sem_inc(s_set, 1)
                        nc.gpsimd.tensor_copy(idx[:, r:r + 1, :], posi[:, ds(s.n, 1), :]).then_inc(s_idx, 1)
                        reached(pool, s_idx, s)
                        pool.sem_inc(s_set, 1)
                        for q in range(K0):
                            pool.indirect_dma_start(yg[:, r, q, :], None, y_dram,
                                                    bass.IndirectOffsetOnAxis(idx[:, r, q:q + 1], 0)).then_inc(s_yg[r], 16)
                pipeline(pool, T, 4, 4, 0, step)

            @block.scalar
            def _(act):
                act.wait_ge(s_v, 1)
                nc.scalar.activation(rs[:], ss[:], ACT.Sqrt).then_inc(s_std, 1)
                with act.Fori(0, NG) as g:
                    for c in range(FSC):
                        act.wait_ge(s_up, g * FSC + c + 1)
                        act.wait_ge(s_hs, g * FSC + 1)
                        nc.scalar.activation(sil[:, c, :], h1[c][:], ACT.Silu).then_inc(s_sil, 1)

            @block.vector
            def _(dve):
                v = nc.vector
                dve.sem_inc(s_hs, 1)
                dve.sem_inc(s_dk, 2)
                v.tensor_scalar(ss[:], ss[:], 1.0 / INTER, SSD_EPS, ALU.mult, ALU.add).then_inc(s_v, 1)
                dve.wait_ge(s_std, 1)
                v.reciprocal(ss[:], rs[:]).then_inc(s_rs, 1)
                dve.wait_ge(s_rs, 1)
                with dve.Fori(0, NG // 2) as g2:
                    for gg in range(2):
                        g = g2 * 2 + gg
                        for c in range(FSC):
                            dve.wait_ge(s_sil, g * FSC + c + 1)
                            if c == 0:
                                dve.wait_ge(s_dn, g * BIG + BIG)
                            v.tensor_tensor(hs[:, gg, c, :], sil[:, c, :], h3[c][:], ALU.mult).then_inc(s_hs, 1)
                        for u in range(BIG):
                            t = g * BIG + u
                            r = u % 2
                            a, b = acc[:, r, :], part[:, r, :]
                            step_end = lambda n: dve.wait_ge(s_ch, t * 5 + n)
                            dve.wait_ge(s_in[r], (g * 2 + u // 2) * 32 + 32)
                            v.scalar_tensor_tensor(a, mr[:, r, :], ss[:, ds(t, 1)], xr[:, r, :],
                                                   ALU.mult, ALU.add).then_inc(s_ch, 1)
                            dve.wait_ge(s_yg[r], (g * 2 + u // 2) * 16 * K0 + 16 * K0)
                            v.tensor_tensor(b, yg[:, r, 0, :], yg[:, r, 1, :], ALU.add).then_inc(s_ch, 1)
                            step_end(1)
                            v.tensor_tensor(a, a, b_out[:], ALU.add).then_inc(s_ch, 1)
                            step_end(2)
                            v.tensor_tensor(b, b, yg[:, r, 2, :], ALU.add).then_inc(s_ch, 1)
                            step_end(4)
                            v.tensor_tensor(b, b, yg[:, r, 3, :], ALU.add).then_inc(s_ys, 1)
                            dve.wait_ge(s_ys, t + 1)
                            v.tensor_tensor(a, a, b, ALU.add).then_inc(s_ch, 1)
                            dve.wait_ge(s_dn, t + 1 + 2 * BIG)
                            step_end(5)
                            v.tensor_tensor(xs[:, ds(t, 1), :], acc[:, r:r + 1, :],
                                            d_ps[r][:, 0:D].unsqueeze(1), ALU.add).then_inc(s_dk, 1)

            @block.tensor
            def _(pe):
                pe.sem_inc(s_dn, 2 * BIG)
                with pe.Fori(0, NG // 2) as g2:
                    for gg in range(2):
                        g = g2 * 2 + gg
                        for c in range(FSC):
                            pe.wait_ge(s_hs, g * FSC + 1)
                            for bank, off in ((h1[c], 0), (h3[c], FS)):
                                for kd in range(KD):
                                    ins = nc.tensor.matmul(bank[:], w13s[:, kd, off + c * P:off + (c + 1) * P],
                                                           xnT[:, kd, ds(g * GT, GT)], start=kd == 0, stop=kd == KD - 1)
                            ins.then_inc(s_up, 1)
                        pe.wait_ge(s_hs, g * FSC + FSC + 1)
                        for u in range(BIG):
                            pe.wait_ge(s_dk, g * BIG + u + 1)
                            for c in range(FSC):
                                ins = nc.tensor.matmul(d_ps[u % 2][:, 0:D], hs[:, gg, c, u * P:(u + 1) * P],
                                                       w2s[:, c, :], start=c == 0, stop=c == FSC - 1)
                            ins.then_inc(s_dn, 1)


def attn_phase(nc, sem, k, xs, xnT, w_qkv, w_p, bn_g, bn_b, bp, s_weights, n_weights, posi, pay, table):
    ctx = ExitStack()
    sb = lambda n, s, d=F32: ctx.enter_context(nc.sbuf_tensor("a_" + n, s, d))
    R = 3 * KD
    SCALE = HD ** -0.5
    with ctx:
        raw = sb("raw", [P, R, S])
        stats = sb("stats", [P, R, NG, 6])
        mv = sb("mv", [P, R, 2])
        std, a_s, a_b = sb("std", [P, R]), sb("a_s", [P, R]), sb("a_b", [P, R])
        vs, vt = sb("vs", [P, 2, KD, GT]), sb("vt", [P, 2, BIG, D])
        vv, weff, mask = sb("vv", [P, KD, P]), sb("weff", [P, KD, D]), sb("mask", [P, P])
        qk, kk = vs, vt[:].rearrange("p r u d -> p r (u d)").rearrange("p r (c t) -> p r c t", c=KD)
        idx_ring, pay_ring = sb("idx_ring", [P, 2, K1], I32), sb("pay_ring", [P, 2, K1, 2], I32)
        s_copy, s_scat, s_pset = sem("a_ring_copied"), [sem.lasting(f"a_scattered{n}") for n in range(2)], sem("a_pool_settled")
        bank = [ctx.enter_context(nc.psum_tensor(f"a_bank{n}", [P, GT], F32)) for n in range(8)]
        s_pj, s_kept, s_st, s_agg, s_std, s_ch, s_coef = (sem("a_" + n) for n in (
            "projected", "raw_kept", "stats_done", "moments", "std", "chain", "coef"))
        s_v, s_vt, s_vk, s_vv, s_va, s_vm, s_we, s_wk, s_m = (sem("a_" + n) for n in (
            "v_done", "v_turned", "vt_kept", "vv_done", "vv_added", "vv_masked", "weff", "weff_kept", "mask"))
        s_q, s_qk, s_o, s_x, s_set = (sem("a_" + n) for n in ("qk_in", "qk_done", "out_done", "x_added", "settled"))
        with nc.Block() as block:
            @block.gpsimd
            def _(pool):
                nc.gpsimd.memset(mask[:], 1.0).then_inc(s_m, 1)
                m3 = mask[:].rearrange("p (h d) -> p h d", d=HD)
                for n, (op, base, sign) in enumerate(((ALU.is_ge, 0, 1), (ALU.is_ge, HD - 1, -1))):
                    pool.wait_ge(s_m, n + 1)
                    nc.gpsimd.affine_select(out=m3, in_=m3, compare_op=op, fill=0.0, base=base,
                                            pattern=[[-sign * HD, P // HD], [0, HD]], channel_multiplier=sign).then_inc(s_m, 1)
                scatter_slots(nc, pool, posi, pay, table, K1, idx_ring, pay_ring, s_copy, s_scat, s_pset)

            @block.tensor
            def _(pe):
                pe.wait_ge(s_weights, 16 * n_weights)
                pe.sem_inc(s_pj, 0 + 1)
                with pe.Fori(0, NG) as g:
                    for r in range(R):
                        pe.wait_ge(s_kept, g * R + r + 1)
                        pe.wait_ge(s_st, g * R + r + 1)
                        for c in range(KD):
                            ins = nc.tensor.matmul(bank[r % 2][:], w_qkv[:, c, r * P:(r + 1) * P],
                                                   xnT[:, c, ds(g * GT, GT)], start=c == 0, stop=c == KD - 1)
                        ins.then_inc(s_pj, 1)
                pe.wait_ge(s_kept, NG * R + 2)
                pe.wait_ge(s_st, NG * R + 2)

                def v_step(s):
                    if s.inside(NG):
                        reached(pe, s_v, s)
                        reached(pe, s_vk, s, 1)
                        for u in range(BIG):
                            for c in range(KD):
                                ins = nc.tensor.transpose(bank[u // 2][:, (u % 2) * D + c * P:(u % 2) * D + (c + 1) * P],
                                                          vs[:, s.slot(2), c, u * P:(u + 1) * P], k["ident"][:])
                        ins.then_inc(s_vt, 1)
                    a = s.back(1)
                    if a.inside(NG):
                        reached(pe, s_vk, a)
                        reached(pe, s_va, a, 1)
                        for c in range(KD):
                            for u in range(BIG):
                                x = vt[:, a.slot(2), u, c * P:(c + 1) * P]
                                ins = nc.tensor.matmul(bank[2 + c][:, 0:P], x, x, start=u == 0, stop=u == BIG - 1)
                        ins.then_inc(s_vv, 1)
                pipeline(pe, NG, 2, 4, 1, v_step)
                pe.wait_ge(s_vm, 1)
                for c in range(KD):
                    ins = nc.tensor.matmul(bank[4 + c][:, 0:D], vv[:, c, :], w_p[:, c, :], start=True, stop=True)
                ins.then_inc(s_we, 1)
                pe.wait_ge(s_wk, 1)

                def o_step(s):
                    if s.inside(NG):
                        reached(pe, s_qk, s)
                        reached(pe, s_x, s, 1)
                        for u in range(BIG):
                            for c in range(KD):
                                ins = nc.tensor.matmul(bank[u][:, 0:D], qk[:, s.slot(2), c, u * P:(u + 1) * P],
                                                       weff[:, c, :], start=c == 0, stop=c == KD - 1)
                        ins.then_inc(s_o, 1)
                pipeline(pe, NG, 2, 2, 0, o_step)

            @block.scalar
            def _(act):
                act.sem_inc(s_kept, 2)
                with act.Fori(0, NG) as g:
                    for r in range(R):
                        act.wait_ge(s_pj, g * R + r + 2)
                        act.wait_ge(s_st, g * R + r + 3)
                        act.sem_inc(s_set, 1)
                        nc.scalar.activation(raw[:, r, ds(g * GT, GT)], bank[r % 2][:], ACT.Copy).then_inc(s_kept, 1)
                act.wait_ge(s_agg, 1)
                nc.scalar.activation(std[:], mv[:, :, 1], ACT.Sqrt).then_inc(s_std, 1)
                act.wait_ge(s_coef, 1)

                def v_step(s):
                    if s.inside(NG):
                        reached(act, s_vt, s, 2)
                        act.sem_inc(s_set, 1)
                        for c in range(KD):
                            r = 2 * KD + c
                            ins = nc.scalar.activation(vs[:, s.slot(2), c, :], raw[:, r, ds(s.n * GT, GT)], ACT.Sigmoid,
                                                       bias=a_b[:, r:r + 1], scale=a_s[:, r:r + 1])
                        ins.then_inc(s_v, 1)
                pipeline(act, NG, 2, 2, 0, v_step)
                act.wait_ge(s_vt, NG)
                act.wait_ge(s_vv, NG)

                def o_step(s):
                    if s.inside(NG):
                        reached(act, s_o, s, 2)
                        reached(act, s_qk, s, 2)
                        act.sem_inc(s_set, 1)
                        for c in range(KD):
                            for dst, r in ((qk, c), (kk, KD + c)):
                                ins = nc.scalar.activation(dst[:, s.slot(2), c, :], raw[:, r, ds(s.n * GT, GT)], ACT.Sigmoid,
                                                           bias=a_b[:, r:r + 1], scale=a_s[:, r:r + 1])
                        ins.then_inc(s_q, 1)
                pipeline(act, NG, 2, 2, 0, o_step)

            @block.vector
            def _(dve):
                v = nc.vector
                dve.sem_inc(s_st, 2)
                with dve.Fori(0, NG) as g:
                    for r in range(R):
                        dve.wait_ge(s_pj, g * R + r + 2)
                        v.bn_stats(stats[:, r, ds(g, 1), :].rearrange("p a s -> p (a s)"), bank[r % 2][:]).then_inc(s_st, 1)
                dve.wait_ge(s_st, NG * R + 2)
                for r in range(R):
                    ins = v.bn_aggr(mv[:, r, :], stats[:, r].rearrange("p g s -> p (g s)"))
                link = Chain(dve, s_ch)
                link(ins)
                link(v.tensor_scalar(mv[:, :, 1], mv[:, :, 1], BN_EPS, None, ALU.add))
                dve.sem_inc(s_agg, 1)
                dve.wait_ge(s_std, 1)
                dve.wait_ge(s_weights, 16 * n_weights)
                link(v.reciprocal(std[:], std[:]))
                link(v.tensor_tensor(std[:], std[:], bn_g[:], ALU.mult))
                link(v.tensor_scalar(a_s[:], std[:], SHARP, None, ALU.mult))
                link(v.tensor_scalar(a_b[:], bn_b[:], V_TH, SHARP, ALU.subtract, ALU.mult))
                link(v.tensor_tensor(std[:], a_s[:], mv[:, :, 0], ALU.mult))
                link(v.tensor_tensor(a_b[:], a_b[:], std[:], ALU.subtract))
                dve.sem_inc(s_coef, 1)
                v.memset(vv[:], 0.0).then_inc(s_ch, 1)
                dve.wait_ge(s_ch, link.count + 1)
                v.tensor_tensor(xs[:], xs[:], middle(bp[:], T), ALU.add).then_inc(s_ch, 1)

                def v_step(s):
                    if s.inside(NG):
                        reached(dve, s_vt, s)
                        reached(dve, s_vv, s, 2)
                        for b in range(2):
                            ins = v.tensor_copy(vt[:, s.slot(2), 2 * b:2 * b + 2, :].rearrange("p u d -> p (u d)"), bank[b][:])
                        ins.then_inc(s_vk, 1)
                    a = s.back(1)
                    if a.inside(NG):
                        reached(dve, s_vv, a)
                        reached(dve, s_va, a, 1)
                        for c in range(KD):
                            ins = v.tensor_tensor(vv[:, c, :], vv[:, c, :], bank[2 + c][:, 0:P], ALU.add)
                        ins.then_inc(s_va, 1)
                pipeline(dve, NG, 2, 4, 1, v_step)
                dve.wait_ge(s_va, NG)
                dve.wait_ge(s_m, 3)
                v.scalar_tensor_tensor(vv[:], vv[:], SCALE, middle(mask[:], KD), ALU.mult, ALU.mult).then_inc(s_vm, 1)
                dve.wait_ge(s_we, 1)
                for c in range(KD):
                    ins = v.tensor_copy(weff[:, c, :], bank[4 + c][:, 0:D])
                ins.then_inc(s_wk, 1)
                dve.wait_ge(s_ch, link.count + 2)

                def o_step(s):
                    if s.inside(NG):
                        reached(dve, s_q, s)
                        v.tensor_tensor(qk[:, s.slot(2)], qk[:, s.slot(2)], kk[:, s.slot(2)], ALU.mult).then_inc(s_qk, 1)
                    a = s.back(1)
                    if a.inside(NG):
                        reached(dve, s_o, a)
                        for u in range(BIG):
                            t = a.n * BIG + u
                            ins = v.tensor_tensor(xs[:, ds(t, 1), :], xs[:, ds(t, 1), :],
                                                  bank[u][:, 0:D].unsqueeze(1), ALU.add)
                        ins.then_inc(s_x, 1)
                pipeline(dve, NG, 2, 2, 1, o_step)


def last_phase(nc, sem, xs, posi, y_dram, out):
    ctx = ExitStack()
    sb = lambda n, s, d=F32: ctx.enter_context(nc.sbuf_tensor("l_" + n, s, d))
    with ctx:
        yg = sb("yg", [P, 4, K1, D])
        idx = sb("idx", [P, 4, K1], I32)
        y, o = sb("y", [P, 4, D]), sb("o", [P, 4, D])
        s_idx, s_y, s_o, s_set = (sem("l_" + n) for n in ("idx", "y_summed", "summed", "settled"))
        s_yg = [sem.lasting(f"l_gathered{n}") for n in range(4)]
        s_st = [sem(f"l_stored{n}") for n in range(4)]
        with nc.Block() as block:
            @block.gpsimd
            def _(pool):
                def step(s):
                    r = s.slot(4)
                    at = s.back(4)
                    if not isinstance(at.n, int) or at.n >= 0:
                        pool.wait_ge(s_yg[r], at.rounds(4) * 16 * K1 + 16 * K1)
                        reached(pool, s_y, s, 4)
                        pool.sem_inc(s_set, 1)
                    nc.gpsimd.tensor_copy(idx[:, r:r + 1, :], posi[:, ds(s.n, 1), :]).then_inc(s_idx, 1)
                    reached(pool, s_idx, s)
                    pool.sem_inc(s_set, 1)
                    for q in range(K1):
                        pool.indirect_dma_start(yg[:, r, q, :], None, y_dram,
                                                bass.IndirectOffsetOnAxis(idx[:, r, q:q + 1], 0)).then_inc(s_yg[r], 16)
                pipeline(pool, T, 4, 4, 0, step)

            @block.vector
            def _(dve):
                def step(s):
                    r = s.slot(4)
                    dve.wait_ge(s_yg[r], s.rounds(4) * 16 * K1 + 16 * K1)
                    nc.vector.tensor_tensor(y[:, r, :], yg[:, r, 0, :], yg[:, r, 1, :], ALU.add).then_inc(s_y, 1)
                    landed(dve, s_st, s, 4)
                    reached(dve, s_y, s)
                    nc.vector.tensor_tensor(o[:, r:r + 1, :], y[:, r:r + 1, :], xs[:, ds(s.n, 1), :], ALU.add).then_inc(s_o, 1)
                pipeline(dve, T, 4, 4, 0, step)

            @block.sync
            def _(sp):
                def step(s):
                    reached(sp, s_o, s)
                    sp.sem_inc(s_set, 1)
                    sp.dma_start(tokens(out, s.n), o[:, s.slot(4):s.slot(4) + 1, :]).then_inc(s_st[s.slot(4)], 16)
                pipeline(sp, T, 4, 4, 0, step)
                for r in range(4):
                    sp.wait_ge(s_st[r], T // 4 * 16)


N_LOADS = 9


def program(nc, x, w_proj, b_proj, b_dt, conv_w, dt_bias, a_log, d_col, norm_col, w_out, b_out,
            w_small0, w_dt, w13, w2, w13_s, w2_s, w_qkv, w_p, bn_g, bn_b, bp, w_gate1, w12, w3, out):
    dram = lambda n, s, d=F32: nc.dram_tensor(n, s, d, kind="Internal").ap()
    rows = dram("xn_rows", (S, D))
    acum = dram("acum_rows_dram", (T, H, P))
    mo = dram("ssd_out", (S, D))
    table0, table1 = dram("table0", (NT0 * P, 2), I32), dram("table1", (NT1 * P, 2), I32)
    y0, y1 = dram("y_slots0", (NT0 * P, D)), dram("y_slots1", (NT1 * P, D))
    row = lambda ap: ap.partition_broadcast(P)

    with ExitStack() as top:
        sem = lambda n: top.enter_context(nc.semaphore(n))
        sb0 = lambda ctx: (lambda n, s, d=F32: ctx.enter_context(nc.sbuf_tensor(n, s, d)))
        k = constants(nc, top, sem)
        sb = sb0(top)
        xnT = sb("xnT", [P, KD, S])
        posi0, posi1 = sb("posi0", [P, T, K0], I32), sb("posi1", [P, T, K1], I32)
        pay0, pay1 = sb("pay0", [P, T, K0, 2], I32), sb("pay1", [P, T, K1, 2], I32)
        etab0, etab1 = sb("etab0", [1, NT0], I32), sb("etab1", [1, NT1], I32)
        b_out_sb = sb("b_out_sb", [P, D])
        ss = sb("ss", [P, T])
        s_w0, s_w1 = sem("layer0_weights"), sem("layer1_weights")

        with ExitStack() as ssd:
            sb = sb0(ssd)
            dt = sb("dt", [P, T, H])
            tabs = sb("tabs", [P, T, 4, H])
            wpj, wo = sb("wpj", [P, KD, (CH + CC) * P]), sb("wo", [P, CH, D])
            bias, conv, dcol, ncol = sb("bias", [P, CH + CC]), sb("conv", [P, CC, TAPS]), sb("dcol", [P, CH]), sb("ncol", [P, CH])
            with ExitStack() as pre:
                sb = sb0(pre)
                small = sb("small0", [P, T, SM0])
                bias_dt, alog = sb("bias_dt", [P, 2, H]), sb("alog", [P, H])
                with ExitStack() as first:
                    sb = sb0(first)
                    xs = sb("xs0", [P, T, D])
                    wsm = sb("wsm0", [P, KD, P])
                    s_sm, s_z = sem("small0_weights"), sem("small0_zeroed")
                    with nc.Block() as block:
                        @block.vector
                        def _(dve):
                            nc.vector.memset(wsm[:], 0.0).then_inc(s_z, 1)

                        @block.sync
                        def _(sp):
                            sp.wait_ge(s_z, 1)
                            sp.dma_start(wsm[:, :, 0:E0], w_small0).then_inc(s_sm, 16)
                            sp.dma_start(wsm[:, :, E0:SM0], w_dt).then_inc(s_sm, 16)
                            sp.wait_ge(s_sm, 32)
                    pairs = ((wpj, w_proj), (wo, w_out), (bias, b_proj), (conv, conv_w), (dcol, d_col), (ncol, norm_col),
                             (bias_dt[:, 0, :], row(b_dt)), (bias_dt[:, 1, :], row(dt_bias)), (alog, row(a_log)))
                    loads = [lambda sp, d=d, s=s: sp.dma_start(d if isinstance(d, bass.AP) else d[:], s).then_inc(s_w0, 16)
                             for d, s in pairs]
                    with Semaphores(nc, sem) as own:
                        norm_phase(nc, own, "n0_", k, xs, x, xnT, rows, wsm, small, SM0, loads)
                with ExitStack() as e, Semaphores(nc, sem) as own:
                    route_phase(nc, own, "r0_", k, small, E0, K0, NT0, True, posi0, pay0, etab0, table0,
                                decay_work(nc, e, own, k, small, bias_dt, alog, dt, tabs, acum, wo, ncol, s_w0))
            with Semaphores(nc, sem) as own:
                ssd_phase(nc, own, k, xnT, wpj, wo, bias, conv, dcol, dt, tabs, acum, ss, mo, posi0, pay0, table0)

        with ExitStack() as e:
            sb = sb0(e)
            wup, wdn = sb("wup0", [P, KD, E0 * 2 * F0]), sb("wdn0", [P, E0 * D])
            loads = [lambda q, c=c: q.dma_start(wup[:, c, :], w13[:, c, :]) for c in range(KD)]
            loads.append(lambda q: q.dma_start(wdn[:], w2))
            with Semaphores(nc, sem) as own:
                expert_phase(nc, own, "e0_", k, rows, table0, etab0, wup, wdn, E0, F0, NT0, y0, loads)

        xs = sb0(top)("xs", [P, T, D])
        wqkv, wp = sb0(top)("wqkv", [P, KD, 3 * D]), sb0(top)("wp", [P, KD, D])
        g_sb, b_sb, bp_sb = sb0(top)("g_sb", [P, 3 * KD]), sb0(top)("b_sb", [P, 3 * KD]), sb0(top)("bp_sb", [P, D])
        wsm1 = sb0(top)("wsm1", [P, KD, P])
        with ExitStack() as e:
            sb = sb0(e)
            w13s, w2s = sb("w13s", [P, KD, 2 * FS]), sb("w2s", [P, FS // P, D])
            s_sh, s_z1 = sem("shared_weights"), sem("small1_zeroed")
            with nc.Block() as block:
                @block.vector
                def _(dve):
                    nc.vector.memset(wsm1[:], 0.0).then_inc(s_z1, 1)

                @block.sync
                def _(sp):
                    for d, s in ((w13s, w13_s), (w2s, w2_s), (b_out_sb, row(b_out))):
                        sp.dma_start(d[:], s).then_inc(s_sh, 16)
                    sp.wait_ge(s_z1, 1)
                    for d, s in ((wqkv[:], w_qkv), (wp[:], w_p), (g_sb[:], bn_g), (b_sb[:], bn_b), (bp_sb[:], row(bp)),
                                 (wsm1[:, :, 0:E1], w_gate1)):
                        sp.dma_start(d, s).then_inc(s_w1, 16)
                    sp.wait_ge(s_sh, 48)
                    sp.wait_ge(s_w1, 96)
            with Semaphores(nc, sem) as own:
                join_phase(nc, own, xs, x, mo, ss, b_out_sb, xnT, w13s, w2s, posi0, y0)

        with ExitStack() as e:
            small = sb0(e)("small1", [P, T, E1])
            with Semaphores(nc, sem) as own:
                norm_phase(nc, own, "n1_", k, xs, None, xnT, rows, wsm1, small, E1, [])
            with Semaphores(nc, sem) as own:
                route_phase(nc, own, "r1_", k, small, E1, K1, NT1, False, posi1, pay1, etab1, table1)
        with Semaphores(nc, sem) as own:
            attn_phase(nc, own, k, xs, xnT, wqkv, wp, g_sb, b_sb, bp_sb, s_w1, 6, posi1, pay1, table1)
        with ExitStack() as e:
            sb = sb0(e)
            wup, wdn = sb("wup1", [P, KD, E1 * 2 * F1]), sb("wdn1", [P, E1 * (F1 // P) * D])
            loads = [lambda q, c=c: q.dma_start(wup[:, c, :], w12[:, c, :]) for c in range(KD)]
            loads.append(lambda q: q.dma_start(wdn[:], w3))
            with Semaphores(nc, sem) as own:
                expert_phase(nc, own, "e1_", k, rows, table1, etab1, wup, wdn, E1, F1, NT1, y1, loads)
        with Semaphores(nc, sem) as own:
            last_phase(nc, own, xs, posi1, y1, out)


def layout(i):
    a = {n: np.asarray(v) for n, v in i.items()}
    kp = lambda m: np.ascontiguousarray(m.T.reshape(-1, P, m.shape[0]).transpose(1, 0, 2))
    col = lambda v: np.ascontiguousarray(v.reshape(-1, P).T)
    big = (CH + CC) * P
    w_in, b_in = a["L0_attn_W_in"], a["L0_attn_b_in"]
    up = lambda w, v: np.concatenate([w, v], axis=1)
    w13, w12 = up(a["L0_ffn_w1_e"], a["L0_ffn_w3_e"]), up(a["L1_ffn_W1"], a["L1_ffn_W2"])
    down = lambda w: np.ascontiguousarray(
        w.transpose(0, 2, 1).reshape(w.shape[0], -1, P, D).transpose(2, 0, 1, 3).reshape(P, -1))
    return {
        "x": a["L0_attn_x"].reshape(S, D),
        "w_proj": kp(w_in[:big]), "b_proj": col(b_in[:big]), "b_dt": b_in[big:],
        "conv_w": np.ascontiguousarray(a["L0_attn_conv_w"].reshape(CC, P, TAPS).transpose(1, 0, 2)),
        "dt_bias": a["L0_attn_dt_bias"], "a_log": a["L0_attn_A_log"],
        "d_col": col(np.repeat(a["L0_attn_D"], HP)), "norm_col": col(a["L0_attn_norm_w"]),
        "w_out": kp(a["L0_attn_W_out"]), "b_out": a["L0_attn_b_out"],
        "w_small0": kp(a["L0_ffn_w_gate"]), "w_dt": kp(w_in[big:]),
        "w13": kp(w13.reshape(-1, D)), "w2": down(a["L0_ffn_w2_e"]),
        "w13_s": kp(np.concatenate([a["L0_ffn_w1_s"], a["L0_ffn_w3_s"]])), "w2_s": kp(a["L0_ffn_w2_s"]),
        "w_qkv": kp(np.concatenate([a["L1_attn_Wq"], a["L1_attn_Wk"], a["L1_attn_Wv"]])), "w_p": kp(a["L1_attn_Wp"]),
        "bn_g": col(np.concatenate([a["L1_attn_gq"], a["L1_attn_gk"], a["L1_attn_gv"]])),
        "bn_b": col(np.concatenate([a["L1_attn_bq"], a["L1_attn_bk"], a["L1_attn_bv"]])),
        "bp": a["L1_attn_bp"], "w_gate1": kp(a["L1_ffn_Wg"]),
        "w12": kp(w12.reshape(-1, D)), "w3": down(a["L1_ffn_W3"]),
    }


def kernel(**inputs):
    import concourse.bacc as bacc
    from concourse.bass_utils import run_bass_kernel_spmd

    nc = bacc.Bacc("TRN2", target_bir_lowering=False, num_devices=1)
    arrays = layout(inputs)
    args = {n: nc.dram_tensor(f"in_{n}", a.shape, mybir.dt.from_np(a.dtype), kind="ExternalInput").ap()
            for n, a in arrays.items()}
    out = nc.dram_tensor("out", (S, D), F32, kind="ExternalOutput").ap()
    program(nc, **args, out=out)
    r = run_bass_kernel_spmd(nc, [{f"in_{n}": a for n, a in arrays.items()}], core_ids=[0])
    return r.results[0]["out"].reshape(1, S, D)
```

```python
import numpy as np
import concourse.bass as bass
from concourse import mybir
from contextlib import ExitStack

F32 = mybir.dt.float32
I32 = mybir.dt.int32
ALU = mybir.AluOpType
ACT = mybir.ActivationFunctionType
AX = mybir.AxisListType
ds = bass.ds

P = 128
S, D = 4096, 256
T = S // P
KD = D // P
LN_EPS = 1e-5
BIG = 4
GT = BIG * P
NG = T // BIG

H, HP, N = 32, 64, 128
INTER = H * HP
CH = INTER // P
CC = CH + 2
TAPS = 4
TB = 2
BLK = TB * P
NB = S // BLK
NQ = 4
HQ = H // NQ
CQ = CH // NQ
GW = HQ * HP
STEPS = TB * NQ
SSD_EPS = 1e-5

E0, K0, F0, GR0, TG0 = 16, 4, 128, 4, 2
E1, K1, F1 = 8, 2, 512
PAY = 3
NT0 = S * K0 // P + E0
NT1 = S * K1 // P + E1
FS = 256
SM0 = E0 + H
N_LOADS = 7

HD = 16
BN_EPS = 1e-5
V_TH, SHARP = 1.0, 4.0


class Step:

    def __init__(self, i, k, unroll):
        self.i, self.k, self.unroll = i, k, unroll
        self.n = i * unroll + k

    def back(self, lag):
        return Step(self.i, self.k - lag, self.unroll)

    def inside(self, total):
        return not isinstance(self.n, int) or 0 <= self.n < total

    def slot(self, ring):
        return self.k % ring

    def rounds(self, ring):
        return self.i * (self.unroll // ring) + self.k // ring


def pipeline(eng, total, unroll, warm, drain, body):
    for s in range(warm):
        body(Step(s // unroll, s % unroll, unroll))
    with eng.Fori(warm // unroll, total // unroll) as i:
        for k in range(unroll):
            body(Step(i, k, unroll))
    for s in range(total, total + drain):
        body(Step(s // unroll, s % unroll, unroll))


def reached(eng, sem, step, ring=0, per=1):
    at = step.back(ring)
    if not isinstance(at.n, int) or at.n >= 0:
        eng.wait_ge(sem, at.n * per + per)


def landed(eng, sems, step, ring=0):
    at = step.back(ring)
    if not isinstance(at.n, int) or at.n >= 0:
        eng.wait_ge(sems[at.slot(len(sems))], at.rounds(len(sems)) * 16 + 16)


class Chain:

    def __init__(self, eng, sem):
        self.eng, self.sem, self.count = eng, sem, 0

    def __call__(self, ins):
        self.count += 1
        ins.then_inc(self.sem, 1)
        self.eng.wait_ge(self.sem, self.count)


def bcast(ap, n):
    return ap.unsqueeze(2).to_broadcast([ap.shape[0], ap.shape[1], n])


def middle(ap, n):
    return ap.unsqueeze(1).to_broadcast([ap.shape[0], n, ap.shape[1]])


def tokens(dram, t, n=1):
    return dram.rearrange("(t p) d -> p t d", p=P)[:, ds(t, n), :]


class Semaphores:

    def __init__(self, nc, lasting):
        self.nc, self.lasting, self.ctx, self.numbers = nc, lasting, ExitStack(), []

    def __call__(self, name):
        handle = self.ctx.enter_context(self.nc.semaphore(name))
        self.numbers.append(handle.num)
        return handle

    def __enter__(self):
        return self

    def __exit__(self, *_):
        with self.nc.Block() as block:
            @block.sync
            def _(sp):
                at = sorted(self.numbers)
                while at:
                    n = 1
                    while n < len(at) and at[n] == at[0] + n:
                        n += 1
                    sp.sem_clear(range(at[0], at[0] + n))
                    at = at[n:]
        self.ctx.close()


def constants(nc, top, sem):
    sb = lambda n, s, d=F32: top.enter_context(nc.sbuf_tensor(n, s, d))
    k = {
        "ident": sb("ident", [P, P]),
        "upto": sb("upto", [P, P]),
        "before": sb("before", [P, P]),
        "ones": sb("ones", [P, P]),
    }
    zeroed, built = sem("const_zeroed"), sem("const_built")
    with nc.Block() as block:
        @block.gpsimd
        def _(pool):
            nc.gpsimd.memset(k["ident"][:], 0.0).then_inc(zeroed, 1)
            nc.gpsimd.memset(k["upto"][:], 1.0).then_inc(zeroed, 1)
            nc.gpsimd.memset(k["before"][:], 1.0).then_inc(zeroed, 1)
            nc.gpsimd.memset(k["ones"][:], 1.0).then_inc(zeroed, 1)
            pool.wait_ge(zeroed, 4)
            for name, op, fill in (("ident", ALU.not_equal, 1.0), ("upto", ALU.is_ge, 0.0),
                                   ("before", ALU.is_gt, 0.0)):
                nc.gpsimd.affine_select(out=k[name][:], in_=k[name][:], compare_op=op, fill=fill, base=0,
                                        pattern=[[1, P]], channel_multiplier=-1).then_inc(built, 1)
            pool.wait_ge(built, 3)
    return k


def norm_phase(nc, sem, tag, k, xs, x_dram, xnT, rows, w_small, small, ns, loads, stats=None):
    ctx = ExitStack()
    sb = lambda n, s, d=F32: ctx.enter_context(nc.sbuf_tensor(tag + n, s, d))
    ps = lambda n: ctx.enter_context(nc.psum_tensor(tag + n, [P, GT], F32))
    with ctx:
        known = stats is not None
        stats = stats if known else sb("stats", [P, T, 6])
        mean, var, rstd, tmp = (sb(n, [P, T]) for n in ("mean", "var", "rstd", "tmp"))
        xn = sb("xn", [P, 4, BIG, D])
        proj = sb("proj", [P, 2, GT])
        t_ps = [[ps(f"t{r}{c}") for c in range(KD)] for r in range(2)]
        p_ps, q_ps = ps("p"), ps("q")
        s_x = [sem(f"{tag}x_loaded{n}") for n in range(4)]
        s_stats, s_small, s_std, s_rstd = (sem(tag + n) for n in ("stats_done", "moments_done", "std_done", "rstd_done"))
        s_xn, s_row = sem(tag + "xn_done"), [sem(f"{tag}rows_stored{n}") for n in range(4)]
        s_t, s_tc, s_p, s_pc, s_q, s_qc = (sem(tag + n) for n in (
            "transposed", "xnT_kept", "projected", "proj_kept", "proj_turned", "small_kept"))
        with nc.Block() as block:
            @block.sync
            def _(sp):
                if x_dram is not None:
                    for n in range(4):
                        sp.dma_start(xs[:, n * 8:n * 8 + 8, :], tokens(x_dram, n * 8, 8)).then_inc(s_x[n], 16)
                for load in loads:
                    load(sp)

                def step(s):
                    g = s.back(1)
                    if g.inside(NG):
                        reached(sp, s_xn, g)
                        sp.sem_inc(s_settled, 1)
                        sp.dma_start(tokens(rows, g.n * BIG, BIG), xn[:, g.slot(4)]).then_inc(s_row[g.slot(4)], 16)
                s_settled = sem(tag + "sp_settled")
                pipeline(sp, NG, 4, 4, 1, step)
                for r in range(4):
                    sp.wait_ge(s_row[r], NG // 4 * 16)

            @block.vector
            def _(dve):
                if not known:
                    for n in range(4):
                        dve.wait_ge(s_x[n], 16)
                        with dve.Fori(n * T // 16, (n + 1) * T // 16) as i:
                            for u in range(4):
                                one = lambda a: a[:, ds(i * 4 + u, 1), :].rearrange("p a s -> p (a s)")
                                nc.vector.bn_stats(one(stats), one(xs)).then_inc(s_stats, 1)
                    dve.wait_ge(s_stats, T)
                link = Chain(dve, s_small)
                link(nc.vector.tensor_tensor(mean[:], stats[:, :, 1], stats[:, :, 4], ALU.add))
                link(nc.vector.tensor_scalar(mean[:], mean[:], 0.5, None, ALU.mult))
                link(nc.vector.tensor_tensor(tmp[:], stats[:, :, 1], stats[:, :, 4], ALU.subtract))
                link(nc.vector.scalar_tensor_tensor(tmp[:], tmp[:], 0.25, tmp[:], ALU.mult, ALU.mult))
                link(nc.vector.tensor_tensor(var[:], stats[:, :, 2], stats[:, :, 5], ALU.add))
                link(nc.vector.scalar_tensor_tensor(var[:], var[:], 1.0 / D, tmp[:], ALU.mult, ALU.add))
                link(nc.vector.tensor_scalar(var[:], var[:], LN_EPS, None, ALU.add))
                dve.wait_ge(s_std, 1)
                nc.vector.reciprocal(rstd[:], tmp[:]).then_inc(s_rstd, 1)
                dve.wait_ge(s_rstd, 1)

                def step(s):
                    if s.inside(NG):
                        reached(dve, s_t, s, 4)
                        landed(dve, s_row, s, 4)
                        for u in range(BIG):
                            t = s.n * BIG + u
                            one = lambda a: a[:, ds(t, 1)]
                            ins = nc.vector.tensor_scalar(xn[:, s.slot(4), u, :],
                                                          xs[:, ds(t, 1), :].rearrange("p a d -> p (a d)"),
                                                          one(mean), one(rstd), ALU.subtract, ALU.mult)
                        ins.then_inc(s_xn, 1)
                    q = s.back(3)
                    if q.inside(NG):
                        reached(dve, s_q, q)
                        dve.sem_inc(s_settled, 1)
                        nc.vector.tensor_copy(small[:, ds(q.n * BIG, BIG), :],
                                              q_ps[:].rearrange("p (t c) -> p t c", t=BIG)[:, :, 0:ns]).then_inc(s_qc, 1)
                s_settled = sem(tag + "dve_settled")
                pipeline(dve, NG, 4, 4, 3, step)

            @block.scalar
            def _(act):
                act.wait_ge(s_small, 7)
                nc.scalar.activation(tmp[:], var[:], ACT.Sqrt).then_inc(s_std, 1)

                def step(s):
                    g = s.back(1)
                    if g.inside(NG):
                        reached(act, s_t, g)
                        act.sem_inc(s_settled, 1)
                        for c in range(KD):
                            ins = nc.scalar.activation(xnT[:, c, ds(g.n * GT, GT)], t_ps[g.slot(2)][c][:], ACT.Copy)
                        ins.then_inc(s_tc, 1)
                    p = s.back(2)
                    if p.inside(NG):
                        reached(act, s_q, p, 2)
                        reached(act, s_p, p)
                        nc.scalar.activation(proj[:, p.slot(2), :], p_ps[:], ACT.Copy).then_inc(s_pc, 1)
                s_settled = sem(tag + "act_settled")
                pipeline(act, NG, 2, 4, 3, step)

            @block.tensor
            def _(pe):
                def step(s):
                    if s.inside(NG):
                        reached(pe, s_tc, s, 2)
                        reached(pe, s_xn, s)
                        for u in range(BIG):
                            for c in range(KD):
                                ins = nc.tensor.transpose(t_ps[s.slot(2)][c][:, u * P:(u + 1) * P],
                                                          xn[:, s.slot(4), u, c * P:(c + 1) * P], k["ident"][:])
                        ins.then_inc(s_t, 1)
                    p = s.back(2)
                    if p.inside(NG):
                        reached(pe, s_pc, p, 1)
                        reached(pe, s_tc, p)
                        for c in range(KD):
                            ins = nc.tensor.matmul(p_ps[:], w_small[:, c, :], xnT[:, c, ds(p.n * GT, GT)],
                                                   start=c == 0, stop=c == KD - 1)
                        ins.then_inc(s_p, 1)
                    q = s.back(3)
                    if q.inside(NG):
                        reached(pe, s_qc, q, 1)
                        reached(pe, s_pc, q)
                        for u in range(BIG):
                            ins = nc.tensor.transpose(q_ps[:, u * P:(u + 1) * P],
                                                      proj[:, q.slot(2), u * P:(u + 1) * P], k["ident"][:])
                        ins.then_inc(s_q, 1)
                pipeline(pe, NG, 4, 4, 3, step)


def route_phase(nc, sem, tag, k, small, e_n, k_n, nt, groups, posi, pay, etab, table, extra=None):
    ctx = ExitStack()
    sb = lambda n, s, d=F32: ctx.enter_context(nc.sbuf_tensor(tag + n, s, d))
    ps = lambda n: ctx.enter_context(nc.psum_tensor(tag + n, [P, GT], F32))
    with ctx:
        sc, masked, sel, wgt, rank, pos, tmp = (sb(n, [P, T, e_n]) for n in (
            "sc", "masked", "sel", "wgt", "rank", "pos", "rtmp"))
        cmp = sb("cmp", [P, T, e_n, e_n])
        gs, grank, pair, gcmp = (sb(n, [P, T, GR0]) for n in ("gs", "grank", "pair", "gsel")) if groups else (None,) * 4
        gpc = sb("gcmp", [P, T, GR0, GR0]) if groups else None
        row = sb("row", [P, T])
        onesT = k["ones"][:, 0:T]
        incl = sb("incl", [P, T, e_n])
        cnt, ntf, endt, base = (sb(n, [P, e_n]) for n in ("cnt", "ntf", "endt", "base"))
        nti = sb("nti", [P, e_n], I32)
        posf = sb("posf", [P, T, k_n])
        gates = sb("gates", [P, T, k_n])
        tokid, rowid = sb("tokid", [P, T], I32), sb("rowid", [P, T, k_n], I32)
        padid = sb("padid", [P, nt], I32)
        ji, jf = sb("ji", [1, nt], I32), sb("jf", [1, nt])
        ecmp = sb("ecmp", [1, nt, e_n])
        ef = sb("ef", [1, nt])
        fill = sb("fill", [P, nt, PAY], I32)
        within, totals = ps("within"), ps("totals")
        s_sc, s_ch, s_sel, s_pre, s_e, s_ex = (sem(tag + n) for n in (
            "scores", "route_chain", "selected", "counted", "exp_in", "exp_out"))
        s_cz = sem(tag + "comparisons_zeroed")
        s_iota, s_pad, s_zero, s_zeroed = (sem(tag + n) for n in ("iotas", "pads", "filled", "table_filled"))
        W = T * e_n
        with nc.Block() as block:
            @block.scalar
            def _(act):
                if groups:
                    nc.scalar.activation(sc[:], small[:, :, 0:e_n], ACT.Sigmoid).then_inc(s_sc, 1)
                else:
                    nc.scalar.activation(sc[:], small[:, :, 0:e_n], ACT.Copy).then_inc(s_sc, 1)
                    act.wait_ge(s_e, 1)
                    nc.scalar.activation(wgt[:], tmp[:], ACT.Exp).then_inc(s_ex, 1)
                if extra:
                    extra["scalar"](act)

            @block.tensor
            def _(pe):
                pe.wait_ge(s_sel, 1)
                nc.tensor.matmul(within[:, 0:W], k["before"][:], sel[:].rearrange("p t e -> p (t e)"),
                                 start=True, stop=True)
                nc.tensor.matmul(totals[:, 0:W], k["ones"][:], sel[:].rearrange("p t e -> p (t e)"),
                                 start=True, stop=True).then_inc(s_pre, 1)
                if extra:
                    extra["tensor"](pe)

            @block.gpsimd
            def _(pool):
                for buf in (gpc, cmp) if groups else (cmp,):
                    nc.gpsimd.memset(buf[:], 0.0).then_inc(s_cz, 1)
                nc.gpsimd.iota(tokid[:], pattern=[[P, T]], base=0, channel_multiplier=1).then_inc(s_iota, 1)
                nc.gpsimd.iota(ji[:], pattern=[[1, nt]], base=0, channel_multiplier=0).then_inc(s_iota, 1)
                nc.gpsimd.iota(rowid[:], pattern=[[P * k_n, T], [1, k_n]], base=0, channel_multiplier=k_n).then_inc(s_iota, 1)
                nc.gpsimd.iota(padid[:], pattern=[[1, nt]], base=S * k_n, channel_multiplier=nt).then_inc(s_pad, 1)
                nc.gpsimd.memset(fill[:], 0).then_inc(s_pad, 1)
                pool.wait_ge(s_pad, 2)
                nc.gpsimd.tensor_copy(fill[:, :, 2], padid[:]).then_inc(s_zero, 1)
                if extra:
                    extra["gpsimd"](pool)

            @block.sync
            def _(sp):
                sp.wait_ge(s_zero, 1)
                sp.dma_start(table.rearrange("(p a) b -> p a b", p=P), fill[:]).then_inc(s_zeroed, 16)
                sp.wait_ge(s_zeroed, 16)
                if extra:
                    extra["sync"](sp)

            @block.vector
            def _(dve):
                link = Chain(dve, s_ch)
                v = nc.vector

                def ranks(dst, src, n, buf):
                    for e in range(n):
                        one = src[:, :, e:e + 1]
                        if e + 1 < n:
                            ins = v.tensor_tensor(buf[:, :, e + 1:, e], one.to_broadcast([P, T, n - 1 - e]), src[:, :, e + 1:], ALU.is_ge)
                        if e:
                            ins = v.tensor_tensor(buf[:, :, :e, e], one.to_broadcast([P, T, e]), src[:, :, :e], ALU.is_gt)
                    link(ins)
                    link(v.tensor_reduce(dst[:], buf[:], AX.X, ALU.add))

                dve.wait_ge(s_sc, 1)
                dve.wait_ge(s_cz, 1)
                if groups:
                    s4 = sc[:].rearrange("p t (g m) -> p t g m", m=E0 // GR0)
                    link(v.tensor_tensor(gs[:], s4[:, :, :, 0], s4[:, :, :, 1], ALU.add))
                    for a, b in ((0, 2), (0, 3), (1, 2), (1, 3), (2, 3)):
                        link(v.tensor_tensor(pair[:], s4[:, :, :, a], s4[:, :, :, b], ALU.add))
                        link(v.tensor_tensor(gs[:], gs[:], pair[:], ALU.max))
                    ranks(grank, gs, GR0, gpc)
                    link(v.tensor_scalar(gcmp[:], grank[:], float(TG0), None, ALU.is_lt))
                    m4 = masked[:].rearrange("p t (g m) -> p (t g) m", m=E0 // GR0)
                    allow = gcmp[:].rearrange("p t g -> p (t g)")
                    link(v.tensor_tensor(m4, sc[:].rearrange("p t (g m) -> p (t g) m", m=E0 // GR0),
                                         bcast(allow, E0 // GR0), ALU.mult))
                    link(v.tensor_scalar(gcmp[:], gcmp[:], 1.0, None, ALU.subtract))
                    link(v.tensor_tensor(m4, m4, bcast(allow, E0 // GR0), ALU.add))
                    dve.wait_ge(s_cz, 2)
                    ranks(rank, masked, e_n, cmp)
                else:
                    ranks(rank, sc, e_n, cmp)
                if extra:
                    extra["middle"](dve)
                link(v.tensor_scalar(sel[:], rank[:], float(k_n), None, ALU.is_lt))
                dve.sem_inc(s_sel, 1)
                if groups:
                    link(v.tensor_tensor(wgt[:], sc[:], sel[:], ALU.mult))
                    link(v.tensor_reduce(row[:], wgt[:], AX.X, ALU.add))
                    link(v.tensor_scalar(row[:], row[:], 1e-6, None, ALU.add))
                else:
                    link(v.tensor_reduce(row[:], sc[:], AX.X, ALU.max))
                    link(v.tensor_tensor(tmp[:], sc[:], bcast(row[:], e_n), ALU.subtract))
                    dve.sem_inc(s_e, 1)
                    dve.wait_ge(s_ex, 1)
                    link(v.tensor_tensor(wgt[:], wgt[:], sel[:], ALU.mult))
                    link(v.tensor_reduce(row[:], wgt[:], AX.X, ALU.add))
                link(v.reciprocal(row[:], row[:]))
                link(v.tensor_tensor(wgt[:], wgt[:], bcast(row[:], e_n), ALU.mult))
                dve.wait_ge(s_pre, 1)
                tot = totals[:, 0:W].rearrange("p (t e) -> p t e", e=e_n)
                for e in range(e_n):
                    ins = v.tensor_tensor_scan(incl[:, :, e], onesT, tot[:, :, e], 0.0, ALU.mult, ALU.add)
                link(ins)
                link(v.tensor_scalar(nti[:], incl[:, T - 1, :], 1.0 / P, (P - 1 - 63.5) / P, ALU.mult, ALU.add))
                link(v.tensor_copy(ntf[:], nti[:]))
                link(v.tensor_tensor_scan(endt[:], k["ones"][:, 0:e_n], ntf[:], 0.0, ALU.mult, ALU.add))
                link(v.tensor_tensor(base[:], endt[:], ntf[:], ALU.subtract))
                link(v.tensor_tensor(pos[:], incl[:], tot, ALU.subtract))
                link(v.tensor_tensor(pos[:], pos[:], within[:, 0:W].rearrange("p (t e) -> p t e", e=e_n), ALU.add))
                link(v.scalar_tensor_tensor(pos[:], middle(base[:], T), float(P), pos[:], ALU.mult, ALU.add))
                for q in range(k_n):
                    link(v.scalar_tensor_tensor(tmp[:], rank[:], float(q), pos[:], ALU.is_equal, ALU.mult))
                    link(v.tensor_reduce(posf[:, :, q], tmp[:], AX.X, ALU.add))
                    link(v.scalar_tensor_tensor(tmp[:], rank[:], float(q), wgt[:], ALU.is_equal, ALU.mult))
                    link(v.tensor_reduce(gates[:, :, q], tmp[:], AX.X, ALU.add))
                link(v.tensor_copy(posi[:], posf[:]))
                dve.wait_ge(s_iota, 3)
                link(v.tensor_copy(pay[:, :, :, 0], bcast(tokid[:], k_n)))
                link(v.tensor_copy(pay[:, :, :, 1].bitcast(F32), gates[:]))
                link(v.tensor_copy(pay[:, :, :, 2], rowid[:]))
                link(v.tensor_copy(jf[:], ji[:]))
                link(v.tensor_tensor(ecmp[:], middle(endt[0:1, :], nt), bcast(jf[:], e_n), ALU.is_le))
                link(v.tensor_reduce(ef[:], ecmp[:], AX.X, ALU.add))
                link(v.tensor_scalar(etab[:], ef[:], float(e_n - 1), None, ALU.min))
                if extra:
                    extra["vector"](dve)


def scatter_slots(nc, pool, posi, pay, table, k_n, idx_ring, pay_ring, s_copy, s_scat, s_settled):
    def step(s):
        r, at = s.slot(2), s.back(2)
        if not isinstance(at.n, int) or at.n >= 0:
            pool.wait_ge(s_scat[r], at.rounds(2) * 16 * k_n + 16 * k_n)
            pool.sem_inc(s_settled, 1)
        nc.gpsimd.tensor_copy(idx_ring[:, r:r + 1, :], posi[:, ds(s.n, 1), :])
        nc.gpsimd.tensor_copy(pay_ring[:, r:r + 1, :, :], pay[:, ds(s.n, 1), :, :]).then_inc(s_copy, 1)
        reached(pool, s_copy, s)
        pool.sem_inc(s_settled, 1)
        for q in range(k_n):
            pool.indirect_dma_start(table, bass.IndirectOffsetOnAxis(idx_ring[:, r, q:q + 1], 0),
                                    pay_ring[:, r, q, :], None).then_inc(s_scat[r], 16)
    pipeline(pool, T, 2, 2, 0, step)
    for r in range(2):
        pool.wait_ge(s_scat[r], T // 2 * k_n * 16)


def decay_work(nc, ctx, sem, k, small, bias_dt, a_log, dt, tabs, acum_dram, w_out, norm_col, s_weights, big):
    sb = lambda n, s, d=F32: ctx.enter_context(nc.sbuf_tensor(n, s, d))
    ps = lambda n: ctx.enter_context(nc.psum_tensor(n, [P, GT], F32))
    u, e, z, z2, acc = (sb(n, [P, T, H]) for n in ("dt_u", "dt_e", "dt_z", "dt_z2", "dt_acc"))
    ea = sb("exp_a", [P, H])
    rowsT = sb("acum_rows", [P, T // BIG, P])
    sum_ps = [ps(f"sum{n}") for n in range(2)]
    tot_ps = [ps(f"tot{n}") for n in range(2)]
    row_ps = [ps(f"row{n}") for n in range(2)]
    s_u, s_e, s_ch, s_adt, s_sum, s_rows, s_rowc, s_k, s_exp, s_st, s_ch2, s_den, s_rec = (sem("dt_" + n) for n in (
        "u", "exp", "chain", "adt", "sums", "rows", "rows_kept", "diff", "exps", "stored", "tabs_chain", "denominator", "reciprocal"))
    s_big = [sem(f"big_weights{n}") for n in range(len(big))]
    cols = T * H // 2
    half = lambda ap, n: ap[:, n * T // 2:(n + 1) * T // 2, :]

    def gpsimd(pool):
        v = nc.gpsimd
        link = Chain(pool, s_ch)
        pool.wait_ge(s_weights, 16 * N_LOADS)
        link(v.tensor_tensor(bias_dt[:, 0, :], bias_dt[:, 0, :], bias_dt[:, 1, :], ALU.add))
        link(v.tensor_tensor(u[:], small[:, :, E0:SM0], middle(bias_dt[:, 0, :], T), ALU.add))
        link(v.tensor_scalar(z[:], u[:], 0.0, 2.0, ALU.max, ALU.mult))
        link(v.tensor_tensor(z[:], u[:], z[:], ALU.subtract))
        pool.sem_inc(s_u, 1)
        pool.wait_ge(s_e, 2)
        link(v.tensor_scalar(z[:], e[:], 2.0, None, ALU.add))
        pool.sem_inc(s_den, 1)

    def middle_of_vector(dve):
        v = nc.vector
        link = Chain(dve, s_rec)
        dve.wait_ge(s_den, 1)
        link(v.reciprocal(z[:], z[:]))
        link(v.tensor_tensor(z[:], z[:], e[:], ALU.mult))
        link(v.tensor_tensor(z2[:], z[:], z[:], ALU.mult))
        top = 17
        link(v.tensor_scalar(acc[:], z2[:], 1.0 / top, None, ALU.mult))
        for n in range(top - 2, 1, -2):
            link(v.scalar_tensor_tensor(acc[:], acc[:], 1.0 / n, z2[:], ALU.add, ALU.mult))
        link(v.scalar_tensor_tensor(acc[:], acc[:], 1.0, z[:], ALU.add, ALU.mult))
        link(v.tensor_scalar(u[:], u[:], 0.0, None, ALU.max))
        link(v.scalar_tensor_tensor(dt[:], acc[:], 2.0, u[:], ALU.mult, ALU.add))
        link(v.scalar_tensor_tensor(u[:], dt[:], -1.0, middle(ea[:], T), ALU.mult, ALU.mult))
        dve.sem_inc(s_adt, 1)

    def vector(dve):
        v = nc.vector
        link = Chain(dve, s_ch2)
        dve.wait_ge(s_sum, 1)
        for n in range(2):
            s3 = sum_ps[n][:].rearrange("p (t h) -> p t h", h=H)
            t3 = tot_ps[n][:].rearrange("p (t h) -> p t h", h=H)
            link(v.tensor_copy(half(tabs[:, :, 0, :], n), s3))
            link(v.tensor_tensor(half(tabs[:, :, 1, :], n), t3, half(tabs[:, :, 0, :], n), ALU.subtract))
            link(v.tensor_copy(half(tabs[:, :, 2, :], n), t3))
        dve.sem_inc(s_k, 1)

    def scalar(act):
        act.wait_ge(s_weights, 16 * N_LOADS)
        act.wait_ge(s_u, 1)
        nc.scalar.activation(e[:], z[:], ACT.Exp).then_inc(s_e, 1)
        nc.scalar.activation(ea[:], a_log[:], ACT.Exp).then_inc(s_e, 1)
        for g in range(T // BIG):
            act.wait_ge(s_rows, g + 1)
            nc.scalar.activation(rowsT[:, g, :], row_ps[g % 2][:, 0:P], ACT.Copy).then_inc(s_rowc, 1)
        act.wait_ge(s_big[0], 16)
        for c in range(CH):
            nc.scalar.activation(w_out[:, c, :], w_out[:, c, :], ACT.Copy, scale=norm_col[:, c:c + 1])
        act.wait_ge(s_k, 1)
        nc.scalar.activation(tabs[:, :, 1:3, :].rearrange("p t a h -> p t (a h)"),
                             tabs[:, :, 1:3, :].rearrange("p t a h -> p t (a h)"), ACT.Exp).then_inc(s_exp, 1)

    def tensor(pe):
        pe.wait_ge(s_adt, 1)
        flat = u[:].rearrange("p t h -> p (t h)")
        for n in range(2):
            nc.tensor.matmul(sum_ps[n][:], k["upto"][:], flat[:, n * cols:(n + 1) * cols], start=True, stop=True)
            ins = nc.tensor.matmul(tot_ps[n][:], k["ones"][:], flat[:, n * cols:(n + 1) * cols], start=True, stop=True)
        ins.then_inc(s_sum, 1)
        for g in range(T // BIG):
            if g >= 2:
                pe.wait_ge(s_rowc, g - 1)
            nc.tensor.matmul(row_ps[g % 2][:, 0:P], flat[:, g * P:(g + 1) * P], k["upto"][:],
                             start=True, stop=True).then_inc(s_rows, 1)

    def sync(sp):
        for (d, s), sm in zip(big, s_big):
            sp.dma_start(d[:], s).then_inc(sm, 16)
        for sm in s_big:
            sp.wait_ge(sm, 16)
        sp.wait_ge(s_rowc, T // BIG)
        sp.dma_start(acum_dram.rearrange("(g a) h l -> (a h) g l", a=BIG), rowsT[:]).then_inc(s_st, 16)
        sp.wait_ge(s_st, 16)

    return {"gpsimd": gpsimd, "middle": middle_of_vector, "vector": vector, "scalar": scalar, "tensor": tensor, "sync": sync}


BEATS = 32


class Events:

    def __init__(self, sem, per):
        self.sem, self.per = sem, per

    def wait(self, eng, i, n):
        value = i * self.per + n
        if not isinstance(value, int) or value > 0:
            eng.wait_ge(self.sem, value)


def beats(eng, tail, body):
    def run(i, b):
        def at(lag):
            j, c = (i, b - lag) if b >= lag else (i - 1, b - lag + BEATS)
            return None if isinstance(j, int) and not 0 <= j < NB else (j, c)
        body(at)

    for b in range(BEATS):
        run(0, b)
    with eng.Fori(1, NB) as i:
        for b in range(BEATS):
            run(i, b)
    for b in range(tail):
        run(NB, b)


def ssd_phase(nc, sem, k, xnT, w_proj, w_out, bias, conv, d_col, dt, tabs, acum_dram, ss, mo_dram,
              posi, pay, table):
    ctx = ExitStack()
    sb = lambda n, s, d=F32: ctx.enter_context(nc.sbuf_tensor("m_" + n, s, d))
    with ctx:
        raw = sb("raw", [P, 2, TAPS - 1 + BLK])
        halo = sb("halo", [P, CC, TAPS - 1])
        cv = sb("cv", [P, 3, BLK])
        hT = sb("hT", [P, CC, BLK])
        cT = sb("cT", [P, BLK])
        gT = sb("gT", [P, CH, BLK])
        hdt = sb("hdt", [P, TB, INTER])
        btok = sb("btok", [P, TB, N])
        ta = sb("ta", [P, TB, H])
        tb = sb("tb", [P, TB, 2, H])
        gm = sb("gm", [P, TB, P])
        ar = sb("ar", [P, 4, HQ, P])
        er = sb("er", [P, 2, CQ, P])
        y1 = sb("y1", [P, GW])
        hdd = sb("hdd", [P, 2, GW])
        state = sb("state", [P, INTER])
        sq = sb("sq", [P, 2, CQ, P])
        sqs = sb("sqs", [P, TB, P])
        bias3 = sb("bias3", [P, CC])
        mo = sb("mo", [P, TB, D])
        idx_ring = sb("idx_ring", [P, TB, K0], I32)
        pay_ring = sb("pay_ring", [P, TB, K0, PAY], I32)
        pj = [ctx.enter_context(nc.psum_tensor(f"m_pj{n}", [P, GT], F32)) for n in range(2)]
        x_ps = [ctx.enter_context(nc.psum_tensor(f"m_x{n}", [P, GT], F32)) for n in range(2)]
        yt = [ctx.enter_context(nc.psum_tensor(f"m_yt{n}", [P, GT], F32)) for n in range(2)]
        tr, out_ps = (ctx.enter_context(nc.psum_tensor("m_" + n, [P, GT], F32)) for n in ("tr", "out"))
        ev = lambda name, per: Events(sem("m_" + name), per)

        items = [([("h", b // 2)] if b % 2 == 0 else [("h", CH + b // 2)] * (b in (1, 3)) + [("g", b // 2)])
                 for b in range(BEATS)]
        flat = [x for beat in items for x in beat]
        convs = [x for x in flat if x[0] == "h"]
        convs_at = lambda b: [(convs.index(x), x[1]) for x in items[b] if x[0] == "h"]
        TURN_G, TURN_B = 6, 10
        turns = sorted([(2 * c + 3, c) for c in range(CH)] + [(TURN_G, "G"), (TURN_B, "B")], key=lambda x: x[0])
        turn_no = {what: n for n, (_, what) in enumerate(turns)}

        def turned_at(b, late):
            return [(n, what) for n, (beat, what) in enumerate(turns) if beat == b - late]

        NTURN = len(turns)
        OLD = TAPS - 1
        projected, kept = ev("projected", len(flat)), ev("kept", len(flat))
        haloed, saved = ev("haloed", CC), ev("saved", CC)
        tapped, silued = ev("tapped", CC * OLD), ev("silued", CC)
        turned, turn_kept = ev("turned", NTURN), ev("turn_kept", NTURN)
        ta_done, tb_done, c_copied = ev("sums_copied", 1), ev("decays_copied", 1), ev("c_copied", 1)
        clipped, exped, mixed = ev("clipped", STEPS), ev("exped", STEPS), ev("mixed", STEPS)
        off, upd, diag = ev("off_done", STEPS), ev("update_done", STEPS), ev("diag_done", STEPS)
        er_exped = ev("er_exped", STEPS)
        y2d = ev("y2_done", STEPS)
        y1d, grown = ev("y1_done", STEPS), ev("state_grown", STEPS)
        hddd, aged = ev("hdd_done", STEPS), ev("state_aged", STEPS)
        y3d, gated = ev("y3_done", STEPS * CQ), ev("gated", STEPS)
        squared, summed, outd, mok = ev("squared", STEPS), ev("squares_summed", STEPS), ev("out_done", STEPS), ev("mo_kept", 1)
        ss_done, ss_kept, parted = ev("ss_done", 1), ev("ss_kept", 1), ev("part_summed", STEPS * 2 - TB)
        s_er = [sem(f"m_decay_rows_loaded{n}") for n in range(2)]
        s_ar = [sem(f"m_rows_loaded{n}") for n in range(4)]
        s_mo, s_ring = sem("m_mo_stored"), sem("m_ring_copied")
        s_scat = sem.lasting("m_scattered")
        s_bias, s_init, s_sp, s_act, s_dve, s_pool = (sem("m_" + n) for n in (
            "tap_bias", "init", "sp_settled", "act_settled", "dve_settled", "pool_settled"))
        acum_rows = acum_dram.rearrange("t h l -> t (h l)")
        acum_halves = acum_dram.rearrange("t (c n) l -> t n c l", n=2)

        LAG_ROWS, LAG_CLIP, LAG_EXP, LAG_MIX = 2, 4, 7, 9
        LAG_ER, LAG_ERX = 6, 11
        LAG_OFF, LAG_DIAG, LAG_GATE, LAG_SQ, LAG_SUM, LAG_SS, LAG_OUT = 12, 13, 15, 17, 17, 18, 19
        LAG_MO = (STEPS - 1) * 4 + 20
        LAG_TILE = LAG_MO - (STEPS - 1) * 4
        TAIL = LAG_MO - BEATS + 1

        def step_at(at, lag):
            x = at(lag)
            if x is None or x[1] % 4:
                return None
            s = x[1] // 4
            return x[0], s, s // TB, s % TB

        with nc.Block() as block:
            @block.sync
            def _(sp):
                def body(at):
                    st = step_at(at, LAG_ROWS)
                    if st:
                        i, s, q, t = st
                        diag.wait(sp, i, s - 3)
                        sp.sem_inc(s_sp, 1)
                        src = acum_rows[ds(i * TB + t, 1), q * HQ * P:(q + 1) * HQ * P]
                        sp.dma_start(ar[:, s % 4].rearrange("p h l -> p (h l)"),
                                     src.rearrange("a n -> (a n)").partition_broadcast(P)).then_inc(s_ar[s % 4], 16)
                    st = step_at(at, LAG_ER)
                    if st:
                        i, s, q, t = st
                        y1d.wait(sp, i, s - 1)
                        sp.sem_inc(s_sp, 1)
                        for n in range(2):
                            src = acum_halves[ds(i * TB + t, 1), n, q * CQ:(q + 1) * CQ, :]
                            sp.dma_start(er[n * HP:(n + 1) * HP, s % 2],
                                         src.rearrange("a c l -> (a c) l").partition_broadcast(HP)).then_inc(s_er[s % 2], 16)
                sp.sem_inc(s_mo, 16)
                beats(sp, TAIL, body)
                sp.wait_ge(s_mo, NB * 16 + 16)

            @block.gpsimd
            def _(pool):
                g = nc.gpsimd
                g.memset(halo[:], 0.0).then_inc(s_init, 1)
                g.memset(state[:], 0.0).then_inc(s_init, 1)
                pool.wait_ge(s_init, 2)

                def body(at):
                    st = step_at(at, LAG_MIX)
                    if st:
                        i, s, q, t = st
                        exped.wait(pool, i, s + 1)
                        turn_kept.wait(pool, i, turn_no["G"] + 1)
                        g.tensor_tensor(ar[:, s % 4], ar[:, s % 4], middle(gm[:, t, :], HQ), ALU.mult).then_inc(mixed.sem, 1)
                    st = step_at(at, LAG_OFF)
                    if st:
                        i, s, q, t = st
                        cols = slice(q * GW, (q + 1) * GW)
                        tb_done.wait(pool, i, 1)
                        turn_kept.wait(pool, i, turn_no[q * CQ + CQ - 1] + 1)
                        upd.wait(pool, i, s - 1)
                        g.tensor_tensor(hdd[:, s % 2].rearrange("p (h c) -> p h c", c=HP),
                                        hdt[:, t, cols].rearrange("p (h c) -> p h c", c=HP),
                                        bcast(tb[:, t, 0, q * HQ:(q + 1) * HQ], HP), ALU.mult).then_inc(hddd.sem, 1)
                        off.wait(pool, i, s + 1)
                        grown.wait(pool, i, s)
                        sv = state[:, cols].rearrange("p (h c) -> p h c", c=HP)
                        g.tensor_tensor(sv, sv, bcast(tb[:, t, 1, q * HQ:(q + 1) * HQ], HP), ALU.mult).then_inc(aged.sem, 1)
                    x = at(1)
                    if x:
                        for n, c in convs_at(x[1]):
                            kept.wait(pool, x[0], flat.index(("h", c)) + 1)
                            haloed.wait(pool, x[0], n + 1)
                            pool.sem_inc(s_pool, 1)
                            g.tensor_copy(halo[:, c, :], raw[:, n % 2, BLK:]).then_inc(saved.sem, 1)
                    x = at(0)
                    if x:
                        for n, c in convs_at(x[1]):
                            tapped.wait(pool, x[0], (n - 1) * OLD)
                            saved.wait(pool, x[0], n + 1 - CC)
                            pool.sem_inc(s_pool, 1)
                            g.tensor_copy(raw[:, n % 2, 0:TAPS - 1], halo[:, c, :]).then_inc(haloed.sem, 1)
                    st = step_at(at, LAG_SUM)
                    if st:
                        i, s, q, t = st
                        squared.wait(pool, i, s + 1)
                        pair = sq[:, s % 2, 0:CQ // 2]
                        g.tensor_tensor(pair, pair, sq[:, s % 2, CQ // 2:], ALU.add).then_inc(parted.sem, 1)
                        parted.wait(pool, i, s + 1 + max(0, s - TB))
                        if q == 0:
                            if s == 0:
                                ss_done.wait(pool, i, 0)
                            g.tensor_tensor(sqs[:, t, :], pair[:, 0], pair[:, 1], ALU.add).then_inc(summed.sem, 1)
                        else:
                            g.tensor_tensor(pair[:, 0], pair[:, 0], pair[:, 1], ALU.add).then_inc(parted.sem, 1)
                            parted.wait(pool, i, s + 2 + s - TB)
                            summed.wait(pool, i, s - 1)
                            g.tensor_tensor(sqs[:, t, :], sqs[:, t, :], pair[:, 0], ALU.add).then_inc(summed.sem, 1)
                    x = at(0)
                    if x and x[1] == 0:
                        i = x[0]
                        if not isinstance(i, int) or i:
                            pool.wait_ge(s_scat, i * (TB * K0 * 16))
                            pool.sem_inc(s_pool, 1)
                        g.tensor_copy(idx_ring[:], posi[:, ds(i * TB, TB), :]).then_inc(s_ring, 1)
                        g.tensor_copy(pay_ring[:], pay[:, ds(i * TB, TB), :, :]).then_inc(s_ring, 1)
                    if x and x[1] % 4 == 3:
                        t, q = divmod(x[1] // 4, K0)
                        if x[1] == 3:
                            pool.wait_ge(s_ring, x[0] * 2 + 2)
                            pool.sem_inc(s_pool, 1)
                        pool.indirect_dma_start(table, bass.IndirectOffsetOnAxis(idx_ring[:, t, q:q + 1], 0),
                                                pay_ring[:, t, q, :], None).then_inc(s_scat, 16)
                beats(pool, TAIL, body)
                pool.wait_ge(s_scat, NB * TB * K0 * 16)

            @block.scalar
            def _(act):
                act.wait_ge(s_bias, 1)
                def body(at):
                    st = step_at(at, LAG_EXP)
                    if st:
                        i, s, q, t = st
                        clipped.wait(act, i, s + 1)
                        a = ar[:, s % 4].rearrange("p h l -> p (h l)")
                        nc.scalar.activation(a, a, ACT.Exp).then_inc(exped.sem, 1)
                    st = step_at(at, LAG_ERX)
                    if st:
                        i, s, q, t = st
                        act.wait_ge(s_er[s % 2], (i * (STEPS // 2) + s // 2) * 32 + 32)
                        nc.scalar.activation(er[:, s % 2], er[:, s % 2], ACT.Exp).then_inc(er_exped.sem, 1)
                    st = step_at(at, LAG_SQ)
                    if st:
                        i, s, q, t = st
                        gated.wait(act, i, s + 1)
                        summed.wait(act, i, s - 1)
                        nc.scalar.activation(sq[:, s % 2], gT[:, q * CQ:(q + 1) * CQ, t * P:(t + 1) * P],
                                             ACT.Square).then_inc(squared.sem, 1)
                    st = step_at(at, LAG_SS)
                    if st and st[1] == STEPS - 1:
                        i = st[0]
                        ss_done.wait(act, i, 1)
                        act.sem_inc(s_act, 1)
                        nc.scalar.activation(ss[:, ds(i * TB, TB)], tr[:, 0:TB], ACT.Copy).then_inc(ss_kept.sem, 1)
                    st = step_at(at, LAG_TILE)
                    if st and st[1] == STEPS - 1:
                        i = st[0]
                        outd.wait(act, i, STEPS)
                        act.wait_ge(s_mo, i * 16 + 16)
                        act.sem_inc(s_act, 1)
                        nc.scalar.activation(mo[:].rearrange("p t d -> p (t d)"), out_ps[:], ACT.Copy).then_inc(mok.sem, 1)
                        mok.wait(act, i, 1)
                        act.sem_inc(s_act, 1)
                        act.dma_start(tokens(mo_dram, i * TB, TB), mo[:]).then_inc(s_mo, 16)
                    x = at(2)
                    if x:
                        i = x[0]
                        for n, c in convs_at(x[1]):
                            if c < CH:
                                y3d.wait(act, i - 1, (c // CQ + 1) * TB * CQ)
                            else:
                                turned.wait(act, i - 1, turn_no["B"] + 1)
                                c_copied.wait(act, i, 0)
                            tapped.wait(act, i, (n + 1) * OLD)
                            nc.scalar.activation(hT[:, c, :], cv[:, n % 3, :], ACT.Silu).then_inc(silued.sem, 1)
                    x = at(0)
                    if x:
                        i = x[0]
                        for kind, c in items[x[1]]:
                            m = flat.index((kind, c))
                            if kind == "h":
                                n = convs.index((kind, c))
                                tapped.wait(act, i, (n - 1) * OLD)
                                saved.wait(act, i, n - 1)
                                projected.wait(act, i, m + 1)
                                nc.scalar.activation(raw[:, n % 2, TAPS - 1:], pj[m % 2][:, 0:BLK], ACT.Identity,
                                                     bias=bias[:, CH + c:CH + c + 1])
                                silued.wait(act, i, n - 2)
                                nc.scalar.activation(cv[:, n % 3, :], pj[m % 2][:, 0:BLK], ACT.Identity,
                                                     bias=bias3[:, c:c + 1],
                                                     scale=conv[:, c, OLD:TAPS]).then_inc(kept.sem, 1)
                            else:
                                outd.wait(act, i - 1, (c // CQ + 1) * TB)
                                projected.wait(act, i, m + 1)
                                nc.scalar.activation(gT[:, c, :], pj[m % 2][:, 0:BLK], ACT.Silu,
                                                     bias=bias[:, c:c + 1]).then_inc(kept.sem, 1)
                beats(act, TAIL, body)

            @block.vector
            def _(dve):
                v = nc.vector
                v.tensor_tensor(bias3[:], bias[:, CH:CH + CC], conv[:, :, OLD], ALU.mult).then_inc(s_bias, 1)

                def body(at):
                    x = at(0)
                    if x and x[1] == 4:
                        clipped.wait(dve, x[0], 0)
                        dve.sem_inc(s_dve, 1)
                        v.tensor_copy(ta[:], tabs[:, ds(x[0] * TB, TB), 0, :]).then_inc(ta_done.sem, 1)
                    if x and x[1] == 11:
                        hddd.wait(dve, x[0], 0)
                        aged.wait(dve, x[0], 0)
                        dve.sem_inc(s_dve, 1)
                        v.tensor_copy(tb[:], tabs[:, ds(x[0] * TB, TB), 1:3, :]).then_inc(tb_done.sem, 1)
                    if x and x[1] == 10:
                        silued.wait(dve, x[0], convs.index(("h", CH + 1)) + 1)
                        off.wait(dve, x[0], 0)
                        v.tensor_copy(cT[:], hT[:, CH + 1, :]).then_inc(c_copied.sem, 1)

                    st = step_at(at, LAG_CLIP)
                    if st:
                        i, s, q, t = st
                        dve.wait_ge(s_ar[s % 4], (i * 2 + s // 4) * 16 + 16)
                        if s == 0:
                            ta_done.wait(dve, i, 1)
                        for h in range(HQ):
                            a = ar[:, s % 4, h, :]
                            ins = v.tensor_scalar(a, a, ta[:, t, q * HQ + h:q * HQ + h + 1], 0.0, ALU.subtract, ALU.min)
                        ins.then_inc(clipped.sem, 1)
                    st = step_at(at, LAG_OFF)
                    if st:
                        i, s, q, t = st
                        off.wait(dve, i, s + 1)
                        er_exped.wait(dve, i, s + 1)
                        gated.wait(dve, i, s)
                        v.tensor_tensor(y1[:], x_ps[0][:], er[:, s % 2].rearrange("p c l -> p (c l)"), ALU.mult).then_inc(y1d.sem, 1)
                        upd.wait(dve, i, s + 1)
                        aged.wait(dve, i, s + 1)
                        cols = slice(q * GW, (q + 1) * GW)
                        v.tensor_tensor(state[:, cols], state[:, cols], x_ps[1][:], ALU.add).then_inc(grown.sem, 1)
                    st = step_at(at, LAG_GATE)
                    if st:
                        i, s, q, t = st
                        diag.wait(dve, i, s + 1)
                        y1d.wait(dve, i, s + 1)
                        v.tensor_tensor(y1[:], y1[:], yt[s % 2][:], ALU.add).then_inc(y2d.sem, 1)
                        y2d.wait(dve, i, s + 1)
                        for c in range(CQ):
                            cc = q * CQ + c
                            v.scalar_tensor_tensor(y1[:, c * P:(c + 1) * P], hT[:, cc, t * P:(t + 1) * P],
                                                   d_col[:, cc:cc + 1], y1[:, c * P:(c + 1) * P],
                                                   ALU.mult, ALU.add).then_inc(y3d.sem, 1)
                        y3d.wait(dve, i, s * CQ + CQ)
                        kept.wait(dve, i, flat.index(("g", q * CQ + CQ - 1)) + 1)
                        gg = gT[:, q * CQ:(q + 1) * CQ, t * P:(t + 1) * P]
                        v.tensor_tensor(gg, gg, y1[:].rearrange("p (c l) -> p c l", l=P), ALU.mult).then_inc(gated.sem, 1)

                    for lag_block in (0, BEATS):
                        x = at(0) if not lag_block else at(BEATS)
                        if x:
                            for n, what in turned_at(x[1] + lag_block, 1):
                                i = x[0]
                                src = tr[:, 0:BLK].rearrange("p (t c) -> p t c", t=TB)
                                turned.wait(dve, i, n + 1)
                                if what == "G":
                                    mixed.wait(dve, i, 0)
                                    v.tensor_tensor(gm[:], src, middle(k["upto"][:], TB), ALU.mult).then_inc(turn_kept.sem, 1)
                                elif what == "B":
                                    upd.wait(dve, i, 0)
                                    v.tensor_copy(btok[:], src).then_inc(turn_kept.sem, 1)
                                else:
                                    diag.wait(dve, i - 1, (what // CQ + 1) * TB)
                                    hddd.wait(dve, i - 1, (what // CQ + 1) * TB)
                                    v.tensor_tensor(hdt[:, :, what * P:(what + 1) * P].rearrange("p t (h d) -> p t h d", d=HP),
                                                    src.rearrange("p t (h d) -> p t h d", d=HP),
                                                    dt[:, ds(i * TB, TB), 2 * what:2 * what + 2].unsqueeze(3)
                                                    .to_broadcast([P, TB, 2, HP]), ALU.mult).then_inc(turn_kept.sem, 1)
                    x = at(1)
                    if x:
                        i = x[0]
                        for n, c in convs_at(x[1]):
                            haloed.wait(dve, i, n + 1)
                            kept.wait(dve, i, flat.index(("h", c)) + 1)
                            r, o = raw[:, n % 2], cv[:, n % 3, :]
                            for j in range(OLD):
                                if j:
                                    tapped.wait(dve, i, n * OLD + j)
                                v.scalar_tensor_tensor(o, r[:, j:j + BLK], conv[:, c, j:j + 1], o,
                                                       ALU.mult, ALU.add).then_inc(tapped.sem, 1)
                beats(dve, TAIL, body)

            @block.tensor
            def _(pe):
                mm = nc.tensor.matmul

                def body(at):
                    st = step_at(at, LAG_OFF)
                    if st:
                        i, s, q, t = st
                        grown.wait(pe, i, s)
                        y1d.wait(pe, i, s)
                        c_copied.wait(pe, i, 1)
                        for c in range(CQ):
                            at_c = slice(q * GW + c * P, q * GW + (c + 1) * P)
                            ins = mm(x_ps[0][:, c * P:(c + 1) * P], state[:, at_c], cT[:, t * P:(t + 1) * P], start=True, stop=True)
                        ins.then_inc(off.sem, 1)
                        hddd.wait(pe, i, s + 1)
                        turn_kept.wait(pe, i, turn_no["B"] + 1)
                        mm(x_ps[1][:], btok[:, t, :], hdd[:, s % 2], start=True, stop=True).then_inc(upd.sem, 1)
                    st = step_at(at, LAG_DIAG)
                    if st:
                        i, s, q, t = st
                        y2d.wait(pe, i, s - 1)
                        mixed.wait(pe, i, s + 1)
                        for h in range(HQ):
                            hc, c = (q * HQ + h) * HP, h // 2
                            half = slice(h % 2 * HP, (h % 2 + 1) * HP)
                            ins = mm(yt[s % 2][half, c * P:(c + 1) * P], hdt[:, t, hc:hc + HP], ar[:, s % 4, h, :],
                                     start=True, stop=True)
                        ins.then_inc(diag.sem, 1)
                    st = step_at(at, LAG_OUT)
                    if st:
                        i, s, q, t = st
                        gated.wait(pe, i, s + 1)
                        if s == 0:
                            mok.wait(pe, i, 0)
                        for c in range(CQ):
                            cc = q * CQ + c
                            ins = mm(out_ps[:, t * D:(t + 1) * D], gT[:, cc, t * P:(t + 1) * P], w_out[:, cc, :],
                                     start=s == 0 and c == 0, stop=cc == CH - 1, skip_group_check=True)
                        ins.then_inc(outd.sem, 1)
                    st = step_at(at, LAG_SS)
                    if st and st[1] == STEPS - 1:
                        i = st[0]
                        if isinstance(i, int) and i == NB - 1:
                            turn_kept.wait(pe, i, NTURN)
                        else:
                            turn_kept.wait(pe, i + 1, len([b for b, _ in turns if b < (STEPS - 1) * 4 + LAG_SS - BEATS]))
                        summed.wait(pe, i, STEPS)
                        for t in range(TB):
                            ins = mm(tr[:, t:t + 1], sqs[:, t, :], k["ones"][:, 0:1], start=True, stop=True)
                        ins.then_inc(ss_done.sem, 1)

                    for lag_block in (0, BEATS):
                        x = at(0) if not lag_block else at(BEATS)
                        if x:
                            for n, what in turned_at(x[1] + lag_block, 0):
                                i = x[0]
                                turn_kept.wait(pe, i, n)
                                if turns[n][0] > (STEPS - 1) * 4 + LAG_SS - BEATS:
                                    ss_kept.wait(pe, i, 0)
                                chunk = {"G": CH + 1, "B": CH}.get(what, what)
                                silued.wait(pe, i, convs.index(("h", chunk)) + 1)
                                for t in range(TB):
                                    rows = slice(t * P, (t + 1) * P)
                                    if what == "G":
                                        ins = mm(tr[:, rows], hT[:, CH, rows], hT[:, CH + 1, rows], start=True, stop=True)
                                    else:
                                        ins = nc.tensor.transpose(tr[:, rows], hT[:, chunk, rows], k["ident"][:])
                                ins.then_inc(turned.sem, 1)
                    x = at(0)
                    if x:
                        i = x[0]
                        for kind, c in items[x[1]]:
                            m = flat.index((kind, c))
                            kept.wait(pe, i, m - 1)
                            col = ((CH if kind == "h" else 0) + c) * P
                            for kd in range(KD):
                                ins = mm(pj[m % 2][:, 0:BLK], w_proj[:, kd, col:col + P], xnT[:, kd, ds(i * BLK, BLK)],
                                         start=kd == 0, stop=kd == KD - 1)
                            ins.then_inc(projected.sem, 1)
                beats(pe, TAIL, body)


def expert_loads(wup, up, wdn, down, nu, nd):
    def load(q, e, s):
        q.dma_start(wup[:, :, e * nu:(e + 1) * nu], up[:, :, e * nu:(e + 1) * nu]).then_inc(s, 16)
        q.dma_start(wdn[:, e * nd:(e + 1) * nd], down[:, e * nd:(e + 1) * nd]).then_inc(s, 16)
    return load


def expert_phase(nc, sem, tag, k, rows, table, etab, wup, wdown, e_n, f, nt, y_dram, load):
    ctx = ExitStack()
    sb = lambda n, s, d=F32: ctx.enter_context(nc.sbuf_tensor(tag + n, s, d))
    ps = lambda n, w=GT: ctx.enter_context(nc.psum_tensor(tag + n, [P, w], F32))
    FC = f // P
    UB = max(1, 2 * f // GT)
    with ctx:
        U, AHEAD = 12, 4
        tab = sb("tab", [P, nt, PAY], I32)
        ring = sb("ring", [P, U, PAY], I32)
        xg = sb("xg", [P, 6, D])
        xgT = sb("xgT", [P, 2, KD, P])
        sil = sb("sil", [P, 2, f])
        hid = sb("hid", [P, 2, f])
        hidT = sb("hidT", [P, 2, f])
        y = sb("y", [P, 4, D])
        x_ps = ps("x_ps")
        u_ps = [[ps(f"u{r}{b}") for b in range(UB)] for r in range(2)]
        h_ps = ps("h_ps")
        d_ps = [ps("d0"), ps("d1")] if UB == 1 else [ps("d0")] * 2
        RD = 2 if UB == 1 else 1
        s_w = sem(f"{tag}weights")
        s_tab, s_rest, s_ring = sem(f"{tag}first_entries"), sem(f"{tag}entries"), sem(f"{tag}ring_copied")
        s_xg = [sem.lasting(f"{tag}gathered{n}") for n in range(6)]
        s_y = [sem.lasting(f"{tag}y_scattered{n}") for n in range(4)]
        s_xt, s_xk, s_up, s_sil, s_hid, s_ht, s_hk, s_dn, s_yk, s_set = (sem(tag + n) for n in (
            "x_turned", "x_kept", "up_done", "silu_done", "hidden", "hidden_turned", "hidden_kept",
            "down_done", "y_kept", "settled"))
        with nc.Block() as block:
            @block.sync
            def _(sp):
                entries = table.rearrange("(t p) b -> p t b", p=P)
                sp.dma_start(tab[:, 0:U, :], entries[:, 0:U, :]).then_inc(s_tab, 16)
                for n in range(e_n):
                    if n:
                        sp.wait_ge(s_w, 32 * n)
                    load(sp, n, s_w)
                    if n == 0:
                        for t in range(U, nt, U):
                            sp.dma_start(tab[:, t:t + U, :], entries[:, t:t + U, :]).then_inc(s_rest, 16)
                sp.wait_ge(s_w, 32 * e_n)

            @block.gpsimd
            def _(pool):
                def step(s):
                    if s.inside(nt):
                        r = s.slot(U)
                        if not isinstance(s.i, int) and s.k == 0:
                            pool.wait_ge(s_rest, (nt // U - 1) * 16)
                        elif isinstance(s.i, int) and s.n == 0:
                            pool.wait_ge(s_tab, 16)
                        landed(pool, s_y, s, U)
                        pool.sem_inc(s_set, 1)
                        nc.gpsimd.tensor_copy(ring[:, r:r + 1, :], tab[:, ds(s.n, 1), :]).then_inc(s_ring, 1)
                        reached(pool, s_ring, s)
                        reached(pool, s_xt, s, 6)
                        landed(pool, s_xg, s, 6)
                        pool.sem_inc(s_set, 1)
                        pool.indirect_dma_start(xg[:, s.slot(6), :], None, rows,
                                                bass.IndirectOffsetOnAxis(ring[:, r, 0:1], 0)).then_inc(s_xg[s.slot(6)], 16)
                    o = s.back(3 + AHEAD)
                    if o.inside(nt):
                        reached(pool, s_yk, o)
                        pool.sem_inc(s_set, 1)
                        pool.indirect_dma_start(y_dram, bass.IndirectOffsetOnAxis(ring[:, o.slot(U), 2:3], 0),
                                                y[:, o.slot(4), :], None).then_inc(s_y[o.slot(4)], 16)
                pipeline(pool, nt, U, U, 3 + AHEAD, step)
                for r in range(4):
                    pool.wait_ge(s_y[r], nt // 4 * 16)

            @block.scalar
            def _(act):
                def step(s):
                    a = s.back(1)
                    if a.inside(nt):
                        reached(act, s_up, a)
                        reached(act, s_hid, a, 2)
                        nc.scalar.activation(sil[:, a.slot(2), :], u_ps[a.slot(2)][0][:, 0:f], ACT.Silu).then_inc(s_sil, 1)
                    b = s.back(2)
                    if b.inside(nt):
                        reached(act, s_ht, b)
                        reached(act, s_dn, b, 2)
                        nc.scalar.activation(hidT[:, b.slot(2), :], h_ps[:, 0:f], ACT.Copy).then_inc(s_hk, 1)
                pipeline(act, nt, U, U, 3, step)

            @block.vector
            def _(dve):
                v = nc.vector

                def step(s):
                    if s.inside(nt):
                        reached(dve, s_xt, s)
                        reached(dve, s_up, s, 2)
                        v.tensor_copy(xgT[:, s.slot(2)].rearrange("p c t -> p (c t)"), x_ps[:, 0:D]).then_inc(s_xk, 1)
                    a = s.back(1)
                    if a.inside(nt):
                        reached(dve, s_sil, a)
                        reached(dve, s_ht, a, 2)
                        second = u_ps[a.slot(2)][UB - 1][:, f * (2 - UB):f * (3 - UB)] if UB == 1 else u_ps[a.slot(2)][1][:, 0:f]
                        v.scalar_tensor_tensor(hid[:, a.slot(2), :], sil[:, a.slot(2), :],
                                               ring[:, a.slot(U), 1:2].bitcast(F32), second,
                                               ALU.mult, ALU.mult).then_inc(s_hid, 1)
                    c = s.back(3)
                    if c.inside(nt):
                        reached(dve, s_dn, c)
                        landed(dve, s_y, c, 4)
                        v.tensor_copy(y[:, c.slot(4), :], d_ps[c.slot(2)][:, 0:D]).then_inc(s_yk, 1)
                pipeline(dve, nt, U, U, 3, step)

            @block.tensor
            def _(pe):
                held = {}

                def expert(s):
                    key = (id(s.i), s.k) if s.k >= 0 else None
                    if key is None or key not in held:
                        held[key] = pe.value_load(etab[0:1, ds(s.n, 1)], min_val=0, max_val=e_n - 1)
                    return held[key]

                def step(s):
                    if s.inside(nt):
                        reached(pe, s_xk, s, 1)
                        landed(pe, s_xg, s)
                        for c in range(KD):
                            ins = nc.tensor.transpose(x_ps[:, c * P:(c + 1) * P], xg[:, s.slot(6), c * P:(c + 1) * P], k["ident"][:])
                        ins.then_inc(s_xt, 1)
                    a = s.back(1)
                    if a.inside(nt):
                        e = expert(a)
                        pe.wait_ge(s_w, e * 32 + 32)
                        reached(pe, s_xk, a)
                        reached(pe, s_hid, a, 2)
                        for b in range(UB):
                            width = 2 * f // UB
                            for c in range(KD):
                                ins = nc.tensor.matmul(u_ps[a.slot(2)][b][:, 0:width], xgT[:, a.slot(2), c, :],
                                                       wup[:, c, ds(e * (2 * f) + b * width, width)],
                                                       start=c == 0, stop=c == KD - 1)
                        ins.then_inc(s_up, 1)
                    b = s.back(2)
                    if b.inside(nt):
                        reached(pe, s_hk, b, 1)
                        reached(pe, s_hid, b)
                        for c in range(FC):
                            ins = nc.tensor.transpose(h_ps[:, c * P:(c + 1) * P], hid[:, b.slot(2), c * P:(c + 1) * P], k["ident"][:])
                        ins.then_inc(s_ht, 1)
                    d = s.back(3)
                    if d.inside(nt):
                        e = expert(d)
                        reached(pe, s_hk, d)
                        reached(pe, s_yk, d, RD)
                        for c in range(FC):
                            ins = nc.tensor.matmul(d_ps[d.slot(2)][:, 0:D], hidT[:, d.slot(2), c * P:(c + 1) * P],
                                                   wdown[:, ds(e * (FC * D) + c * D, D)], start=c == 0, stop=c == FC - 1)
                        ins.then_inc(s_dn, 1)
                pipeline(pe, nt, U, U, 3, step)


def join_phase(nc, sem, xs, x_dram, mo_dram, ss, b_out, xnT, w13s, w2s, y_dram, stats):
    ctx = ExitStack()
    sb = lambda n, s, d=F32: ctx.enter_context(nc.sbuf_tensor("j_" + n, s, d))
    ps = lambda n: ctx.enter_context(nc.psum_tensor("j_" + n, [P, GT], F32))
    FSC = FS // P
    by_token = y_dram[0:S * K0, :].rearrange("(s k) d -> s (k d)", k=K0)
    with ctx:
        rs = sb("rs", [P, T])
        xr, mr, acc, part = sb("xr", [P, BIG, D]), sb("mr", [P, BIG, D]), sb("acc", [P, 2, D]), sb("part", [P, 2, D])
        yg = sb("yg", [P, BIG, K0, D])
        sil, hs = sb("sil", [P, FSC, GT]), sb("hs", [P, 2, FSC, GT])
        h1, h3 = [ps(f"h1{c}") for c in range(FSC)], [ps(f"h3{c}") for c in range(FSC)]
        d_ps = [ps(f"d{n}") for n in range(BIG)]
        s_v, s_std, s_rs = sem("j_moment"), sem("j_std"), sem("j_rstd")
        s_up, s_sil, s_hs, s_dn, s_dk, s_set, s_ys, s_ch, s_pc = (sem("j_" + n) for n in (
            "up", "silu", "hidden", "down", "joined", "settled", "y_summed", "chain", "part_chain"))
        s_in = [sem(f"j_rows{n}") for n in range(BIG)]
        s_yg = [sem(f"j_experts{n}") for n in range(BIG)]
        with nc.Block() as block:
            @block.sync
            def _(sp):
                def step(s):
                    if s.inside(T):
                        r = s.slot(BIG)
                        sp.wait_ge(s_dk, s.n + 1)
                        sp.sem_inc(s_set, 1)
                        sp.dma_start(xr[:, r:r + 1, :], tokens(x_dram, s.n)).then_inc(s_in[r], 16)
                        sp.dma_start(mr[:, r:r + 1, :], tokens(mo_dram, s.n)).then_inc(s_in[r], 16)
                        sp.dma_start(yg[:, r:r + 1].rearrange("p t k d -> p t (k d)"),
                                     tokens(by_token, s.n)).then_inc(s_yg[r], 16)
                pipeline(sp, T, 4, 4, 0, step)

            @block.gpsimd
            def _(pool):
                pool.sem_inc(s_ys, 2)
                with pool.Fori(0, NG) as g:
                    for u in range(BIG):
                        b, t = part[:, u % 2, :], g * BIG + u
                        pool.wait_ge(s_dk, t + BIG - 1)
                        pool.wait_ge(s_yg[u], g * 16 + 16)
                        nc.gpsimd.tensor_tensor(b, yg[:, u, 0, :], yg[:, u, 1, :], ALU.add).then_inc(s_pc, 1)
                        pool.wait_ge(s_pc, t * 2 + 1)
                        nc.gpsimd.tensor_tensor(b, b, yg[:, u, 2, :], ALU.add).then_inc(s_pc, 1)
                        pool.wait_ge(s_pc, t * 2 + 2)
                        nc.gpsimd.tensor_tensor(b, b, yg[:, u, 3, :], ALU.add).then_inc(s_ys, 1)

            @block.scalar
            def _(act):
                act.wait_ge(s_v, 1)
                nc.scalar.activation(rs[:], ss[:], ACT.Sqrt).then_inc(s_std, 1)
                with act.Fori(0, NG) as g:
                    for c in range(FSC):
                        act.wait_ge(s_up, g * FSC + c + 1)
                        act.wait_ge(s_hs, g * FSC + 1)
                        nc.scalar.activation(sil[:, c, :], h1[c][:], ACT.Silu).then_inc(s_sil, 1)

            @block.vector
            def _(dve):
                v = nc.vector
                dve.sem_inc(s_hs, 1)
                dve.sem_inc(s_dk, BIG)
                v.tensor_scalar(ss[:], ss[:], 1.0 / INTER, SSD_EPS, ALU.mult, ALU.add).then_inc(s_v, 1)
                dve.wait_ge(s_std, 1)
                v.reciprocal(ss[:], rs[:]).then_inc(s_rs, 1)
                dve.wait_ge(s_rs, 1)
                with dve.Fori(0, NG // 2) as g2:
                    for gg in range(2):
                        g = g2 * 2 + gg
                        for c in range(FSC):
                            dve.wait_ge(s_sil, g * FSC + c + 1)
                            if c == 0:
                                dve.wait_ge(s_dn, g * BIG + BIG)
                            v.tensor_tensor(hs[:, gg, c, :], sil[:, c, :], h3[c][:], ALU.mult).then_inc(s_hs, 1)
                        for u in range(BIG):
                            t = g * BIG + u
                            r = u % 2
                            a, b = acc[:, r, :], part[:, r, :]
                            step_end = lambda n: dve.wait_ge(s_ch, t * 3 + n)
                            dve.wait_ge(s_in[u], g * 32 + 32)
                            v.scalar_tensor_tensor(a, mr[:, u, :], ss[:, ds(t, 1)], xr[:, u, :],
                                                   ALU.mult, ALU.add).then_inc(s_ch, 1)
                            step_end(1)
                            v.tensor_tensor(a, a, b_out[:], ALU.add).then_inc(s_ch, 1)
                            dve.wait_ge(s_ys, t + 3)
                            step_end(2)
                            v.tensor_tensor(a, a, b, ALU.add).then_inc(s_ch, 1)
                            dve.wait_ge(s_dn, t + 1 + 2 * BIG)
                            step_end(3)
                            v.tensor_tensor(xs[:, ds(t, 1), :], acc[:, r:r + 1, :],
                                            d_ps[u][:, 0:D].unsqueeze(1), ALU.add).then_inc(s_dk, 1)
                            dve.wait_ge(s_dk, t + 1 + BIG)
                            v.bn_stats(stats[:, ds(t, 1), :].rearrange("p a s -> p (a s)"),
                                       xs[:, ds(t, 1), :].rearrange("p a d -> p (a d)"))

            @block.tensor
            def _(pe):
                pe.sem_inc(s_dn, 2 * BIG)

                def up(g):
                    for c in range(FSC):
                        pe.wait_ge(s_hs, g * FSC + 1)
                        for bank, off in ((h1[c], 0), (h3[c], FS)):
                            for kd in range(KD):
                                ins = nc.tensor.matmul(bank[:], w13s[:, kd, off + c * P:off + (c + 1) * P],
                                                       xnT[:, kd, ds(g * GT, GT)], start=kd == 0, stop=kd == KD - 1)
                        ins.then_inc(s_up, 1)

                def down(g, gg):
                    pe.wait_ge(s_hs, g * FSC + FSC + 1)
                    for u in range(BIG):
                        pe.wait_ge(s_dk, g * BIG + u + 1)
                        for c in range(FSC):
                            ins = nc.tensor.matmul(d_ps[u][:, 0:D], hs[:, gg, c, u * P:(u + 1) * P],
                                                   w2s[:, c, :], start=c == 0, stop=c == FSC - 1)
                        ins.then_inc(s_dn, 1)

                up(0)
                with pe.Fori(0, NG // 2 - 1) as g2:
                    for gg in range(2):
                        down(g2 * 2 + gg, gg)
                        up(g2 * 2 + gg + 1)
                down(NG - 2, 0)
                up(NG - 1)
                down(NG - 1, 1)


def attn_phase(nc, sem, k, xs, xnT, w_qkv, w_p, bn_g, bn_b, bp, s_weights, n_weights, posi, pay, table):
    ctx = ExitStack()
    sb = lambda n, s, d=F32: ctx.enter_context(nc.sbuf_tensor("a_" + n, s, d))
    R = 3 * KD
    SCALE = HD ** -0.5
    with ctx:
        raw = sb("raw", [P, R, S])
        stats = sb("stats", [P, R, NG, 6])
        mv = sb("mv", [P, R, 2])
        std, a_s, a_b = sb("std", [P, R]), sb("a_s", [P, R]), sb("a_b", [P, R])
        vs, vt = sb("vs", [P, 2, KD, GT]), sb("vt", [P, 2, BIG, D])
        vv, weff, mask = sb("vv", [P, KD, P]), sb("weff", [P, KD, D]), sb("mask", [P, P])
        qk, kk = vs, vt[:].rearrange("p r u d -> p r (u d)").rearrange("p r (c t) -> p r c t", c=KD)
        idx_ring, pay_ring = sb("idx_ring", [P, 2, K1], I32), sb("pay_ring", [P, 2, K1, PAY], I32)
        s_copy, s_scat, s_pset = sem("a_ring_copied"), [sem.lasting(f"a_scattered{n}") for n in range(2)], sem("a_pool_settled")
        bank = [ctx.enter_context(nc.psum_tensor(f"a_bank{n}", [P, GT], F32)) for n in range(8)]
        s_pj, s_kept, s_st, s_agg, s_std, s_ch, s_coef = (sem("a_" + n) for n in (
            "projected", "raw_kept", "stats_done", "moments", "std", "chain", "coef"))
        s_v, s_vt, s_vk, s_vv, s_va, s_vm, s_we, s_wk, s_m = (sem("a_" + n) for n in (
            "v_done", "v_turned", "vt_kept", "vv_done", "vv_added", "vv_masked", "weff", "weff_kept", "mask"))
        s_bp = sem("a_bias_added")
        s_q, s_qk, s_o, s_x, s_set = (sem("a_" + n) for n in ("qk_in", "qk_done", "out_done", "x_added", "settled"))
        with nc.Block() as block:
            @block.gpsimd
            def _(pool):
                nc.gpsimd.memset(mask[:], 1.0).then_inc(s_m, 1)
                m3 = mask[:].rearrange("p (h d) -> p h d", d=HD)
                for n, (op, base, sign) in enumerate(((ALU.is_ge, 0, 1), (ALU.is_ge, HD - 1, -1))):
                    pool.wait_ge(s_m, n + 1)
                    nc.gpsimd.affine_select(out=m3, in_=m3, compare_op=op, fill=0.0, base=base,
                                            pattern=[[-sign * HD, P // HD], [0, HD]], channel_multiplier=sign).then_inc(s_m, 1)
                pool.wait_ge(s_weights, 16 * n_weights)
                nc.gpsimd.tensor_tensor(xs[:], xs[:], middle(bp[:], T), ALU.add).then_inc(s_bp, 1)
                scatter_slots(nc, pool, posi, pay, table, K1, idx_ring, pay_ring, s_copy, s_scat, s_pset)

            @block.tensor
            def _(pe):
                pe.wait_ge(s_weights, 16 * n_weights)
                pe.sem_inc(s_pj, 1)
                with pe.Fori(0, NG) as g:
                    for r in range(R):
                        pe.wait_ge(s_kept, g * R + r + 1)
                        pe.wait_ge(s_st, g * R + r + 1)
                        for c in range(KD):
                            ins = nc.tensor.matmul(bank[r % 2][:], w_qkv[:, c, r * P:(r + 1) * P],
                                                   xnT[:, c, ds(g * GT, GT)], start=c == 0, stop=c == KD - 1)
                        ins.then_inc(s_pj, 1)
                pe.wait_ge(s_kept, NG * R + 2)
                pe.wait_ge(s_st, NG * R + 2)

                def v_step(s):
                    if s.inside(NG):
                        reached(pe, s_v, s)
                        reached(pe, s_vk, s, 1)
                        for u in range(BIG):
                            for c in range(KD):
                                ins = nc.tensor.transpose(bank[u // 2][:, (u % 2) * D + c * P:(u % 2) * D + (c + 1) * P],
                                                          vs[:, s.slot(2), c, u * P:(u + 1) * P], k["ident"][:])
                        ins.then_inc(s_vt, 1)
                    a = s.back(1)
                    if a.inside(NG):
                        reached(pe, s_vk, a)
                        reached(pe, s_va, a, 1)
                        for c in range(KD):
                            for u in range(BIG):
                                x = vt[:, a.slot(2), u, c * P:(c + 1) * P]
                                ins = nc.tensor.matmul(bank[2 + c][:, 0:P], x, x, start=u == 0, stop=u == BIG - 1)
                        ins.then_inc(s_vv, 1)
                pipeline(pe, NG, 2, 4, 1, v_step)
                pe.wait_ge(s_vm, 1)
                for c in range(KD):
                    ins = nc.tensor.matmul(bank[4 + c][:, 0:D], vv[:, c, :], w_p[:, c, :], start=True, stop=True)
                ins.then_inc(s_we, 1)
                pe.wait_ge(s_wk, 1)

                def o_step(s):
                    if s.inside(NG):
                        reached(pe, s_qk, s)
                        reached(pe, s_x, s, 2)
                        for u in range(BIG):
                            for c in range(KD):
                                ins = nc.tensor.matmul(bank[s.slot(2) * BIG + u][:, 0:D], qk[:, s.slot(2), c, u * P:(u + 1) * P],
                                                       weff[:, c, :], start=c == 0, stop=c == KD - 1)
                        ins.then_inc(s_o, 1)
                pipeline(pe, NG, 2, 2, 0, o_step)

            @block.scalar
            def _(act):
                act.sem_inc(s_kept, 2)
                with act.Fori(0, NG) as g:
                    for r in range(R):
                        act.wait_ge(s_pj, g * R + r + 2)
                        act.wait_ge(s_st, g * R + r + 3)
                        act.sem_inc(s_set, 1)
                        nc.scalar.activation(raw[:, r, ds(g * GT, GT)], bank[r % 2][:], ACT.Copy).then_inc(s_kept, 1)
                act.wait_ge(s_agg, 1)
                nc.scalar.activation(std[:], mv[:, :, 1], ACT.Sqrt).then_inc(s_std, 1)
                act.wait_ge(s_coef, 1)

                def v_step(s):
                    if s.inside(NG):
                        reached(act, s_vt, s, 2)
                        act.sem_inc(s_set, 1)
                        for c in range(KD):
                            r = 2 * KD + c
                            ins = nc.scalar.activation(vs[:, s.slot(2), c, :], raw[:, r, ds(s.n * GT, GT)], ACT.Sigmoid,
                                                       bias=a_b[:, r:r + 1], scale=a_s[:, r:r + 1])
                        ins.then_inc(s_v, 1)
                pipeline(act, NG, 2, 2, 0, v_step)
                act.wait_ge(s_vt, NG)
                act.wait_ge(s_vv, NG)

                def o_step(s):
                    if s.inside(NG):
                        reached(act, s_o, s, 2)
                        reached(act, s_qk, s, 2)
                        act.sem_inc(s_set, 1)
                        for c in range(KD):
                            for dst, r in ((qk, c), (kk, KD + c)):
                                ins = nc.scalar.activation(dst[:, s.slot(2), c, :], raw[:, r, ds(s.n * GT, GT)], ACT.Sigmoid,
                                                           bias=a_b[:, r:r + 1], scale=a_s[:, r:r + 1])
                        ins.then_inc(s_q, 1)
                pipeline(act, NG, 2, 2, 0, o_step)

            @block.vector
            def _(dve):
                v = nc.vector
                dve.sem_inc(s_st, 2)
                with dve.Fori(0, NG) as g:
                    for r in range(R):
                        dve.wait_ge(s_pj, g * R + r + 2)
                        v.bn_stats(stats[:, r, ds(g, 1), :].rearrange("p a s -> p (a s)"), bank[r % 2][:]).then_inc(s_st, 1)
                dve.wait_ge(s_st, NG * R + 2)
                for r in range(R):
                    ins = v.bn_aggr(mv[:, r, :], stats[:, r].rearrange("p g s -> p (g s)"))
                link = Chain(dve, s_ch)
                link(ins)
                link(v.tensor_scalar(mv[:, :, 1], mv[:, :, 1], BN_EPS, None, ALU.add))
                dve.sem_inc(s_agg, 1)
                dve.wait_ge(s_std, 1)
                dve.wait_ge(s_weights, 16 * n_weights)
                link(v.reciprocal(std[:], std[:]))
                link(v.tensor_tensor(std[:], std[:], bn_g[:], ALU.mult))
                link(v.tensor_scalar(a_s[:], std[:], SHARP, None, ALU.mult))
                link(v.tensor_scalar(a_b[:], bn_b[:], V_TH, SHARP, ALU.subtract, ALU.mult))
                link(v.tensor_tensor(std[:], a_s[:], mv[:, :, 0], ALU.mult))
                link(v.tensor_tensor(a_b[:], a_b[:], std[:], ALU.subtract))
                dve.sem_inc(s_coef, 1)
                v.memset(vv[:], 0.0).then_inc(s_ch, 1)
                dve.wait_ge(s_ch, link.count + 1)
                def v_step(s):
                    if s.inside(NG):
                        reached(dve, s_vt, s)
                        reached(dve, s_vv, s, 2)
                        for b in range(2):
                            ins = v.tensor_copy(vt[:, s.slot(2), 2 * b:2 * b + 2, :].rearrange("p u d -> p (u d)"), bank[b][:])
                        ins.then_inc(s_vk, 1)
                    a = s.back(1)
                    if a.inside(NG):
                        reached(dve, s_vv, a)
                        reached(dve, s_va, a, 1)
                        for c in range(KD):
                            ins = v.tensor_tensor(vv[:, c, :], vv[:, c, :], bank[2 + c][:, 0:P], ALU.add)
                        ins.then_inc(s_va, 1)
                pipeline(dve, NG, 2, 4, 1, v_step)
                dve.wait_ge(s_va, NG)
                dve.wait_ge(s_m, 3)
                v.scalar_tensor_tensor(vv[:], vv[:], SCALE, middle(mask[:], KD), ALU.mult, ALU.mult).then_inc(s_vm, 1)
                dve.wait_ge(s_we, 1)
                for c in range(KD):
                    ins = v.tensor_copy(weff[:, c, :], bank[4 + c][:, 0:D])
                ins.then_inc(s_wk, 1)
                dve.wait_ge(s_bp, 1)

                def o_step(s):
                    if s.inside(NG):
                        reached(dve, s_q, s)
                        v.tensor_tensor(qk[:, s.slot(2)], qk[:, s.slot(2)], kk[:, s.slot(2)], ALU.mult).then_inc(s_qk, 1)
                    a = s.back(1)
                    if a.inside(NG):
                        reached(dve, s_o, a)
                        for u in range(BIG):
                            t = a.n * BIG + u
                            ins = v.tensor_tensor(xs[:, ds(t, 1), :], xs[:, ds(t, 1), :],
                                                  bank[a.slot(2) * BIG + u][:, 0:D].unsqueeze(1), ALU.add)
                        ins.then_inc(s_x, 1)
                pipeline(dve, NG, 2, 2, 1, o_step)


def last_phase(nc, sem, xs, y_dram, out):
    ctx = ExitStack()
    sb = lambda n, s, d=F32: ctx.enter_context(nc.sbuf_tensor("l_" + n, s, d))
    by_token = y_dram[0:S * K1, :].rearrange("(s k) d -> s (k d)", k=K1)
    with ctx:
        yg = sb("yg", [P, 4, BIG, K1, D])
        y, o = sb("y", [P, 2, BIG, D]), sb("o", [P, 4, BIG, D])
        s_y, s_o = sem("l_y_summed"), sem("l_summed")
        s_yg = [sem(f"l_loaded{n}") for n in range(4)]
        s_st = sem("l_stored")
        with nc.Block() as block:
            @block.scalar
            def _(act):
                for g in range(NG):
                    if g >= 4:
                        act.wait_ge(s_y, g - 3)
                    act.dma_start(yg[:, g % 4].rearrange("p t k d -> p t (k d)"),
                                  tokens(by_token, g * BIG, BIG)).then_inc(s_yg[g % 4], 16)

            @block.vector
            def _(dve):
                for g in range(NG):
                    dve.wait_ge(s_yg[g % 4], g // 4 * 16 + 16)
                    if g >= 4:
                        dve.wait_ge(s_st, (g - 3) * 16)
                    nc.vector.tensor_tensor(y[:, g % 2], yg[:, g % 4, :, 0, :], yg[:, g % 4, :, 1, :], ALU.add).then_inc(s_y, 1)
                    dve.wait_ge(s_y, g + 1)
                    nc.vector.tensor_tensor(o[:, g % 4], y[:, g % 2], xs[:, g * BIG:(g + 1) * BIG, :], ALU.add).then_inc(s_o, 1)

            @block.sync
            def _(sp):
                for g in range(NG):
                    sp.wait_ge(s_o, g + 1)
                    if g:
                        sp.wait_ge(s_st, g * 16)
                    sp.dma_start(tokens(out, g * BIG, BIG), o[:, g % 4]).then_inc(s_st, 16)
                sp.wait_ge(s_st, NG * 16)


def program(nc, x, w_proj, b_proj, b_dt, conv_w, dt_bias, a_log, d_col, norm_col, w_out, b_out,
            w_small0, w_dt, w13, w2, w13_s, w2_s, w_qkv, w_p, bn_g, bn_b, bp, w_gate1, w12, w3, out):
    dram = lambda n, s, d=F32: nc.dram_tensor(n, s, d, kind="Internal").ap()
    rows = dram("xn_rows", (S, D))
    acum = dram("acum_rows_dram", (T, H, P))
    mo = dram("ssd_out", (S, D))
    table0, table1 = dram("table0", (NT0 * P, PAY), I32), dram("table1", (NT1 * P, PAY), I32)
    y0, y1 = dram("y_rows0", (S * K0 + NT0 * P, D)), dram("y_rows1", (S * K1 + NT1 * P, D))
    row = lambda ap: ap.partition_broadcast(P)

    with ExitStack() as top:
        sem = lambda n: top.enter_context(nc.semaphore(n))
        sb0 = lambda ctx: (lambda n, s, d=F32: ctx.enter_context(nc.sbuf_tensor(n, s, d)))
        k = constants(nc, top, sem)
        sb = sb0(top)
        xnT = sb("xnT", [P, KD, S])
        posi0, posi1 = sb("posi0", [P, T, K0], I32), sb("posi1", [P, T, K1], I32)
        pay0, pay1 = sb("pay0", [P, T, K0, PAY], I32), sb("pay1", [P, T, K1, PAY], I32)
        etab0, etab1 = sb("etab0", [1, NT0], I32), sb("etab1", [1, NT1], I32)
        b_out_sb = sb("b_out_sb", [P, D])
        ss = sb("ss", [P, T])
        s_w0, s_w1 = sem("layer0_weights"), sem("layer1_weights")

        with ExitStack() as ssd:
            sb = sb0(ssd)
            dt = sb("dt", [P, T, H])
            tabs = sb("tabs", [P, T, 3, H])
            wpj, wo = sb("wpj", [P, KD, (CH + CC) * P]), sb("wo", [P, CH, D])
            bias, conv, dcol, ncol = sb("bias", [P, CH + CC]), sb("conv", [P, CC, TAPS]), sb("dcol", [P, CH]), sb("ncol", [P, CH])
            with ExitStack() as pre:
                sb = sb0(pre)
                small = sb("small0", [P, T, SM0])
                bias_dt, alog = sb("bias_dt", [P, 2, H]), sb("alog", [P, H])
                with ExitStack() as first:
                    sb = sb0(first)
                    xs = sb("xs0", [P, T, D])
                    wsm = sb("wsm0", [P, KD, P])
                    s_sm, s_z = sem("small0_weights"), sem("small0_zeroed")
                    with nc.Block() as block:
                        @block.vector
                        def _(dve):
                            nc.vector.memset(wsm[:], 0.0).then_inc(s_z, 1)

                        @block.sync
                        def _(sp):
                            sp.wait_ge(s_z, 1)
                            sp.dma_start(wsm[:, :, 0:E0], w_small0).then_inc(s_sm, 16)
                            sp.dma_start(wsm[:, :, E0:SM0], w_dt).then_inc(s_sm, 16)
                            sp.wait_ge(s_sm, 32)
                    pairs = ((bias, b_proj), (conv, conv_w), (dcol, d_col), (ncol, norm_col),
                             (bias_dt[:, 0, :], row(b_dt)), (bias_dt[:, 1, :], row(dt_bias)), (alog, row(a_log)))
                    loads = [lambda sp, d=d, s=s: sp.dma_start(d if isinstance(d, bass.AP) else d[:], s).then_inc(s_w0, 16)
                             for d, s in pairs]
                    with Semaphores(nc, sem) as own:
                        norm_phase(nc, own, "n0_", k, xs, x, xnT, rows, wsm, small, SM0, loads)
                with ExitStack() as e, Semaphores(nc, sem) as own:
                    route_phase(nc, own, "r0_", k, small, E0, K0, NT0, True, posi0, pay0, etab0, table0,
                                decay_work(nc, e, own, k, small, bias_dt, alog, dt, tabs, acum, wo, ncol, s_w0, ((wo, w_out), (wpj, w_proj))))
            with Semaphores(nc, sem) as own:
                ssd_phase(nc, own, k, xnT, wpj, wo, bias, conv, dcol, dt, tabs, acum, ss, mo, posi0, pay0, table0)

        with ExitStack() as e:
            sb = sb0(e)
            wup, wdn = sb("wup0", [P, KD, E0 * 2 * F0]), sb("wdn0", [P, E0 * D])
            load = expert_loads(wup, w13, wdn, w2, 2 * F0, F0 // P * D)
            with Semaphores(nc, sem) as own:
                expert_phase(nc, own, "e0_", k, rows, table0, etab0, wup, wdn, E0, F0, NT0, y0, load)

        xs = sb0(top)("xs", [P, T, D])
        wqkv, wp = sb0(top)("wqkv", [P, KD, 3 * D]), sb0(top)("wp", [P, KD, D])
        g_sb, b_sb, bp_sb = sb0(top)("g_sb", [P, 3 * KD]), sb0(top)("b_sb", [P, 3 * KD]), sb0(top)("bp_sb", [P, D])
        wsm1 = sb0(top)("wsm1", [P, KD, P])
        stats1 = sb0(top)("stats1", [P, T, 6])
        with ExitStack() as e:
            sb = sb0(e)
            w13s, w2s = sb("w13s", [P, KD, 2 * FS]), sb("w2s", [P, FS // P, D])
            s_sh, s_z1 = sem("shared_weights"), sem("small1_zeroed")
            with nc.Block() as block:
                @block.vector
                def _(dve):
                    nc.vector.memset(wsm1[:], 0.0).then_inc(s_z1, 1)

                @block.sync
                def _(sp):
                    for d, s in ((w13s, w13_s), (w2s, w2_s), (b_out_sb, row(b_out))):
                        sp.dma_start(d[:], s).then_inc(s_sh, 16)
                    sp.wait_ge(s_z1, 1)
                    for d, s in ((wqkv[:], w_qkv), (wp[:], w_p), (g_sb[:], bn_g), (b_sb[:], bn_b), (bp_sb[:], row(bp)),
                                 (wsm1[:, :, 0:E1], w_gate1)):
                        sp.dma_start(d, s).then_inc(s_w1, 16)
                    sp.wait_ge(s_sh, 48)
                    sp.wait_ge(s_w1, 96)
            with Semaphores(nc, sem) as own:
                join_phase(nc, own, xs, x, mo, ss, b_out_sb, xnT, w13s, w2s, y0, stats1)

        with ExitStack() as e:
            small = sb0(e)("small1", [P, T, E1])
            with Semaphores(nc, sem) as own:
                norm_phase(nc, own, "n1_", k, xs, None, xnT, rows, wsm1, small, E1, [], stats1)
            with Semaphores(nc, sem) as own:
                route_phase(nc, own, "r1_", k, small, E1, K1, NT1, False, posi1, pay1, etab1, table1)
        with Semaphores(nc, sem) as own:
            attn_phase(nc, own, k, xs, xnT, wqkv, wp, g_sb, b_sb, bp_sb, s_w1, 6, posi1, pay1, table1)
        with ExitStack() as e:
            sb = sb0(e)
            wup, wdn = sb("wup1", [P, KD, E1 * 2 * F1]), sb("wdn1", [P, E1 * (F1 // P) * D])
            load = expert_loads(wup, w12, wdn, w3, 2 * F1, F1 // P * D)
            with Semaphores(nc, sem) as own:
                expert_phase(nc, own, "e1_", k, rows, table1, etab1, wup, wdn, E1, F1, NT1, y1, load)
        with Semaphores(nc, sem) as own:
            last_phase(nc, own, xs, y1, out)


def layout(i):
    a = {n: np.asarray(v) for n, v in i.items()}
    kp = lambda m: np.ascontiguousarray(m.T.reshape(-1, P, m.shape[0]).transpose(1, 0, 2))
    col = lambda v: np.ascontiguousarray(v.reshape(-1, P).T)
    big = (CH + CC) * P
    w_in, b_in = a["L0_attn_W_in"], a["L0_attn_b_in"]
    up = lambda w, v: np.concatenate([w, v], axis=1)
    w13, w12 = up(a["L0_ffn_w1_e"], a["L0_ffn_w3_e"]), up(a["L1_ffn_W1"], a["L1_ffn_W2"])
    down = lambda w: np.ascontiguousarray(
        w.transpose(0, 2, 1).reshape(w.shape[0], -1, P, D).transpose(2, 0, 1, 3).reshape(P, -1))
    return {
        "x": a["L0_attn_x"].reshape(S, D),
        "w_proj": kp(w_in[:big]), "b_proj": col(b_in[:big]), "b_dt": b_in[big:],
        "conv_w": np.ascontiguousarray(a["L0_attn_conv_w"].reshape(CC, P, TAPS).transpose(1, 0, 2)),
        "dt_bias": a["L0_attn_dt_bias"], "a_log": a["L0_attn_A_log"],
        "d_col": col(np.repeat(a["L0_attn_D"], HP)), "norm_col": col(a["L0_attn_norm_w"]),
        "w_out": kp(a["L0_attn_W_out"]), "b_out": a["L0_attn_b_out"],
        "w_small0": kp(a["L0_ffn_w_gate"]), "w_dt": kp(w_in[big:]),
        "w13": kp(w13.reshape(-1, D)), "w2": down(a["L0_ffn_w2_e"]),
        "w13_s": kp(np.concatenate([a["L0_ffn_w1_s"], a["L0_ffn_w3_s"]])), "w2_s": kp(a["L0_ffn_w2_s"]),
        "w_qkv": kp(np.concatenate([a["L1_attn_Wq"], a["L1_attn_Wk"], a["L1_attn_Wv"]])), "w_p": kp(a["L1_attn_Wp"]),
        "bn_g": col(np.concatenate([a["L1_attn_gq"], a["L1_attn_gk"], a["L1_attn_gv"]])),
        "bn_b": col(np.concatenate([a["L1_attn_bq"], a["L1_attn_bk"], a["L1_attn_bv"]])),
        "bp": a["L1_attn_bp"], "w_gate1": kp(a["L1_ffn_Wg"]),
        "w12": kp(w12.reshape(-1, D)), "w3": down(a["L1_ffn_W3"]),
    }


def kernel(**inputs):
    import concourse.bacc as bacc
    from concourse.bass_utils import run_bass_kernel_spmd

    nc = bacc.Bacc("TRN2", target_bir_lowering=False, num_devices=1)
    arrays = layout(inputs)
    args = {n: nc.dram_tensor(f"in_{n}", a.shape, mybir.dt.from_np(a.dtype), kind="ExternalInput").ap()
            for n, a in arrays.items()}
    out = nc.dram_tensor("out", (S, D), F32, kind="ExternalOutput").ap()
    program(nc, **args, out=out)
    r = run_bass_kernel_spmd(nc, [{f"in_{n}": a for n, a in arrays.items()}], core_ids=[0])
    return r.results[0]["out"].reshape(1, S, D)
```
